# Optimizing a Trainium2 kernel written in Bass

```python
import numpy as np
import jax
import jax.numpy as jnp

def _softmax(x, axis=-1):
    return jax.nn.softmax(x, axis=axis)
def _gelu(x):
    return jax.nn.gelu(x, approximate=True)
def _silu(x):
    return jax.nn.silu(x)
def _sigmoid(x):
    return jax.nn.sigmoid(x)
def _layernorm(x, axis=-1, eps=1e-5):
    m = jnp.mean(x, axis=axis, keepdims=True)
    v = jnp.var(x, axis=axis, keepdims=True)
    return (x - m) / jnp.sqrt(v + eps)
def _scatter_add(tgt, idx, src, axis=0):
    return tgt.at[idx].add(src)
def _segment_sum(src, seg, n):
    return jax.ops.segment_sum(src, seg, n)

kernel_name = 'mk_adj_resnorm_d4_adj_512_6e130a'

def setup_inputs(seed: int = 0):
    np.random.seed(seed)
    _w = jnp.asarray
    def _rec_inputs():
        import jax
        import jax.numpy as jnp
        _gk = jax.random.key(seed)
        x = -0.000929 + 1 * jax.random.normal(jax.random.fold_in(_gk, 1), (128, 64, 512), jnp.float32)
        _a = jax.random.bernoulli(jax.random.fold_in(_gk, 2), 0.125, (64, 64))
        adj = _a.astype(jnp.int32)
        return x, adj
    x, adj = _rec_inputs()
    def _L0_gnn_setup():
        import jax, jax.numpy as jnp
        import numpy as np
        B, K, DIN, DOUT = (32, 64, 512, 512)
        key = jax.random.key(seed)
        k1, k2, k3, k4 = jax.random.split(key, 4)
        x = jax.random.normal(k1, (B, K, DIN), dtype=jnp.float32)
        adj = jax.random.randint(k2, (K, K), 0, 2, dtype=jnp.int32)
        W = jax.random.normal(k3, (DOUT, 2 * DIN), dtype=jnp.float32) * 0.02
        b = jax.random.normal(k4, (DOUT,), dtype=jnp.float32) * 0.02
        return {'x': x, 'adj': adj, 'W': W, 'b': b}
    _L0_gnn_all = _L0_gnn_setup()
    _L0_gnn_in = {k: v for k, v in _L0_gnn_all.items() if k in ('W', 'b', )}
    del _L0_gnn_all

    def _L1_gnn_setup():
        import jax, jax.numpy as jnp
        import numpy as np
        LEAKY_ALPHA = 0.01
        NEG_INF = -1000000000.0
        LN_EPS = 1e-05

        def _gat_heads(x, adj, W, a):
            O = W.shape[-1]
            Wh = jnp.einsum('bnf,hfo->bhno', x, W)
            f1 = jnp.einsum('bhno,ho->bhn', Wh, a[:, :O])
            f2 = jnp.einsum('bhno,ho->bhn', Wh, a[:, O:])
            e = f1[:, :, :, None] + f2[:, :, None, :]
            e = jnp.where(e > 0, e, LEAKY_ALPHA * e)
            e = jnp.where(adj[None, None] > 0, e, NEG_INF)
            attn = jax.nn.softmax(e, axis=-1)
            return jnp.einsum('bhnm,bhmo->bhno', attn, Wh)
        key = jax.random.key(seed)
        ks = jax.random.split(key, 10)
        B, N, F_in, F_hid, H, F_out, D_ff = (8, 2048, 512, 512, 4, 512, 512)
        s = 0.05
        return {'enc_inputs': jax.random.normal(ks[0], (B, N, F_in), jnp.float32), 'adj': jax.random.randint(ks[1], (N, N), 0, 2, jnp.int32), 'W_heads': jax.random.normal(ks[2], (H, F_in, F_hid), jnp.float32) * s, 'a_heads': jax.random.normal(ks[3], (H, 2 * F_hid), jnp.float32) * s, 'W_out': jax.random.normal(ks[4], (H * F_hid, F_out), jnp.float32) * s, 'a_out': jax.random.normal(ks[5], (2 * F_out,), jnp.float32) * s, 'w1': jax.random.normal(ks[6], (F_out, D_ff), jnp.float32) * s, 'b1': jnp.zeros((D_ff,), jnp.float32), 'w2': jax.random.normal(ks[7], (D_ff, F_out), jnp.float32) * s, 'b2': jnp.zeros((F_out,), jnp.float32), 'ln_gamma': jnp.ones((F_out,), jnp.float32), 'ln_beta': jnp.zeros((F_out,), jnp.float32)}
    _L1_gnn_all = _L1_gnn_setup()
    _L1_gnn_in = {k: v for k, v in _L1_gnn_all.items() if k in ('W_heads', 'a_heads', 'W_out', 'a_out', 'w1', 'b1', 'w2', 'b2', 'ln_gamma', 'ln_beta', )}
    del _L1_gnn_all

    def _L2_gnn_setup():
        import jax, jax.numpy as jnp
        import numpy as np
        B, N, D = (8, 2048, 512)
        NEG_SLOPE = 0.2
        key = jax.random.key(seed)
        k1, k2, k3, k4, k5 = jax.random.split(key, 5)
        x = jax.random.normal(k1, (B, N, D), dtype=jnp.float32)
        adj = jax.random.randint(k2, (N, N), 0, 2, dtype=jnp.int32)
        adj = jnp.maximum(adj, jnp.eye(N, dtype=jnp.int32))
        W = jax.random.normal(k3, (D, D), dtype=jnp.float32) * (1.0 / np.sqrt(D))
        a_src = jax.random.normal(k4, (D,), dtype=jnp.float32) * (1.0 / np.sqrt(D))
        a_dst = jax.random.normal(k5, (D,), dtype=jnp.float32) * (1.0 / np.sqrt(D))
        return {'x': x, 'adj': adj, 'W': W, 'a_src': a_src, 'a_dst': a_dst}
    _L2_gnn_all = _L2_gnn_setup()
    _L2_gnn_in = {k: v for k, v in _L2_gnn_all.items() if k in ('W', 'a_src', 'a_dst', )}
    del _L2_gnn_all

    def _L3_gnn_setup():
        import jax, jax.numpy as jnp
        import numpy as np
        B, N, D = (8, 2048, 512)
        NEG_SLOPE = 0.2
        key = jax.random.key(seed)
        k1, k2, k3, k4, k5 = jax.random.split(key, 5)
        x = jax.random.normal(k1, (B, N, D), dtype=jnp.float32)
        adj = jax.random.randint(k2, (N, N), 0, 2, dtype=jnp.int32)
        adj = jnp.maximum(adj, jnp.eye(N, dtype=jnp.int32))
        W = jax.random.normal(k3, (D, D), dtype=jnp.float32) * (1.0 / np.sqrt(D))
        a_src = jax.random.normal(k4, (D,), dtype=jnp.float32) * (1.0 / np.sqrt(D))
        a_dst = jax.random.normal(k5, (D,), dtype=jnp.float32) * (1.0 / np.sqrt(D))
        return {'x': x, 'adj': adj, 'W': W, 'a_src': a_src, 'a_dst': a_dst}
    _L3_gnn_all = _L3_gnn_setup()
    _L3_gnn_in = {k: v for k, v in _L3_gnn_all.items() if k in ('W', 'a_src', 'a_dst', )}
    del _L3_gnn_all

    return {
        "x": x,
        "adj": adj,
        "L0_gnn_W": _L0_gnn_in["W"],
        "L0_gnn_b": _L0_gnn_in["b"],
        "L1_gnn_W_heads": _L1_gnn_in["W_heads"],
        "L1_gnn_a_heads": _L1_gnn_in["a_heads"],
        "L1_gnn_W_out": _L1_gnn_in["W_out"],
        "L1_gnn_a_out": _L1_gnn_in["a_out"],
        "L1_gnn_w1": _L1_gnn_in["w1"],
        "L1_gnn_b1": _L1_gnn_in["b1"],
        "L1_gnn_w2": _L1_gnn_in["w2"],
        "L1_gnn_b2": _L1_gnn_in["b2"],
        "L1_gnn_ln_gamma": _L1_gnn_in["ln_gamma"],
        "L1_gnn_ln_beta": _L1_gnn_in["ln_beta"],
        "L2_gnn_W": _L2_gnn_in["W"],
        "L2_gnn_a_src": _L2_gnn_in["a_src"],
        "L2_gnn_a_dst": _L2_gnn_in["a_dst"],
        "L3_gnn_W": _L3_gnn_in["W"],
        "L3_gnn_a_src": _L3_gnn_in["a_src"],
        "L3_gnn_a_dst": _L3_gnn_in["a_dst"],
    }

def reference(x, adj, L0_gnn_W, L0_gnn_b, L1_gnn_W_heads, L1_gnn_a_heads, L1_gnn_W_out, L1_gnn_a_out, L1_gnn_w1, L1_gnn_b1, L1_gnn_w2, L1_gnn_b2, L1_gnn_ln_gamma, L1_gnn_ln_beta, L2_gnn_W, L2_gnn_a_src, L2_gnn_a_dst, L3_gnn_W, L3_gnn_a_src, L3_gnn_a_dst):
    import jax
    import jax.numpy as jnp
    def _L0_gnn_ref(x, adj, W, b):
        import jax, jax.numpy as jnp
        import numpy as np
        B, K, DIN, DOUT = (32, 64, 512, 512)
        Din = x.shape[-1]
        Wi, Wj = (W[:, :Din], W[:, Din:])
        mi = jnp.einsum('bkd,od->bko', x, Wi)
        mj = jnp.einsum('bkd,od->bko', x, Wj)
        a = adj.astype(x.dtype)
        deg = a.sum(axis=1)
        out = deg[None, :, None] * (mi + b) + jnp.einsum('ij,bjo->bio', a, mj)
        return out

    def _L1_gnn_ref(enc_inputs, adj, W_heads, a_heads, W_out, a_out, w1, b1, w2, b2, ln_gamma, ln_beta):
        import jax, jax.numpy as jnp
        import numpy as np
        LEAKY_ALPHA = 0.01
        NEG_INF = -1000000000.0
        LN_EPS = 1e-05

        def _gat_heads(x, adj, W, a):
            O = W.shape[-1]
            Wh = jnp.einsum('bnf,hfo->bhno', x, W)
            f1 = jnp.einsum('bhno,ho->bhn', Wh, a[:, :O])
            f2 = jnp.einsum('bhno,ho->bhn', Wh, a[:, O:])
            e = f1[:, :, :, None] + f2[:, :, None, :]
            e = jnp.where(e > 0, e, LEAKY_ALPHA * e)
            e = jnp.where(adj[None, None] > 0, e, NEG_INF)
            attn = jax.nn.softmax(e, axis=-1)
            return jnp.einsum('bhnm,bhmo->bhno', attn, Wh)
        B, N, _ = enc_inputs.shape
        h = jax.nn.elu(_gat_heads(enc_inputs, adj, W_heads, a_heads))
        h = jnp.transpose(h, (0, 2, 1, 3)).reshape(B, N, -1)
        out = _gat_heads(h, adj, W_out[None], a_out[None])[:, 0]
        out = jax.nn.elu(out)
        ffn = jnp.maximum(out @ w1 + b1, 0.0) @ w2 + b2
        y = ffn + out
        mu = jnp.mean(y, axis=-1, keepdims=True)
        var = jnp.var(y, axis=-1, keepdims=True)
        return (y - mu) / jnp.sqrt(var + LN_EPS) * ln_gamma + ln_beta

    def _L2_gnn_ref(x, adj, W, a_src, a_dst):
        import jax, jax.numpy as jnp
        import numpy as np
        B, N, D = (8, 2048, 512)
        NEG_SLOPE = 0.2
        Wh = jnp.einsum('bnd,de->bne', x, W)
        e_src = jnp.einsum('bnd,d->bn', Wh, a_src)
        e_dst = jnp.einsum('bnd,d->bn', Wh, a_dst)
        logits = e_src[:, :, None] + e_dst[:, None, :]
        logits = jnp.where(logits >= 0, logits, NEG_SLOPE * logits)
        mask = (adj == 0)[None, :, :]
        logits = jnp.where(mask, -jnp.inf, logits)
        attn = jax.nn.softmax(logits, axis=-1)
        attn = jnp.nan_to_num(attn, nan=0.0)
        out = jnp.einsum('bnm,bmd->bnd', attn, Wh)
        return out

    def _L3_gnn_ref(x, adj, W, a_src, a_dst):
        import jax, jax.numpy as jnp
        import numpy as np
        B, N, D = (8, 2048, 512)
        NEG_SLOPE = 0.2
        Wh = jnp.einsum('bnd,de->bne', x, W)
        e_src = jnp.einsum('bnd,d->bn', Wh, a_src)
        e_dst = jnp.einsum('bnd,d->bn', Wh, a_dst)
        logits = e_src[:, :, None] + e_dst[:, None, :]
        logits = jnp.where(logits >= 0, logits, NEG_SLOPE * logits)
        mask = (adj == 0)[None, :, :]
        logits = jnp.where(mask, -jnp.inf, logits)
        attn = jax.nn.softmax(logits, axis=-1)
        attn = jnp.nan_to_num(attn, nan=0.0)
        out = jnp.einsum('bnm,bmd->bnd', attn, Wh)
        return out

    x = _layernorm(x + _L0_gnn_ref(x, adj, L0_gnn_W, L0_gnn_b), axis=-1)
    x = _layernorm(x + _L1_gnn_ref(x, adj, L1_gnn_W_heads, L1_gnn_a_heads, L1_gnn_W_out, L1_gnn_a_out, L1_gnn_w1, L1_gnn_b1, L1_gnn_w2, L1_gnn_b2, L1_gnn_ln_gamma, L1_gnn_ln_beta), axis=-1)
    x = _layernorm(x + _L2_gnn_ref(x, adj, L2_gnn_W, L2_gnn_a_src, L2_gnn_a_dst), axis=-1)
    x = _layernorm(x + _L3_gnn_ref(x, adj, L3_gnn_W, L3_gnn_a_src, L3_gnn_a_dst), axis=-1)
    return x


_drawn_inputs = setup_inputs


def setup_inputs(seed=0):
    import zlib

    import numpy as np

    out = dict(_drawn_inputs(seed))
    spreads = {'L1_gnn_b1': (0.0, 0.1),
     'L1_gnn_b2': (0.0, 0.1),
     'L1_gnn_ln_gamma': (1.0, 0.2),
     'L1_gnn_ln_beta': (0.0, 0.1)}
    factors = {}
    for name, (base, spread) in spreads.items():
        noise = np.random.default_rng([zlib.crc32(name.encode()), seed]).standard_normal(out[name].shape)
        drawn = base * np.exp(spread * noise) if base else spread * noise
        out[name] = jnp.asarray(drawn.astype(out[name].dtype))
    for name, factor in factors.items():
        out[name] = (out[name] * factor).astype(out[name].dtype)
    return out
```

```python
from contextlib import ExitStack

import concourse.bass as bass
from concourse import mybir

F32 = mybir.dt.float32
F32R = mybir.dt.float32r
I32 = mybir.dt.int32
ALU = mybir.AluOpType
ACT = mybir.ActivationFunctionType
AX_X = mybir.AxisListType.X

P = 128
D = 512
KC = D // P
NODES = 64
HEADS = 4
LN_EPS = 1e-5
SLOPE_L1 = 0.01
SLOPE_L23 = 0.2
MASKED_L1 = -1e9
MASKED_L23 = -3e38


def ge(eng, sem, value):
    if not isinstance(value, int) or value > 0:
        eng.wait_ge(sem, value)


def capped(n, most):
    return min(n, most) if isinstance(n, int) else n


def split_passes(hi_lhs, lo_lhs, hi_rhs, lo_rhs):
    return ((hi_lhs, hi_rhs), (hi_lhs, lo_rhs), (lo_lhs, hi_rhs))


def product(nc, out, lhs, rhs, chunks, first=True, last=True):
    n = len(chunks)
    for c, (kl, kr) in enumerate(chunks):
        passes = split_passes(lhs[0][:, kl, :], lhs[1][:, kl, :], rhs[0][:, kr, :], rhs[1][:, kr, :])
        for q, (a, b) in enumerate(passes):
            ins = nc.tensor.matmul(out, a, b, start=first and c == 0 and q == 0,
                                   stop=last and c == n - 1 and q == 2)
    return ins


class Attention:

    def __init__(self, nc, ctx, name, heads, slope, mask, fill, scores_psum, turned_psum):
        def sb(n, shape, dt=F32):
            return ctx.enter_context(nc.sbuf_tensor(f"{name}_{n}", shape, dt))

        def sem(n):
            return ctx.enter_context(nc.semaphore(f"{name}_{n}"))

        self.heads, self.slope, self.mask, self.fill = heads, slope, mask, fill
        self.scores_psum = scores_psum
        self.turned_psum = turned_psum
        self.f = sb("f", [P, 2 * heads])
        self.diag = sb("diag", [P, heads, NODES])
        self.e1 = sb("e1", [P, heads, NODES])
        self.e2 = sb("e2", [P, heads, NODES])
        self.ex = sb("ex", [P, heads, NODES])
        self.peak = sb("peak", [P, heads])
        self.total = sb("total", [P, heads])
        self.inv = sb("inv", [P, heads])
        self.prob = sb("prob", [P, heads, 2, NODES])
        self.turned = sb("turned", [P, heads, P])
        self.pause = sb("pause", [P, 1])
        self.zeroed = sem("zeroed")
        self.f_ready, self.diag_ready, self.scores_done = sem("f_ready"), sem("diag_ready"), sem("scores_done")
        self.summed, self.leaky, self.masked = sem("summed"), sem("leaky"), sem("masked")
        self.peaked, self.shifted, self.exp_ready = sem("peaked"), sem("shifted"), sem("exp_ready")
        self.totalled, self.inverted, self.gated = sem("totalled"), sem("inverted"), sem("gated")
        self.prob_ready, self.turned_done, self.turned_ready = (
            sem("prob_ready"), sem("turned_done"), sem("turned_ready"))

    def pool_zero(self, nc):
        nc.gpsimd.memset(self.turned[:], 0.0).then_inc(self.zeroed, 1)

    def pool_diag(self, nc, pool, t, i64):
        pool.wait_ge(self.f_ready, t + 1)
        ge(pool, self.scores_done, t)
        shape = [P, self.heads, NODES]
        nc.gpsimd.tensor_tensor(self.diag[:], i64[:, None, :].to_broadcast(shape),
                                self.f[:, 0:self.heads, None].to_broadcast(shape),
                                ALU.mult).then_inc(self.diag_ready, 1)

    def pe_scores(self, nc, pe, t, same_graph):
        pe.wait_ge(self.diag_ready, t + 1)
        ge(pe, self.summed, t)
        nc.tensor.matmul(self.scores_psum, same_graph[:], self.diag[:].rearrange("p h j -> p (h j)"),
                         start=True, stop=True).then_inc(self.scores_done, 1)

    def dve_before_exp(self, nc, dve, t, fill):
        shape = [P, self.heads, NODES]
        dve.wait_ge(self.scores_done, t + 1)
        dve.wait_ge(self.f_ready, t + 1)
        ge(dve, self.exp_ready, t)
        nc.vector.tensor_tensor(self.e1[:], self.scores_psum.rearrange("p (h j) -> p h j", h=self.heads),
                                self.f[:, self.heads:, None].to_broadcast(shape), ALU.add
                                ).then_inc(self.summed, 1)
        dve.wait_ge(self.summed, t + 1)
        nc.vector.scalar_tensor_tensor(self.e2[:], self.e1[:], self.slope, self.e1[:], ALU.mult, ALU.max
                                       ).then_inc(self.leaky, 1)
        dve.wait_ge(self.leaky, t + 1)
        nc.vector.memset(self.pause[:], 0.0)
        nc.vector.copy_predicated(self.e2[:], self.mask[:, None, :].to_broadcast(shape),
                                  fill[:, 0:1, None].to_broadcast(shape)).then_inc(self.masked, 1)
        dve.wait_ge(self.masked, t + 1)
        nc.vector.reduce_max(self.peak[:], self.e2[:], AX_X).then_inc(self.peaked, 1)
        dve.wait_ge(self.peaked, t + 1)
        nc.vector.tensor_tensor(self.e1[:], self.e2[:], self.peak[:, :, None].to_broadcast(shape),
                                ALU.subtract).then_inc(self.shifted, 1)

    def act_exp(self, nc, act, t):
        act.wait_ge(self.shifted, t + 1)
        ge(act, self.prob_ready, t)
        ge(act, self.totalled, t)
        nc.scalar.activation(self.ex[:], self.e1[:], ACT.Exp).then_inc(self.exp_ready, 1)

    def dve_after_exp(self, nc, dve, t, gate=None):
        dve.wait_ge(self.exp_ready, t + 1)
        nc.vector.reduce_sum(self.total[:], self.ex[:], AX_X).then_inc(self.totalled, 1)
        dve.wait_ge(self.totalled, t + 1)
        ge(dve, self.prob_ready, t)
        nc.vector.reciprocal(self.inv[:], self.total[:]).then_inc(self.inverted, 1)
        if gate is not None:
            dve.wait_ge(self.inverted, t + 1)
            nc.vector.tensor_tensor(self.inv[:], self.inv[:], gate[:], ALU.mult).then_inc(self.gated, 1)

    def pool_prob(self, nc, pool, t, gate=None):
        if gate is not None:
            pool.wait_ge(self.gated, t + 1)
        else:
            pool.wait_ge(self.inverted, t + 1)
        pool.wait_ge(self.exp_ready, t + 1)
        ge(pool, self.turned_done, t)
        for g in range(2):
            ins = nc.gpsimd.tensor_tensor(self.prob[:, :, g, :], self.ex[:],
                                          self.inv[:, :, None].to_broadcast([P, self.heads, NODES]), ALU.mult)
        ins.then_inc(self.prob_ready, 1)

    def pe_turn(self, nc, pe, t, ident):
        pe.wait_ge(self.prob_ready, t + 1)
        ge(pe, self.turned_ready, 2 * t)
        for h in range(self.heads):
            ins = nc.tensor.transpose(self.turned_psum[:, h, :],
                                      self.prob[:, h, :, :].rearrange("p g j -> p (g j)"), ident[:])
        ins.then_inc(self.turned_done, 1)

    def act_turned(self, nc, act, t):
        act.wait_ge(self.turned_done, t + 1)
        if isinstance(t, int) and t == 0:
            act.wait_ge(self.zeroed, 1)
        for g in range(2):
            r = slice(g * NODES, (g + 1) * NODES)
            nc.scalar.copy(self.turned[r, :, r], self.turned_psum[r, :, r]).then_inc(self.turned_ready, 1)


class Norm:

    def __init__(self, nc, ctx, name):
        def sb(n, shape):
            return ctx.enter_context(nc.sbuf_tensor(f"{name}_{n}", shape, F32))

        def sem(n):
            return ctx.enter_context(nc.semaphore(f"{name}_{n}"))

        self.pause = sb("pause", [P, 1])
        self.stats, self.mv = sb("stats", [P, 6]), sb("mv", [P, 2])
        self.veps, self.rstd = sb("veps", [P, 1]), sb("rstd", [P, 1])
        self.stats_ready, self.mv_ready, self.veps_ready, self.rstd_ready = (
            sem("stats_ready"), sem("mv_ready"), sem("veps_ready"), sem("rstd_ready"))

    def dve_stats(self, nc, dve, t, x, used):
        ge(dve, used, t)
        nc.vector.bn_stats(self.stats[:], x).then_inc(self.stats_ready, 1)
        dve.wait_ge(self.stats_ready, t + 1)
        nc.vector.memset(self.pause[:], 0.0)
        nc.vector.bn_aggr(self.mv[:], self.stats[:]).then_inc(self.mv_ready, 1)
        dve.wait_ge(self.mv_ready, t + 1)
        ge(dve, self.rstd_ready, t)
        nc.vector.tensor_scalar(self.veps[:], self.mv[:, 1:2], LN_EPS, None, ALU.add
                                ).then_inc(self.veps_ready, 1)

    def pool_rstd(self, nc, pool, t, used, neg_half):
        pool.wait_ge(self.veps_ready, t + 1)
        ge(pool, used, t)
        nc.gpsimd.tensor_tensor(self.rstd[:], self.veps[:], neg_half[:], ALU.pow
                                ).then_inc(self.rstd_ready, 1)


def gnn_stack_kernel(nc, x, adj, W0T, b0, Wh, ah, Wo, ao, w1, b1, w2, b2, gamma, beta,
                     W2, a2s, a2d, W3, a3s, a3d, out):
    B, N, _ = x.shape
    T = B * N // P
    x_rows = x.rearrange("b n d -> (b n) d")
    out_rows = out.rearrange("b n d -> (b n) d")
    x1_rows = nc.dram_tensor("x1_scratch", (B * N, D), F32).ap()
    att_rows = nc.dram_tensor("att_scratch", (T * P, D), F32).ap()

    def rows(dram, t):
        return dram[bass.ts(t, P), :]

    def chunked(w):
        return w.rearrange("(c p) n -> p c n", p=P)

    with ExitStack() as top:
        def sb(n, shape, dt=F32):
            return top.enter_context(nc.sbuf_tensor(n, shape, dt))

        def sem(n):
            return top.enter_context(nc.semaphore(n))

        NQ = 2 * HEADS * KC
        held = top.enter_context(ExitStack())
        ident = sb("ident", [P, P])
        same_graph = sb("same_graph", [P, P])
        i64 = sb("i64", [P, NODES])
        neg_half = sb("neg_half", [P, 1])
        fill1 = sb("fill1", [P, 1])
        fill23 = sb("fill23", [P, 1])
        mask1 = sb("mask1", [P, NODES], I32)
        mask23 = sb("mask23", [P, NODES], I32)
        gate = sb("gate", [P, 1])
        big_hi = held.enter_context(nc.sbuf_tensor("big_hi", [P, NQ, D], F32R))
        big_lo = held.enter_context(nc.sbuf_tensor("big_lo", [P, NQ, D], F32R))
        att_stored = sem("att_stored")
        stage_loaded = sem("stage_loaded")

        with ExitStack() as ctx:
            def sb(n, shape, dt=F32):
                return ctx.enter_context(nc.sbuf_tensor(n, shape, dt))

            def sem(n):
                return ctx.enter_context(nc.semaphore(n))

            XR, UN = 4, 4
            w0 = (sb("w0_hi", [P, 2 * KC, D], F32R), sb("w0_lo", [P, 2 * KC, D], F32R))
            w0f = sb("w0f", [P, KC, D])
            stage = sb("stage", [P, D])
            xt = [sb(f"xt{r}", [P, D]) for r in range(XR)]
            mix = [(sb(f"mix_hi{b}", [P, KC, 2 * P], F32R), sb(f"mix_lo{b}", [P, KC, 2 * P], F32R))
                   for b in range(2)]
            z = sb("z", [P, D])
            x1 = [sb(f"x1_{b}", [P, D]) for b in range(2)]
            adj_i = sb("adj_i", [P, NODES], I32)
            adj_f = sb("adj_f", [P, NODES])
            zero_f = sb("zero_f", [P, NODES])
            none = sb("none", [P, 1])
            deg = sb("deg", [P, 1])
            adj_bd = sb("adj_bd", [P, P])
            spread = sb("spread", [P, 2 * P])
            db = sb("db", [P, D])
            mixed = [[ctx.enter_context(nc.psum_tensor(f"mixed{b}{k}", [P, 2, 2 * P], F32)) for k in range(2)]
                     for b in range(2)]
            main = [ctx.enter_context(nc.psum_tensor(f"main{b}", [P, D], F32)) for b in range(2)]
            setup_psum = ctx.enter_context(nc.psum_tensor("setup_psum", [P, P], F32))
            first_sem = sem("first_of_layer0")
            norm = Norm(nc, ctx, "n0")
            loaded = [sem(f"loaded{r}") for r in range(XR)]
            small_loaded, w0_loaded, w0_hi_ready, w0_lo_ready = (
                sem("small_loaded"), sem("w0_loaded"), sem("w0_hi_ready"), sem("w0_lo_ready"))
            zeros_set, consts_set, adj_ready, setup_step, bd_ready, bd_turned, spread_ready = (
                sem("zeros_set"), sem("consts_set"), sem("adj_ready"), sem("setup_step"), sem("bd_ready"),
                sem("bd_turned"), sem("spread_ready"))
            mixed_done, mix_hi_ready, mix_lo_ready, main_done = (
                sem("mixed_done"), sem("mix_hi_ready"), sem("mix_lo_ready"), sem("main_done"))
            xb_ready, z_ready, x1_ready = sem("xb_ready"), sem("z_ready"), sem("x1_ready")
            big_hi_ready, big_lo_ready = sem("big_hi_ready"), sem("big_lo_ready")
            x1_out = [sem(f"x1_out{b}") for b in range(2)]
            layer0_sems = range(first_sem.num, x1_out[1].num + 1)
            block = ctx.enter_context(nc.Block())
            Wh_rows = Wh.rearrange("h k o -> (h k) o")

            @block.sync
            def _(sp):
                for g in range(2):
                    sp.dma_start(adj_i[g * NODES:(g + 1) * NODES, :], adj).then_inc(small_loaded, 16)
                sp.dma_start(db[:], b0.partition_broadcast(P)).then_inc(small_loaded, 16)
                for r in range(XR):
                    sp.dma_start(xt[r][:], rows(x_rows, r)).then_inc(loaded[r], 16)

                for k in range(2):
                    ge(sp, w0_lo_ready, k)
                    sp.dma_start(w0f[:], chunked(W0T[k * D:(k + 1) * D, :])).then_inc(w0_loaded, 16)

                def step(t, r, more):
                    sp.wait_ge(x1_ready, t + 1)
                    sp.dma_start(rows(x1_rows, t), x1[r % 2][:]).then_inc(x1_out[r % 2], 16)
                    if more:
                        sp.dma_start(xt[r][:], rows(x_rows, t + XR)).then_inc(loaded[r], 16)

                with sp.Fori(0, T // UN - 1) as g:
                    t = g * UN
                    for r in range(UN):
                        step(t + r, r, True)
                for r in range(XR):
                    step(T - XR + r, r, False)
                for b in range(2):
                    sp.wait_ge(x1_out[b], 16 * T // 2)

            @block.gpsimd
            def _(pool):
                nc.gpsimd.memset(ident[:], 0.0).then_inc(zeros_set, 1)
                nc.gpsimd.memset(i64[:], 0.0).then_inc(zeros_set, 1)
                nc.gpsimd.memset(adj_bd[:], 0.0).then_inc(zeros_set, 1)
                nc.gpsimd.memset(same_graph[:], 0.0).then_inc(zeros_set, 1)
                nc.gpsimd.memset(neg_half[:], -0.5).then_inc(consts_set, 1)
                nc.gpsimd.memset(fill1[:], MASKED_L1).then_inc(consts_set, 1)
                nc.gpsimd.memset(fill23[:], MASKED_L23).then_inc(consts_set, 1)
                pool.wait_ge(zeros_set, 4)
                for g in range(2):
                    r = slice(g * NODES, (g + 1) * NODES)
                    pool.wait_ge(zeros_set, 4 + g)
                    nc.gpsimd.memset(same_graph[r, r], 1.0).then_inc(consts_set, 1)
                    pool.wait_ge(consts_set, 4 + g)
                    nc.gpsimd.affine_select(out=i64[:], in_=i64[:], compare_op=ALU.not_equal, fill=1.0,
                                            base=-g * NODES, pattern=[[-1, NODES]], channel_multiplier=1
                                            ).then_inc(zeros_set, 1)
                pool.wait_ge(zeros_set, 6)
                nc.gpsimd.affine_select(out=ident[:], in_=ident[:], compare_op=ALU.not_equal, fill=1.0,
                                        base=0, pattern=[[-1, P]], channel_multiplier=1).then_inc(consts_set, 1)
                pool.wait_ge(consts_set, 6)

                def split_block(q, source, k):
                    ge(pool, big_lo_ready, q)
                    pool.dma_start(stage[:], source[bass.ts(k, P), :]).then_inc(stage_loaded, 16)
                    return q

                def split_hi(q):
                    pool.wait_ge(stage_loaded, 16 * q + 16)
                    nc.gpsimd.tensor_copy(big_hi[:, bass.ds(q, 1), :], stage[:, None, :]
                                          ).then_inc(big_hi_ready, 1)

                def split_lo(q):
                    pool.wait_ge(big_hi_ready, q + 1)
                    nc.gpsimd.tensor_tensor(big_lo[:, bass.ds(q, 1), :], stage[:, None, :],
                                            big_hi[:, bass.ds(q, 1), :].bitcast(F32), ALU.subtract
                                            ).then_inc(big_lo_ready, 1)

                def half(source, first_q):
                    def two(q, k):
                        split_block(q, source, k)
                        norm.pool_rstd(nc, pool, 2 * q, x1_ready, neg_half)
                        split_hi(q)
                        norm.pool_rstd(nc, pool, 2 * q + 1, x1_ready, neg_half)
                        split_lo(q)
                    if first_q == 0:
                        two(0, 0)
                        with pool.Fori(1, NQ // 2) as k:
                            two(k, k)
                    else:
                        with pool.Fori(0, NQ // 2) as k:
                            two(k + first_q, k)

                half(Wh_rows, 0)
                half(Wo, NQ // 2)

            @block.scalar
            def _(act):
                for k in range(2):
                    s = slice(k * KC, (k + 1) * KC)
                    act.wait_ge(w0_loaded, 16 * (k + 1))
                    nc.scalar.copy(w0[0][:, s, :], w0f[:]).then_inc(w0_hi_ready, 1)

                def step(t, b):
                    for k in range(2):
                        act.wait_ge(mixed_done, 2 * t + k + 1)
                        ge(act, main_done, t - 1)
                        nc.scalar.copy(mix[b][0][:, 2 * k:2 * k + 2, :], mixed[b][k][:]
                                       ).then_inc(mix_hi_ready, 1)

                step(0, 0)
                step(1, 1)
                with act.Fori(1, T // 2) as g:
                    t = g * 2
                    step(t, 0)
                    step(t + 1, 1)

            @block.vector
            def _(dve):
                dve.wait_ge(small_loaded, 48)
                dve.wait_ge(zeros_set, 6)
                nc.vector.tensor_copy(adj_f[:], adj_i[:]).then_inc(adj_ready, 1)
                dve.wait_ge(adj_ready, 1)
                nc.vector.reduce_sum(deg[:], adj_f[:], AX_X).then_inc(setup_step, 1)
                nc.vector.tensor_scalar(mask1[:], adj_f[:], 0.0, None, ALU.is_le).then_inc(setup_step, 1)
                nc.vector.tensor_scalar(mask23[:], adj_f[:], 0.0, None, ALU.is_equal).then_inc(setup_step, 1)
                nc.vector.tensor_scalar(zero_f[:], adj_f[:], 0.0, None, ALU.is_equal).then_inc(setup_step, 1)
                for g in range(2):
                    r = slice(g * NODES, (g + 1) * NODES)
                    nc.vector.tensor_copy(adj_bd[r, r], adj_f[r, :]).then_inc(bd_ready, 1)
                dve.wait_ge(setup_step, 4)
                nc.vector.tensor_reduce(none[:], zero_f[:], AX_X, ALU.min).then_inc(setup_step, 1)
                dve.wait_ge(consts_set, 6)
                nc.vector.tensor_scalar(spread[:, P:2 * P], ident[:], deg[:], None, ALU.mult
                                        ).then_inc(spread_ready, 1)
                nc.vector.tensor_scalar(db[:], db[:], deg[:], None, ALU.mult).then_inc(setup_step, 1)
                dve.wait_ge(setup_step, 6)
                nc.vector.tensor_scalar(gate[:], none[:], -1.0, 1.0, ALU.mult, ALU.add).then_inc(setup_step, 1)
                dve.wait_ge(bd_turned, 1)
                nc.vector.tensor_copy(spread[:, 0:P], setup_psum[:]).then_inc(spread_ready, 1)
                for k in range(2):
                    s = slice(k * KC, (k + 1) * KC)
                    dve.wait_ge(w0_hi_ready, k + 1)
                    nc.vector.tensor_tensor(w0[1][:, s, :], w0f[:], w0[0][:, s, :].bitcast(F32),
                                            ALU.subtract).then_inc(w0_lo_ready, 1)

                def mix_lo(t, b):
                    for k in range(2):
                        dve.wait_ge(mix_hi_ready, 2 * t + k + 1)
                        nc.vector.tensor_tensor(mix[b][1][:, 2 * k:2 * k + 2, :], mixed[b][k][:],
                                                mix[b][0][:, 2 * k:2 * k + 2, :].bitcast(F32),
                                                ALU.subtract).then_inc(mix_lo_ready, 1)

                def finish(t, r):
                    dve.wait_ge(loaded[r], 16 * (t // XR) + 16 if isinstance(t, int) else 4 * (t - r) + 16)
                    ge(dve, x1_ready, t)
                    nc.vector.tensor_tensor(z[:], xt[r][:], db[:], ALU.add).then_inc(xb_ready, 1)
                    dve.wait_ge(xb_ready, t + 1)
                    dve.wait_ge(main_done, t + 1)
                    nc.vector.tensor_tensor(z[:], main[r % 2][:], z[:], ALU.add).then_inc(z_ready, 1)
                    dve.wait_ge(z_ready, t + 1)
                    norm.dve_stats(nc, dve, t, z[:], x1_ready)
                    dve.wait_ge(norm.rstd_ready, t + 1)
                    ge(dve, x1_out[r % 2], 16 * (t // 2) if isinstance(t, int) else 8 * (t - r) + 16 * (r // 2))
                    nc.vector.tensor_scalar(x1[r % 2][:], z[:], norm.mv[:, 0:1], norm.rstd[:],
                                            ALU.subtract, ALU.mult).then_inc(x1_ready, 1)

                dve.wait_ge(setup_step, 7)
                mix_lo(0, 0)
                for r in range(UN):
                    mix_lo(r + 1, (r + 1) % 2)
                    finish(r, r)
                with dve.Fori(1, T // UN - 1) as g:
                    t = g * UN
                    for r in range(UN):
                        mix_lo(t + r + 1, (r + 1) % 2)
                        finish(t + r, r)
                for r in range(UN):
                    if r < UN - 1:
                        mix_lo(T - UN + r + 1, (r + 1) % 2)
                    finish(T - UN + r, r)

            @block.tensor
            def _(pe):
                pe.wait_ge(bd_ready, 2)
                pe.wait_ge(consts_set, 6)
                nc.tensor.transpose(setup_psum[:], adj_bd[:], ident[:]).then_inc(bd_turned, 1)
                pe.wait_ge(spread_ready, 2)

                def mixes(t, r):
                    pe.wait_ge(loaded[r % XR], 16 * (t // XR) + 16 if isinstance(t, int)
                               else 4 * (t - r % XR) + 16)
                    for c in range(KC):
                        if c % 2 == 0:
                            ge(pe, mix_lo_ready, 2 * t + c // 2 - 3)
                        ins = nc.tensor.matmul(mixed[r % 2][c // 2][:, c % 2, :],
                                               xt[r % XR][:, c * P:(c + 1) * P], spread[:],
                                               start=True, stop=True)
                        if c % 2:
                            ins.then_inc(mixed_done, 1)

                def products(t, r):
                    pe.wait_ge(mix_hi_ready, 2 * t + 2)
                    pe.wait_ge(mix_lo_ready, 2 * t + 2)
                    ge(pe, z_ready, t - 1)
                    hi, lo = mix[r % 2]
                    product(nc, main[r % 2][:], (hi[:, :, P:], lo[:, :, P:]), w0,
                            [(c, c) for c in range(KC)], last=False)
                    product(nc, main[r % 2][:], (hi[:, :, :P], lo[:, :, :P]), w0,
                            [(c, KC + c) for c in range(KC)], first=False).then_inc(main_done, 1)

                mixes(0, 0)
                pe.wait_ge(w0_hi_ready, 2)
                pe.wait_ge(w0_lo_ready, 2)
                for r in range(UN):
                    mixes(r + 1, r + 1)
                    products(r, r)
                with pe.Fori(1, T // UN - 1) as g:
                    t = g * UN
                    for r in range(UN):
                        if r < UN - 1:
                            mixes(t + (r + 1), r + 1)
                        else:
                            mixes(t + UN, 0)
                        products(t + r, r)
                for r in range(UN):
                    if r < UN - 1:
                        mixes(T - UN + r + 1, r + 1)
                    products(T - UN + r, r)

        with ExitStack() as ctx:
            def sb(n, shape, dt=F32):
                return ctx.enter_context(nc.sbuf_tensor(n, shape, dt))

            def sem(n):
                return ctx.enter_context(nc.semaphore(n))

            def pb(n, shape):
                return ctx.enter_context(nc.psum_tensor(n, shape, F32))

            xin = sb("xin", [P, D])
            xT = (sb("xT_hi", [P, KC, P], F32R), sb("xT_lo", [P, KC, P], F32R))
            wh = sb("wh", [P, HEADS, D])
            who = sb("who", [P, D])
            ex = [sb(f"ex{b}", [P, D]) for b in range(2)]
            hv = [sb(f"hv{b}", [P, D]) for b in range(2)]
            hT = [(sb(f"hT_hi{b}", [P, KC, P], F32R), sb(f"hT_lo{b}", [P, KC, P], F32R)) for b in range(2)]
            attT = sb("attT", [P, D])
            junk = sb("junk", [P, D])
            ao_row = sb("ao_row", [P, 2, D])
            v_hl = sb("v_hl", [P, KC, 4 * HEADS], F32R)
            v_f = sb("v_f", [P, KC, 2 * HEADS])
            ws = hv[0]
            whp = [pb(f"whp{b}", [P, D]) for b in range(2)]
            wop = pb("wop", [P, D])
            turn = pb("turn", [P, HEADS, P])
            smallp = pb("smallp", [P, D])
            up = [pb(f"up{b}", [P, D]) for b in range(3)]
            U_HEAD, U_OUT = [0, 1, 2, 0], 1
            SF, SO, SH, ST = 0, NODES, P, 3 * P
            first_sem = sem("first_of_layer1")
            at = Attention(nc, ctx, "ah", HEADS, SLOPE_L1, mask1, fill1,
                           smallp[:, SH:SH + HEADS * NODES], turn[:])
            ao_ = Attention(nc, ctx, "ao", 1, SLOPE_L1, mask1, fill1, smallp[:, SO:SO + NODES],
                            smallp[:, ST:ST + P].rearrange("p (h n) -> p h n", h=1))
            ws_loaded = [sem(f"ws_loaded{b}") for b in range(2)]
            a_loaded, v_part, v_hi_ready, v_lo_ready = (
                sem("a_loaded"), sem("v_part"), sem("v_hi_ready"), sem("v_lo_ready"))
            xin_loaded, xT_done, xT_hi_ready, xT_lo_ready, f_done = (
                sem("xin_loaded"), sem("xT_done"), sem("xT_hi_ready"), sem("xT_lo_ready"), sem("f_done"))
            wh_done, wh_ready, u_done, ex_ready, neg_ready, hv_ready, hT_hi_ready, hT_lo_ready = (
                sem("wh_done"), sem("wh_ready"), sem("u_done"), sem("ex_ready"), sem("neg_ready"),
                sem("hv_ready"), sem("hT_hi_ready"), sem("hT_lo_ready"))
            wo_done, who_ready, fo_part, uo_done, exo_ready, nego_ready, att_ready = (
                sem("wo_done"), sem("who_ready"), sem("fo_part"), sem("uo_done"), sem("exo_ready"),
                sem("nego_ready"), sem("att_ready"))
            layer1_sems = range(first_sem.num, att_ready.num + 1)
            a_rows = ctx.enter_context(nc.sbuf_tensor("a_rows", [P, 2 * HEADS, D], F32))
            block = ctx.enter_context(nc.Block())

            def run(eng, step):
                step(0, True, False, False)
                step(1, True, True, False)
                step(2, True, True, True)
                with eng.Fori(3, T - 1) as n:
                    step(n, True, True, True)
                step(T - 1, True, True, True)
                step(T, False, True, True)
                step(T + 1, False, False, True)

            @block.sync
            def _(sp):
                sp.dma_start(a_rows[:], ah.rearrange("h (s o) -> (h s o)", s=2).partition_broadcast(P)
                             .rearrange("p (k o) -> p k o", o=D)).then_inc(a_loaded, 16)
                sp.dma_start(ao_row[:], ao.partition_broadcast(P).rearrange("p (k o) -> p k o", o=D)
                             ).then_inc(a_loaded, 16)
                sp.dma_start(xin[:], rows(x1_rows, 0)).then_inc(xin_loaded, 16)
                Wr = Wh.rearrange("h k o -> (h k) o")
                for q in range(HEADS * KC):
                    ge(sp, v_part, 2 * (q - 1))
                    sp.dma_start(hv[q % 2][:], rows(Wr, q)).then_inc(ws_loaded[q % 2], 16)

                def store(t):
                    sp.wait_ge(att_ready, t + 1)
                    sp.dma_start(rows(att_rows, t), attT[:]).then_inc(att_stored, 16)

                def load(n):
                    sp.wait_ge(xT_done, n)
                    sp.dma_start(xin[:], rows(x1_rows, n)).then_inc(xin_loaded, 16)

                load(1)
                load(2)
                with sp.Fori(2, T - 1) as n:
                    load(n + 1)
                    store(n - 2)
                for t in range(T - 3, T):
                    store(t)
                sp.wait_ge(att_stored, 16 * T)

            @block.gpsimd
            def _(pool):
                nc.gpsimd.sem_clear(layer0_sems)
                at.pool_zero(nc)
                ao_.pool_zero(nc)

                def step(n, heads, sums, outs):
                    if heads:
                        at.pool_diag(nc, pool, n, i64)
                    if outs:
                        ao_.pool_diag(nc, pool, n - 2, i64)
                    if heads:
                        at.pool_prob(nc, pool, n)
                    if outs:
                        ao_.pool_prob(nc, pool, n - 2)
                run(pool, step)

            @block.scalar
            def _(act):
                def x_hi(t):
                    act.wait_ge(xT_done, t + 1)
                    ge(act, wh_done, 4 * t)
                    nc.scalar.copy(xT[0][:], turn[:]).then_inc(xT_hi_ready, 1)

                def head(n, h, heads, sums):
                    if sums:
                        k = 4 * (n - 1) + h
                        act.wait_ge(u_done, k + 1)
                        ge(act, hv_ready, k - 1)
                        nc.scalar.activation(ex[h % 2][:], up[U_HEAD[h]][:], ACT.Exp).then_inc(ex_ready, 1)
                    if heads:
                        act.wait_ge(wh_done, 4 * n + h + 1)
                        ge(act, u_done, 4 * (n - 1) + h + 1)
                        nc.scalar.copy(wh[:, h, :], whp[h % 2][:]).then_inc(wh_ready, 1)
                    if sums:
                        act.wait_ge(hv_ready, k + 1)
                        ge(act, wo_done, k - 1)
                        nc.scalar.copy(hT[h % 2][0][:].rearrange("p c n -> p (c n)"), hv[h % 2][:]
                                       ).then_inc(hT_hi_ready, 1)

                def step(n, heads, sums, outs):
                    head(n, 0, heads, sums)
                    if outs:
                        act.wait_ge(wo_done, 4 * (n - 1))
                        ge(act, uo_done, n - 2)
                        ge(act, ao_.f_ready, n - 2)
                        nc.scalar.copy(who[:], wop[:]).then_inc(who_ready, 1)
                    head(n, 1, heads, sums)
                    if heads:
                        at.act_exp(nc, act, n)
                    head(n, 2, heads, sums)
                    if outs:
                        ao_.act_exp(nc, act, n - 2)
                    head(n, 3, heads, sums)
                    if outs:
                        ge(act, uo_done, n - 2)
                        ao_.act_turned(nc, act, n - 2)
                    if heads and not (isinstance(n, int) and n == T - 1):
                        x_hi(n + 1)
                    if heads:
                        ge(act, u_done, 4 * n)
                        at.act_turned(nc, act, n)
                    if outs:
                        act.wait_ge(uo_done, n - 1)
                        ge(act, att_ready, n - 2)
                        act.wait_ge(ao_.f_ready, n - 1)
                        nc.scalar.activation(junk[:], up[U_OUT][:], ACT.Exp).then_inc(exo_ready, 1)

                x_hi(0)
                run(act, step)

            @block.vector
            def _(dve):
                dve.wait_ge(a_loaded, 32)
                for q in range(HEADS * KC):
                    h, c = q // KC, q % KC
                    dve.wait_ge(ws_loaded[q % 2], 16 * (q // 2 + 1))
                    for s in range(2):
                        col = h if s == 1 else HEADS + h
                        ge(dve, v_part, 2 * q + s)
                        nc.vector.tensor_tensor_reduce(out=junk[:], in0=hv[q % 2][:], in1=a_rows[:, 2 * h + s, :],
                                                       scale=1.0, scalar=0.0, op0=ALU.mult, op1=ALU.add,
                                                       accum_out=v_f[:, c, col:col + 1]).then_inc(v_part, 1)
                dve.wait_ge(v_part, 2 * HEADS * KC)
                nc.vector.tensor_copy(v_hl[:, :, 0:2 * HEADS], v_f[:]).then_inc(v_hi_ready, 1)
                dve.wait_ge(v_hi_ready, 1)
                nc.vector.tensor_tensor(v_hl[:, :, 2 * HEADS:], v_f[:], v_hl[:, :, 0:2 * HEADS].bitcast(F32),
                                        ALU.subtract).then_inc(v_lo_ready, 1)

                def x_lo(t):
                    dve.wait_ge(xT_hi_ready, t + 1)
                    nc.vector.tensor_tensor(xT[1][:], turn[:], xT[0][:].bitcast(F32), ALU.subtract
                                            ).then_inc(xT_lo_ready, 1)

                def negative(k, h):
                    dve.wait_ge(ex_ready, k + 1)
                    nc.vector.tensor_scalar(ex[h % 2][:], ex[h % 2][:], 1.0, -1.0, ALU.min, ALU.add
                                            ).then_inc(neg_ready, 1)
                    dve.wait_ge(neg_ready, k + 1)
                    ge(dve, hT_lo_ready, k - 1)
                    nc.vector.tensor_tensor(hv[h % 2][:], up[U_HEAD[h]][:], ex[h % 2][:], ALU.max
                                            ).then_inc(hv_ready, 1)

                def low(k, h):
                    dve.wait_ge(hT_hi_ready, k + 1)
                    nc.vector.tensor_tensor(hT[h % 2][1][:].rearrange("p c n -> p (c n)"), hv[h % 2][:],
                                            hT[h % 2][0][:].bitcast(F32).rearrange("p c n -> p (c n)"),
                                            ALU.subtract).then_inc(hT_lo_ready, 1)

                def step(n, heads, sums, outs):
                    k = 4 * (n - 1)
                    if heads:
                        dve.wait_ge(f_done, n + 1)
                        ge(dve, at.diag_ready, n)
                        ge(dve, at.summed, n)
                        nc.vector.reduce_sum(at.f[:], smallp[:, SF:SF + 4 * HEADS]
                                             .rearrange("p (s k) -> p k s", s=2), AX_X).then_inc(at.f_ready, 1)
                    if sums:
                        negative(k, 0)
                        low(k, 0)
                    if outs:
                        dve.wait_ge(who_ready, n - 1)
                        ge(dve, ao_.diag_ready, n - 2)
                        ge(dve, ao_.summed, n - 2)
                        ge(dve, att_ready, n - 2)
                        nc.vector.tensor_tensor_reduce(
                            out=junk[:], in0=who[:], in1=ao_row[:, 0, :], scale=1.0, scalar=0.0,
                            op0=ALU.mult, op1=ALU.add, accum_out=ao_.f[:, 1:2]).then_inc(fo_part, 1)
                        dve.wait_ge(fo_part, n - 1)
                        nc.vector.tensor_tensor_reduce(
                            out=junk[:], in0=who[:], in1=ao_row[:, 1, :], scale=1.0, scalar=0.0,
                            op0=ALU.mult, op1=ALU.add, accum_out=ao_.f[:, 0:1]).then_inc(ao_.f_ready, 1)
                    if heads:
                        at.dve_before_exp(nc, dve, n, fill1)
                    if sums:
                        negative(k + 1, 1)
                        low(k + 1, 1)
                    if outs:
                        ao_.dve_before_exp(nc, dve, n - 2, fill1)
                    if heads:
                        at.dve_after_exp(nc, dve, n)
                    if sums:
                        negative(k + 2, 2)
                    if outs:
                        ao_.dve_after_exp(nc, dve, n - 2)
                    if sums:
                        low(k + 2, 2)
                        negative(k + 3, 3)
                        low(k + 3, 3)
                    if heads and not (isinstance(n, int) and n == T - 1):
                        x_lo(n + 1)
                    if outs:
                        dve.wait_ge(exo_ready, n - 1)
                        nc.vector.tensor_scalar(junk[:], junk[:], 1.0, -1.0, ALU.min, ALU.add
                                                ).then_inc(nego_ready, 1)
                        dve.wait_ge(nego_ready, n - 1)
                        ge(dve, att_stored, 16 * (n - 2))
                        nc.vector.tensor_tensor(attT[:], up[U_OUT][:], junk[:], ALU.max
                                                ).then_inc(att_ready, 1)

                x_lo(0)
                run(dve, step)

            @block.tensor
            def _(pe):
                def turn_x(t):
                    pe.wait_ge(xin_loaded, 16 * t + 16)
                    ge(pe, at.turned_ready, 2 * (t - 1))
                    for c in range(KC):
                        ins = nc.tensor.transpose(turn[:, c, :], xin[:, c * P:(c + 1) * P], ident[:])
                    ins.then_inc(xT_done, 1)

                def sums_of(m, h):
                    k = 4 * m + h
                    pe.wait_ge(wh_ready, k + 1)
                    if h == 1:
                        ge(pe, att_ready, m - 1)
                    else:
                        ge(pe, hv_ready, {0: k, 2: k - 3, 3: k - 2}[h])
                    for c in range(KC):
                        ins = nc.tensor.matmul(up[U_HEAD[h]][:, c * P:(c + 1) * P],
                                               wh[:, h, c * P:(c + 1) * P], at.turned[:, h, :],
                                               start=True, stop=True)
                    ins.then_inc(u_done, 1)

                def project(n, h):
                    ge(pe, wh_ready, 4 * n + h - 1)
                    product(nc, whp[h % 2][:], xT, (big_hi, big_lo),
                            [(c, h * KC + c) for c in range(KC)]).then_inc(wh_done, 1)

                def out_part(k, h):
                    pe.wait_ge(hT_lo_ready, k + 1)
                    pe.wait_ge(hT_hi_ready, k + 1)
                    product(nc, wop[:], hT[h % 2], (big_hi, big_lo),
                            [(c, (HEADS + h) * KC + c) for c in range(KC)],
                            first=h == 0, last=h == HEADS - 1).then_inc(wo_done, 1)

                def step(n, heads, sums, outs):
                    k = 4 * (n - 1)
                    if heads:
                        pe.wait_ge(xT_hi_ready, n + 1)
                        pe.wait_ge(xT_lo_ready, n + 1)
                        ge(pe, at.summed, n)
                        ge(pe, ao_.turned_ready, 2 * (n - 2))
                        for c in range(KC):
                            nc.tensor.matmul(smallp[:, SF:SF + 4 * HEADS], xT[0][:, c, :], v_hl[:, c, :],
                                             start=c == 0, stop=False)
                            ins = nc.tensor.matmul(smallp[:, SF:SF + 2 * HEADS], xT[1][:, c, :],
                                                   v_hl[:, c, 0:2 * HEADS], start=False, stop=c == KC - 1)
                        ins.then_inc(f_done, 1)
                    for h in range(HEADS):
                        if sums:
                            if h == 0:
                                pe.wait_ge(at.turned_ready, 2 * n)
                            sums_of(n - 1, h)
                        if heads:
                            project(n, h)
                        if heads and h == 3 and not (isinstance(n, int) and n == T - 1):
                            turn_x(n + 1)
                        if h == 0:
                            if outs:
                                out_part(k - 1, 3)
                            if heads:
                                at.pe_scores(nc, pe, n, same_graph)
                        else:
                            if sums:
                                if h == 1:
                                    ge(pe, who_ready, n - 1)
                                out_part(k + h - 1, h - 1)
                            if outs and h == 1:
                                ge(pe, at.summed, n + 1 if heads else T)
                                ao_.pe_scores(nc, pe, n - 2, same_graph)
                            if outs and h == 2:
                                pe.wait_ge(ao_.summed, n - 1)
                                ao_.pe_turn(nc, pe, n - 2, ident)
                    if outs:
                        pe.wait_ge(ao_.turned_ready, 2 * (n - 1))
                        if sums:
                            pe.wait_ge(hv_ready, k + 2)
                        for c in range(KC):
                            ins = nc.tensor.matmul(up[U_OUT][:, c * P:(c + 1) * P], who[:, c * P:(c + 1) * P],
                                                   ao_.turned[:, 0, :], start=True, stop=True)
                        ins.then_inc(uo_done, 1)
                    if heads:
                        if not (isinstance(n, int) and n == T - 1):
                            pe.wait_ge(xT_lo_ready, n + 2)
                        at.pe_turn(nc, pe, n, ident)

                turn_x(0)
                pe.wait_ge(v_hi_ready, 1)
                pe.wait_ge(v_lo_ready, 1)
                run(pe, step)

        with nc.Block() as block:
            @block.gpsimd
            def _(pool):
                nc.gpsimd.sem_clear(layer1_sems)

        held.close()
        with ExitStack() as ctx:
            def sb(n, shape, dt=F32):
                return ctx.enter_context(nc.sbuf_tensor(n, shape, dt))

            def sem(n):
                return ctx.enter_context(nc.semaphore(n))

            def pb(n, shape):
                return ctx.enter_context(nc.psum_tensor(n, shape, F32))

            R = 4
            w_hi = sb("w_hi", [P, 4 * KC, D], F32R)
            w_lo = sb("w_lo", [P, 4 * KC, D], F32R)
            stage = [sb(f"stage{b}", [P, KC, D]) for b in range(2)]
            att = [sb(f"att{b}", [P, D]) for b in range(2)]
            attS = [(sb(f"att_hi{b}", [P, KC, P], F32R), sb(f"att_lo{b}", [P, KC, P], F32R)) for b in range(2)]
            h1 = sb("h1", [P, D])
            h1T = (sb("h1T_hi", [P, KC, P], F32R), sb("h1T_lo", [P, KC, P], F32R))
            x1 = [sb(f"x1r{b}", [P, D]) for b in range(2)]
            x1b = sb("x1b", [P, D])
            ident_r = sb("ident_r", [P, P], F32R)
            sixty_fourth = sb("sixty_fourth", [P, P], F32R)
            b2_halves = sb("b2_halves", [P, D], F32R)
            y = sb("y", [P, D])
            z1 = sb("z1", [P, D])
            x2 = [sb(f"x2_{r}", [P, D]) for r in range(R)]
            x3 = [sb(f"x3_{b}", [P, D]) for b in range(2)]
            res = sb("res", [P, D])
            b1_row, b2_row, gamma_row, beta_row = (sb("b1_row", [P, D]), sb("b2_row", [P, D]),
                                                   sb("gamma_row", [P, D]), sb("beta_row", [P, D]))
            a_row = sb("a_row", [P, 4, D])
            v_f = sb("v2_f", [P, KC, 4])
            scrap = sb("scrap", [P, D])
            bank_a, bank_b = pb("bank_a", [P, D]), pb("bank_b", [P, D])
            turn_h, turn_2, turn_3 = (pb("turn_h", [P, KC, P]), pb("turn_2", [P, KC, P]),
                                      pb("turn_3", [P, KC, P]))
            smallp = pb("smallq", [P, D])
            n_y, n_1 = Norm(nc, ctx, "ny"), Norm(nc, ctx, "n1")

            class Gat:

                def __init__(self, name, q, base, tp, prod):
                    self.q, self.turn, self.prod = q, tp, prod
                    self.f_psum = smallp[:, 0:P]
                    self.att = Attention(nc, ctx, name, 1, SLOPE_L23, mask23, fill23, smallp[:, base:base + P],
                                         smallp[:, 3 * P:].rearrange("p (h n) -> p h n", h=1))
                    self.left = sb(name + "_left", [P, P])
                    self.right = sb(name + "_right", [P, P])
                    self.sides_ready = sem(name + "_sides_ready")
                    self.xT = (sb(name + "_xT_hi", [P, KC, P], F32R), sb(name + "_xT_lo", [P, KC, P], F32R))
                    self.v = (sb(name + "_v_hi", [P, KC, P], F32R),
                              sb(name + "_v_lo", [P, KC, P], F32R))
                    self.v_zero = sem(name + "_v_zero")
                    self.wh = sb(name + "_wh", [P, D])
                    self.z = sb(name + "_z", [P, D])
                    self.sums = pb(name + "_sums", [P, D])
                    self.norm = Norm(nc, ctx, name + "_n")
                    self.xT_done, self.xT_hi_ready, self.xT_lo_ready = (
                        sem(name + "_xT_done"), sem(name + "_xT_hi_ready"), sem(name + "_xT_lo_ready"))
                    self.f_done, self.wh_done, self.wh_ready, self.sums_done, self.z_ready, self.x_ready = (
                        sem(name + "_f_done"), sem(name + "_wh_done"), sem(name + "_wh_ready"),
                        sem(name + "_sums_done"), sem(name + "_z_ready"), sem(name + "_x_ready"))
                    self.v_hi_ready, self.v_lo_ready = sem(name + "_v_hi_ready"), sem(name + "_v_lo_ready")

            g2 = Gat("g2", 2 * KC, P, turn_2, bank_b)
            g3 = Gat("g3", 3 * KC, 2 * P, turn_3, bank_a)
            weights = (w1, w2, W2, W3)
            w_loaded = [sem(f"w_loaded{b}") for b in range(2)]
            w_hi_ready, w_lo_ready, v_part, rows_loaded = (
                sem("w_hi_ready"), sem("w_lo_ready"), sem("v2_part"), sem("rows_loaded"))
            att_loaded = [sem(f"att_loaded{b}") for b in range(2)]
            x1_loaded = [sem(f"x1_loaded{b}") for b in range(2)]
            att_hi_ready, att_lo_ready, h1_done, h1_ready, h1T_done, h1T_hi_ready, h1T_lo_ready = (
                sem("att_hi_ready"), sem("att_lo_ready"), sem("h1_done"), sem("h1_ready"), sem("h1T_done"),
                sem("h1T_hi_ready"), sem("h1T_lo_ready"))
            y_done, scaled, x1b_ready, z1_ready, x2_ready = (
                sem("y_done"), sem("scaled"), sem("x1b_ready"), sem("z1_ready"), sem("x2_ready"))
            ident_r_ready, b2_ready = sem("ident_r_ready"), sem("b2_ready")
            res_stored = sem("res_stored")
            block = ctx.enter_context(nc.Block())

            def run(eng, step):
                for n in range(2 * R):
                    step(n, n % R)
                with eng.Fori(2, T // R) as g:
                    n = g * R
                    for r in range(R):
                        step(n + r, r)
                for n in range(T, T + 4):
                    step(n, n % R)

            def live(n, lag):
                return not isinstance(n, int) or 0 <= n - lag < T

            def pair(t, r):
                return 16 * (t // 2 + 1) if isinstance(t, int) else 8 * (t - r % 2) + 16

            @block.sync
            def _(sp):
                for row, src in ((b1_row, b1), (b2_row, b2), (gamma_row, gamma), (beta_row, beta)):
                    sp.dma_start(row[:], src.partition_broadcast(P)).then_inc(rows_loaded, 16)
                for k, src in enumerate((a2d, a2s, a3d, a3s)):
                    sp.dma_start(a_row[:, k, :], src.partition_broadcast(P)).then_inc(rows_loaded, 16)
                for k, w in enumerate(weights):
                    ge(sp, w_lo_ready, k - 1)
                    sp.dma_start(stage[k % 2][:], chunked(w)).then_inc(w_loaded[k % 2], 16)
                    if k < 2:
                        sp.dma_start(att[k][:], rows(att_rows, k)).then_inc(att_loaded[k], 16)
                        sp.dma_start(x1[k][:], rows(x1_rows, k)).then_inc(x1_loaded[k], 16)

                def step(n, r):
                    if live(n, 4):
                        sp.wait_ge(g3.x_ready, n - 3)
                        sp.dma_start(rows(out_rows, n - 4), res[:]).then_inc(res_stored, 16)
                    if live(n, 0) and live(n, -2):
                        if isinstance(n, int) or True:
                            sp.wait_ge(att_lo_ready, n + 1)
                            sp.dma_start(att[r % 2][:], rows(att_rows, n + 2)).then_inc(att_loaded[r % 2], 16)
                            sp.wait_ge(x1b_ready, n + 1)
                            sp.dma_start(x1[r % 2][:], rows(x1_rows, n + 2)).then_inc(x1_loaded[r % 2], 16)

                for n in range(2 * R):
                    step(n, n % R)
                with sp.Fori(2, T // R - 1) as g:
                    n = g * R
                    for r in range(R):
                        step(n + r, r)
                for n in range(T - R, T + 4):
                    step(n, n % R)
                sp.wait_ge(res_stored, 16 * T)

            @block.gpsimd
            def _(pool):
                g2.att.pool_zero(nc)
                g3.att.pool_zero(nc)
                for g in (g2, g3):
                    nc.gpsimd.memset(g.v[0][:].bitcast(I32), 0).then_inc(g.v_zero, 1)
                    nc.gpsimd.memset(g.v[1][:].bitcast(I32), 0).then_inc(g.v_zero, 1)
                nc.gpsimd.memset(sixty_fourth[:].bitcast(F32), 1.0 / NODES).then_inc(b2_ready, 1)
                pool.wait_ge(rows_loaded, 128)

                def att_lo(t, r):
                    pool.wait_ge(att_hi_ready, t + 1)
                    nc.gpsimd.tensor_tensor(attS[r % 2][1][:].rearrange("p c n -> p (c n)"), att[r % 2][:],
                                            attS[r % 2][0][:].bitcast(F32).rearrange("p c n -> p (c n)"),
                                            ALU.subtract).then_inc(att_lo_ready, 1)

                def step(n, r):
                    if live(n, 4):
                        g3.norm.pool_rstd(nc, pool, n - 4, g3.x_ready, neg_half)
                    if live(n, 0):
                        pool.wait_ge(x1_loaded[r % 2], pair(n, r))
                        ge(pool, z1_ready, n)
                        nc.gpsimd.tensor_tensor(x1b[:], x1[r % 2][:], beta_row[:], ALU.add
                                                ).then_inc(x1b_ready, 1)
                    if live(n, 2):
                        g2.att.pool_prob(nc, pool, n - 2, gate)
                    if live(n, 3):
                        g3.att.pool_prob(nc, pool, n - 3, gate)
                    if live(n, -1):
                        att_lo(n + 1, (r + 1) % R)
                    if live(n, 0):
                        n_y.pool_rstd(nc, pool, n, z1_ready, neg_half)
                    if live(n, 2):
                        g2.norm.pool_rstd(nc, pool, n - 2, g2.x_ready, neg_half)
                    if live(n, 0):
                        n_1.pool_rstd(nc, pool, n, x2_ready, neg_half)

                att_lo(0, 0)
                for n in range(2 * R):
                    step(n, n % R)
                with pool.Fori(2, T // R - 1) as g:
                    n = g * R
                    for r in range(R):
                        step(n + r, r)
                for n in range(T - R, T + 4):
                    step(n, n % R)

            @block.scalar
            def _(act):
                def att_hi(t, r):
                    act.wait_ge(att_loaded[r % 2], pair(t, r))
                    ge(act, y_done, t - 1)
                    nc.scalar.copy(attS[r % 2][0][:].rearrange("p c n -> p (c n)"), att[r % 2][:]
                                   ).then_inc(att_hi_ready, 1)

                def x_hi(g, t):
                    act.wait_ge(g.xT_done, t + 1)
                    ge(act, g.wh_done, t)
                    nc.scalar.copy(g.xT[0][:], g.turn[:]).then_inc(g.xT_hi_ready, 1)

                def wh_out(g, t):
                    act.wait_ge(g.wh_done, t + 1)
                    ge(act, g.sums_done, t)
                    nc.scalar.copy(g.wh[:], g.prod[:]).then_inc(g.wh_ready, 1)

                def turned(g, t):
                    ge(act, g.sums_done, t)
                    g.att.act_turned(nc, act, t)

                def step(n, r):
                    if live(n, 4):
                        turned(g3, n - 4)
                    if live(n, 3):
                        x_hi(g3, n - 3)
                    if live(n, -1):
                        att_hi(n + 1, (r + 1) % R)
                    if live(n, 2):
                        wh_out(g2, n - 2)
                    if live(n, 0):
                        act.wait_ge(h1T_done, n + 1)
                        ge(act, y_done, n)
                        nc.scalar.activation(h1T[0][:], turn_h[:], ACT.Relu).then_inc(h1T_hi_ready, 1)
                    if live(n, 1):
                        x_hi(g2, n - 1)
                    if live(n, 2):
                        g2.att.act_exp(nc, act, n - 2)
                    if live(n, 3):
                        wh_out(g3, n - 3)
                        g3.att.act_exp(nc, act, n - 3)
                    if live(n, 2):
                        turned(g2, n - 2)

                for k in range(4):
                    act.wait_ge(w_loaded[k % 2], 16 * (k // 2 + 1))
                    nc.scalar.copy(w_hi[:, k * KC:(k + 1) * KC, :], stage[k % 2][:]
                                   ).then_inc(w_hi_ready, 1)
                    if k == 0:
                        att_hi(0, 0)
                for n in range(2 * R):
                    step(n, n % R)
                with act.Fori(2, T // R - 1) as g:
                    n = g * R
                    for r in range(R):
                        step(n + r, r)
                for n in range(T - R, T + 4):
                    step(n, n % R)

            @block.vector
            def _(dve):
                dve.wait_ge(rows_loaded, 128)
                nc.vector.tensor_copy(ident_r[:], ident[:]).then_inc(ident_r_ready, 1)
                nc.vector.tensor_copy(b2_halves[:], b2_row[:]).then_inc(ident_r_ready, 1)
                dve.wait_ge(ident_r_ready, 2)
                nc.vector.tensor_tensor(b2_halves[NODES:, :], b2_row[NODES:, :], b2_halves[NODES:, :].bitcast(F32),
                                        ALU.subtract).then_inc(b2_ready, 1)
                for k in range(4):
                    dve.wait_ge(w_hi_ready, k + 1)
                    nc.vector.tensor_tensor(w_lo[:, k * KC:(k + 1) * KC, :], stage[k % 2][:],
                                            w_hi[:, k * KC:(k + 1) * KC, :].bitcast(F32),
                                            ALU.subtract).then_inc(w_lo_ready, 1)
                    if k < 2:
                        continue
                    g = (g2, g3)[k - 2]
                    for c in range(KC):
                        for s in range(2):
                            j = 2 * KC * (k - 2) + 2 * c + s
                            ge(dve, v_part, j)
                            nc.vector.tensor_tensor_reduce(
                                out=scrap[:], in0=stage[k % 2][:, c, :], in1=a_row[:, 2 * (k - 2) + s, :],
                                scale=1.0, scalar=0.0, op0=ALU.mult, op1=ALU.add,
                                accum_out=v_f[:, c, 2 * (k - 2) + s:2 * (k - 2) + s + 1]).then_inc(v_part, 1)
                    dve.wait_ge(v_part, 2 * KC * (k - 1))
                    own = v_f[:, :, 2 * (k - 2):2 * (k - 1)]
                    dve.wait_ge(g.v_zero, 2)
                    nc.vector.tensor_copy(g.v[0][:, :, 0:2], own).then_inc(g.v_hi_ready, 1)
                    dve.wait_ge(g.v_hi_ready, 1)
                    nc.vector.tensor_tensor(g.v[1][:, :, 0:2], own, g.v[0][:, :, 0:2].bitcast(F32), ALU.subtract
                                            ).then_inc(g.v_lo_ready, 1)

                def x_lo(g, t):
                    dve.wait_ge(g.xT_hi_ready, t + 1)
                    nc.vector.tensor_tensor(g.xT[1][:], g.turn[:], g.xT[0][:].bitcast(F32), ALU.subtract
                                            ).then_inc(g.xT_lo_ready, 1)

                def sides(g, t):
                    dve.wait_ge(g.f_done, t + 1)
                    ge(dve, g.att.scores_done, t)
                    one, two = ident[0:2, 0:1], ident[0:2, 1:2]
                    nc.vector.tensor_scalar(g.left[0:2, :], g.f_psum[0:2, :], two, one, ALU.mult, ALU.add
                                            ).then_inc(g.sides_ready, 1)
                    nc.vector.tensor_scalar(g.right[0:2, :], g.f_psum[0:2, :], one, two, ALU.mult, ALU.add
                                            ).then_inc(g.sides_ready, 1)

                def leaky(g, t):
                    a = g.att
                    dve.wait_ge(a.scores_done, t + 1)
                    ge(dve, a.exp_ready, t)
                    for h in range(2):
                        r = slice(h * NODES, (h + 1) * NODES)
                        nc.vector.tensor_copy(a.e1[r, 0, :], a.scores_psum[r, r]).then_inc(a.summed, 1)
                    dve.wait_ge(a.summed, 2 * t + 2)
                    nc.vector.scalar_tensor_tensor(a.e2[:], a.e1[:], SLOPE_L23, a.e1[:], ALU.mult, ALU.max
                                                   ).then_inc(a.leaky, 1)

                def mask(g, t):
                    dve.wait_ge(g.att.leaky, t + 1)
                    nc.vector.memset(g.att.pause[:], 0.0)
                    nc.vector.copy_predicated(g.att.e2[:, 0, :], mask23[:],
                                              fill23[:, 0:1].to_broadcast([P, NODES])).then_inc(g.att.masked, 1)

                def peak(g, t):
                    dve.wait_ge(g.att.masked, t + 1)
                    nc.vector.reduce_max(g.att.peak[:], g.att.e2[:], AX_X).then_inc(g.att.peaked, 1)

                def shift(g, t):
                    dve.wait_ge(g.att.peaked, t + 1)
                    nc.vector.tensor_scalar(g.att.e1[:, 0, :], g.att.e2[:, 0, :], g.att.peak[:], None,
                                            ALU.subtract).then_inc(g.att.shifted, 1)

                def residual(g, t, x):
                    dve.wait_ge(g.sums_done, t + 1)
                    ge(dve, g.x_ready, t)
                    nc.vector.tensor_tensor(g.z[:], g.sums[:], x, ALU.add).then_inc(g.z_ready, 1)
                    dve.wait_ge(g.z_ready, t + 1)
                    g.norm.dve_stats(nc, dve, t, g.z[:], g.x_ready)

                def normalise(norm, t, z, x, ready):
                    dve.wait_ge(norm.rstd_ready, t + 1)
                    nc.vector.tensor_scalar(x, z, norm.mv[:, 0:1], norm.rstd[:], ALU.subtract, ALU.mult
                                            ).then_inc(ready, 1)

                def step(n, r):
                    if live(n, 1):
                        ge(dve, g2.z_ready, n - 4)
                        normalise(n_1, n - 1, z1[:], x2[(r - 1) % R][:], x2_ready)
                    if live(n, 0):
                        dve.wait_ge(h1_done, n + 1)
                        ge(dve, h1T_done, n)
                        nc.vector.tensor_tensor(h1[:], bank_a[:], b1_row[:], ALU.add).then_inc(h1_ready, 1)
                    if live(n, 4):
                        residual(g3, n - 4, x3[r % 2][:])
                    if live(n, 3):
                        x_lo(g3, n - 3)
                    if live(n, 2):
                        sides(g2, n - 2)
                    if live(n, 4):
                        ge(dve, res_stored, 16 * (n - 4))
                        normalise(g3.norm, n - 4, g3.z[:], res[:], g3.x_ready)
                    if live(n, 2):
                        leaky(g2, n - 2)
                        mask(g2, n - 2)
                        peak(g2, n - 2)
                        shift(g2, n - 2)
                    if live(n, 0):
                        dve.wait_ge(h1T_hi_ready, n + 1)
                        nc.vector.scalar_tensor_tensor(h1T[1][:], turn_h[:], 0.0, h1T[0][:].bitcast(F32),
                                                       ALU.max, ALU.subtract).then_inc(h1T_lo_ready, 1)
                    if live(n, 1):
                        x_lo(g2, n - 1)
                    if live(n, 2):
                        g2.att.dve_after_exp(nc, dve, n - 2, gate)
                    if live(n, 3):
                        sides(g3, n - 3)
                        leaky(g3, n - 3)
                        mask(g3, n - 3)
                        peak(g3, n - 3)
                        shift(g3, n - 3)
                        g3.att.dve_after_exp(nc, dve, n - 3, gate)
                    if live(n, 0):
                        dve.wait_ge(y_done, n + 1)
                        n_y.dve_stats(nc, dve, n, bank_b[:], scaled)
                    if live(n, 2):
                        residual(g2, n - 2, x2[(r - 2) % R][:])
                    if live(n, 0):
                        ge(dve, z1_ready, n)
                        nc.vector.scalar_tensor_tensor(y[:], bank_b[:], n_y.mv[:, 0:1], gamma_row[:],
                                                       ALU.subtract, ALU.mult).then_inc(scaled, 1)
                    if live(n, 2):
                        ge(dve, g3.z_ready, n - 3)
                        normalise(g2.norm, n - 2, g2.z[:], x3[r % 2][:], g2.x_ready)
                    if live(n, 0):
                        dve.wait_ge(scaled, n + 1)
                        dve.wait_ge(n_y.rstd_ready, n + 1)
                        dve.wait_ge(x1b_ready, n + 1)
                        ge(dve, x2_ready, n)
                        nc.vector.scalar_tensor_tensor(z1[:], y[:], n_y.rstd[:], x1b[:], ALU.mult, ALU.add
                                                       ).then_inc(z1_ready, 1)
                        dve.wait_ge(z1_ready, n + 1)
                        n_1.dve_stats(nc, dve, n, z1[:], x2_ready)

                run(dve, step)

            @block.tensor
            def _(pe):
                def turn_x(g, t, x, ready):
                    pe.wait_ge(ready, t + 1)
                    ge(pe, g.xT_lo_ready, t)
                    for c in range(KC):
                        ins = nc.tensor.transpose(g.turn[:, c, :], x[:, c * P:(c + 1) * P], ident[:])
                    ins.then_inc(g.xT_done, 1)

                def project(g, t):
                    pe.wait_ge(g.xT_lo_ready, t + 1)
                    if isinstance(t, int) and t == 0:
                        pe.wait_ge(g.v_hi_ready, 1)
                        pe.wait_ge(g.v_lo_ready, 1)
                        pe.wait_ge(w_lo_ready, g.q // KC + 1)
                    for c in range(KC):
                        for q, (a, b) in enumerate(split_passes(g.v[0][:, c, :], g.v[1][:, c, :],
                                                                g.xT[0][:, c, :], g.xT[1][:, c, :])):
                            ins = nc.tensor.matmul(g.f_psum, a, b, start=c == 0 and q == 0,
                                                   stop=c == KC - 1 and q == 2)
                    ins.then_inc(g.f_done, 1)
                    product(nc, g.prod[:], g.xT, (w_hi, w_lo),
                            [(c, g.q + c) for c in range(KC)]).then_inc(g.wh_done, 1)
                    pe.wait_ge(g.sides_ready, 2 * t + 2)
                    nc.tensor.matmul(g.att.scores_psum, g.left[0:2, :], g.right[0:2, :],
                                     start=True, stop=True).then_inc(g.att.scores_done, 1)

                def sums(g, t):
                    pe.wait_ge(g.att.turned_ready, 2 * t + 2)
                    pe.wait_ge(g.wh_ready, t + 1)
                    ge(pe, g.z_ready, t)
                    nc.tensor.matmul(g.sums[:], g.att.turned[:, 0, :], g.wh[:], start=True, stop=True
                                     ).then_inc(g.sums_done, 1)

                def step(n, r):
                    if live(n, 4):
                        if live(n, 3):
                            pe.wait_ge(g3.att.summed, 2 * (n - 3))
                        if live(n, 3):
                            ge(pe, g2.att.turned_ready, 2 * (n - 2))
                        g3.att.pe_turn(nc, pe, n - 4, ident)
                    if live(n, 0):
                        pe.wait_ge(att_lo_ready, n + 1)
                        ge(pe, g3.wh_ready, n - 3)
                        ge(pe, h1_ready, n)
                        product(nc, bank_a[:], attS[r % 2], (w_hi, w_lo), [(c, c) for c in range(KC)]
                                ).then_inc(h1_done, 1)
                    if live(n, 4):
                        sums(g3, n - 4)
                    if live(n, 3):
                        turn_x(g3, n - 3, x3[(r - 1) % 2], g2.x_ready)
                    if live(n, 2):
                        ge(pe, scaled, capped(n, T))
                        if live(n, 3):
                            pe.wait_ge(g2.att.turned_ready, 2 * (n - 2))
                        project(g2, n - 2)
                    if live(n, 0):
                        pe.wait_ge(h1_ready, n + 1)
                        ge(pe, h1T_lo_ready, n)
                        for c in range(KC):
                            ins = nc.tensor.transpose(turn_h[:, c, :], h1[:, c * P:(c + 1) * P], ident[:])
                        ins.then_inc(h1T_done, 1)
                    if live(n, 1):
                        turn_x(g2, n - 1, x2[(r - 1) % R], x2_ready)
                    if live(n, 3):
                        if live(n, 0):
                            pe.wait_ge(h1_ready, n + 1)
                        if live(n, 2):
                            pe.wait_ge(g2.att.summed, 2 * (n - 1))
                        project(g3, n - 3)
                    if live(n, 2):
                        if live(n, 3):
                            pe.wait_ge(g3.att.summed, 2 * (n - 2))
                        g2.att.pe_turn(nc, pe, n - 2, ident)
                    if live(n, 0):
                        if isinstance(n, int) and n == 0:
                            pe.wait_ge(ident_r_ready, 2)
                            pe.wait_ge(b2_ready, 2)
                        pe.wait_ge(h1T_lo_ready, n + 1)
                        ge(pe, g2.wh_ready, n - 1)
                        ge(pe, scaled, n)
                        product(nc, bank_b[:], h1T, (w_hi, w_lo), [(c, KC + c) for c in range(KC)], last=False)
                        nc.tensor.matmul(bank_b[:], sixty_fourth[:], b2_halves[:], start=False, stop=False)
                        for c in range(KC):
                            for k in range(2):
                                ins = nc.tensor.matmul(bank_b[:, c * P:(c + 1) * P], attS[r % 2][k][:, c, :], ident_r[:],
                                                       start=False, stop=c == KC - 1 and k == 1)
                        ins.then_inc(y_done, 1)
                    if live(n, 2):
                        sums(g2, n - 2)

                pe.wait_ge(w_lo_ready, 2)
                run(pe, step)


_INS = ['x', 'adj', 'L0_gnn_W', 'L0_gnn_b', 'L1_gnn_W_heads', 'L1_gnn_a_heads', 'L1_gnn_W_out', 'L1_gnn_a_out',
        'L1_gnn_w1', 'L1_gnn_b1', 'L1_gnn_w2', 'L1_gnn_b2', 'L1_gnn_ln_gamma', 'L1_gnn_ln_beta',
        'L2_gnn_W', 'L2_gnn_a_src', 'L2_gnn_a_dst', 'L3_gnn_W', 'L3_gnn_a_src', 'L3_gnn_a_dst']


def kernel(**inputs):
    import numpy as _np
    import concourse.bacc as _bacc
    from concourse import mybir as _mybir
    from concourse.bass_utils import run_bass_kernel_spmd as _run

    nc = _bacc.Bacc("TRN2", target_bir_lowering=False, num_devices=1)
    arrays, args = {}, []
    for name in _INS:
        a = _np.asarray(inputs[name])
        if name == 'L0_gnn_W':
            a = a.T
        a = _np.ascontiguousarray(a)
        arrays[f"in_{name}"] = a
        args.append(nc.dram_tensor(f"in_{name}", a.shape, _mybir.dt.from_np(a.dtype), kind="ExternalInput").ap())
    shape = inputs['x'].shape
    out = nc.dram_tensor("out_0", shape, _mybir.dt.float32, kind="ExternalOutput").ap()
    gnn_stack_kernel(nc, *args, out)
    r = _run(nc, [arrays], core_ids=[0])
    return r.results[0]["out_0"]
```

```python
from contextlib import ExitStack

import concourse.bass as bass
from concourse import mybir

F32 = mybir.dt.float32
F32R = mybir.dt.float32r
I32 = mybir.dt.int32
ALU = mybir.AluOpType
ACT = mybir.ActivationFunctionType
AX_X = mybir.AxisListType.X

P = 128
D = 512
KC = D // P
NODES = 64
HEADS = 4
LN_EPS = 1e-5
SLOPE_L1 = 0.01
SLOPE_L23 = 0.2
MASKED_L1 = -1e9
MASKED_L23 = -3e38


def ge(eng, sem, value):
    if not isinstance(value, int) or value > 0:
        eng.wait_ge(sem, value)


def capped(n, most):
    return min(n, most) if isinstance(n, int) else n


def split_passes(hi_lhs, lo_lhs, hi_rhs, lo_rhs):
    return ((hi_lhs, hi_rhs), (hi_lhs, lo_rhs), (lo_lhs, hi_rhs))


def product(nc, out, lhs, rhs, chunks, first=True, last=True):
    n = len(chunks)
    for c, (kl, kr) in enumerate(chunks):
        passes = split_passes(lhs[0][:, kl, :], lhs[1][:, kl, :], rhs[0][:, kr, :], rhs[1][:, kr, :])
        for q, (a, b) in enumerate(passes):
            ins = nc.tensor.matmul(out, a, b, start=first and c == 0 and q == 0,
                                   stop=last and c == n - 1 and q == 2)
    return ins


class Attention:

    def __init__(self, nc, ctx, name, heads, slope, scores_psum, turned_psum, mask=None):
        def sb(n, shape, dt=F32):
            return ctx.enter_context(nc.sbuf_tensor(f"{name}_{n}", shape, dt))

        def sem(n):
            return ctx.enter_context(nc.semaphore(f"{name}_{n}"))

        self.heads, self.slope, self.mask = heads, slope, mask
        self.scores_psum = scores_psum
        self.turned_psum = turned_psum
        self.f = sb("f", [P, 2 * heads])
        self.diag = sb("diag", [P, heads, NODES])
        self.e1 = sb("e1", [P, heads, NODES])
        self.e2 = sb("e2", [P, heads, NODES])
        self.ex = sb("ex", [P, heads, NODES])
        self.peak = sb("peak", [P, heads])
        self.total = sb("total", [P, heads])
        self.inv = sb("inv", [P, heads])
        self.prob = sb("prob", [P, heads, 2, NODES])
        self.turned = sb("turned", [P, heads, P])
        self.pause = sb("pause", [P, 1])
        self.zeroed = sem("zeroed")
        self.f_ready, self.diag_ready, self.scores_done = sem("f_ready"), sem("diag_ready"), sem("scores_done")
        self.summed, self.leaky, self.masked = sem("summed"), sem("leaky"), sem("masked")
        self.peaked, self.shifted, self.exp_ready = sem("peaked"), sem("shifted"), sem("exp_ready")
        self.totalled, self.inverted, self.gated = sem("totalled"), sem("inverted"), sem("gated")
        self.prob_ready, self.turned_done, self.turned_ready = (
            sem("prob_ready"), sem("turned_done"), sem("turned_ready"))

    def pool_zero(self, nc):
        nc.gpsimd.memset(self.turned[:], 0.0).then_inc(self.zeroed, 1)

    def pool_diag(self, nc, pool, t, i64):
        pool.wait_ge(self.f_ready, t + 1)
        ge(pool, self.scores_done, t)
        shape = [P, self.heads, NODES]
        nc.gpsimd.tensor_tensor(self.diag[:], i64[:, None, :].to_broadcast(shape),
                                self.f[:, 0:self.heads, None].to_broadcast(shape),
                                ALU.mult).then_inc(self.diag_ready, 1)

    def pe_scores(self, nc, pe, t, same_graph):
        pe.wait_ge(self.diag_ready, t + 1)
        ge(pe, self.summed, t)
        nc.tensor.matmul(self.scores_psum, same_graph[:], self.diag[:].rearrange("p h j -> p (h j)"),
                         start=True, stop=True).then_inc(self.scores_done, 1)

    def dve_before_exp(self, nc, dve, t, fill):
        shape = [P, self.heads, NODES]
        dve.wait_ge(self.scores_done, t + 1)
        dve.wait_ge(self.f_ready, t + 1)
        ge(dve, self.exp_ready, t)
        nc.vector.tensor_tensor(self.e1[:], self.scores_psum.rearrange("p (h j) -> p h j", h=self.heads),
                                self.f[:, self.heads:, None].to_broadcast(shape), ALU.add
                                ).then_inc(self.summed, 1)
        dve.wait_ge(self.summed, t + 1)
        nc.vector.scalar_tensor_tensor(self.e2[:], self.e1[:], self.slope, self.e1[:], ALU.mult, ALU.max
                                       ).then_inc(self.leaky, 1)
        dve.wait_ge(self.leaky, t + 1)
        nc.vector.memset(self.pause[:], 0.0)
        nc.vector.copy_predicated(self.e2[:], self.mask[:, None, :].to_broadcast(shape),
                                  fill[:, 0:1, None].to_broadcast(shape)).then_inc(self.masked, 1)
        dve.wait_ge(self.masked, t + 1)
        if self.heads == 1:
            nc.vector.tensor_reduce(self.peak[:], self.e2[:], AX_X, ALU.max, negate=True
                                    ).then_inc(self.peaked, 1)
            return
        nc.vector.reduce_max(self.peak[:], self.e2[:], AX_X).then_inc(self.peaked, 1)
        dve.wait_ge(self.peaked, t + 1)
        nc.vector.tensor_tensor(self.e1[:], self.e2[:], self.peak[:, :, None].to_broadcast(shape),
                                ALU.subtract).then_inc(self.shifted, 1)

    def act_exp(self, nc, act, t):
        ge(act, self.prob_ready, t)
        if self.heads == 1:
            act.wait_ge(self.peaked, t + 1)
            ge(act, self.inverted, t)
            nc.scalar.activation(self.ex[:, 0, :], self.e2[:, 0, :], ACT.Exp, bias=self.peak[:],
                                 accum_out=self.total[:]).then_inc(self.exp_ready, 1)
        else:
            act.wait_ge(self.shifted, t + 1)
            ge(act, self.totalled, t)
            nc.scalar.activation(self.ex[:], self.e1[:], ACT.Exp).then_inc(self.exp_ready, 1)

    def dve_after_exp(self, nc, dve, t, gate=None):
        dve.wait_ge(self.exp_ready, t + 1)
        if self.heads > 1:
            nc.vector.reduce_sum(self.total[:], self.ex[:], AX_X).then_inc(self.totalled, 1)
            dve.wait_ge(self.totalled, t + 1)
        ge(dve, self.prob_ready, t)
        nc.vector.reciprocal(self.inv[:], self.total[:]).then_inc(self.inverted, 1)
        if gate is not None:
            dve.wait_ge(self.inverted, t + 1)
            nc.vector.tensor_tensor(self.inv[:], self.inv[:], gate[:], ALU.mult).then_inc(self.gated, 1)

    def pool_prob(self, nc, pool, t, gate=None):
        if gate is not None:
            pool.wait_ge(self.gated, t + 1)
        else:
            pool.wait_ge(self.inverted, t + 1)
        pool.wait_ge(self.exp_ready, t + 1)
        ge(pool, self.turned_done, t)
        for g in range(2):
            ins = nc.gpsimd.tensor_tensor(self.prob[:, :, g, :], self.ex[:],
                                          self.inv[:, :, None].to_broadcast([P, self.heads, NODES]), ALU.mult)
        ins.then_inc(self.prob_ready, 1)

    def pe_turn(self, nc, pe, t, ident):
        pe.wait_ge(self.prob_ready, t + 1)
        ge(pe, self.turned_ready, 2 * t)
        for h in range(self.heads):
            ins = nc.tensor.transpose(self.turned_psum[:, h, :],
                                      self.prob[:, h, :, :].rearrange("p g j -> p (g j)"), ident[:])
        ins.then_inc(self.turned_done, 1)

    def act_turned(self, nc, act, t):
        act.wait_ge(self.turned_done, t + 1)
        if isinstance(t, int) and t == 0:
            act.wait_ge(self.zeroed, 1)
        for g in range(2):
            r = slice(g * NODES, (g + 1) * NODES)
            nc.scalar.copy(self.turned[r, :, r], self.turned_psum[r, :, r]).then_inc(self.turned_ready, 1)


class Norm:

    def __init__(self, nc, ctx, name, shifted=False):
        def sb(n, shape):
            return ctx.enter_context(nc.sbuf_tensor(f"{name}_{n}", shape, F32))

        def sem(n):
            return ctx.enter_context(nc.semaphore(f"{name}_{n}"))

        self.shifted = shifted
        self.pause = sb("pause", [P, 1])
        self.stats, self.mv = sb("stats", [P, 6]), sb("mv", [P, 2])
        self.veps, self.rstd, self.shift = sb("veps", [P, 1]), sb("rstd", [P, 1]), sb("shift", [P, 1])
        self.stats_ready, self.mv_ready, self.veps_ready, self.rstd_ready = (
            sem("stats_ready"), sem("mv_ready"), sem("veps_ready"), sem("rstd_ready"))
        self.shift_ready = self.rstd_ready
        if shifted:
            self.less = sb("less", [P, 1])
            self.less_ready, self.shift_ready = sem("less_ready"), sem("shift_ready")

    def dve_stats(self, nc, dve, t, x):
        nc.vector.bn_stats(self.stats[:], x).then_inc(self.stats_ready, 1)

    def dve_mean(self, nc, dve, t, used):
        dve.wait_ge(self.stats_ready, t + 1)
        ge(dve, used, t)
        ge(dve, self.shift_ready, t)
        nc.vector.memset(self.pause[:], 0.0)
        nc.vector.bn_aggr(self.mv[:], self.stats[:]).then_inc(self.mv_ready, 1)

    def pool_rstd(self, nc, pool, t, used, consts):
        pool.wait_ge(self.mv_ready, t + 1)
        nc.gpsimd.tensor_tensor(self.veps[:], self.mv[:, 1:2], consts[:, 0:1], ALU.add
                                ).then_inc(self.veps_ready, 1)
        if self.shifted:
            nc.gpsimd.tensor_tensor(self.less[:], self.mv[:, 0:1], consts[:, 2:3], ALU.mult
                                    ).then_inc(self.less_ready, 1)
        pool.wait_ge(self.veps_ready, t + 1)
        ge(pool, used, t)
        nc.gpsimd.tensor_tensor(self.rstd[:], self.veps[:], consts[:, 1:2], ALU.pow
                                ).then_inc(self.rstd_ready, 1)
        if self.shifted:
            pool.wait_ge(self.rstd_ready, t + 1)
            pool.wait_ge(self.less_ready, t + 1)
            nc.gpsimd.tensor_tensor(self.shift[:], self.less[:], self.rstd[:], ALU.mult
                                    ).then_inc(self.shift_ready, 1)


def gnn_stack_kernel(nc, x, adj, W0T, b0, Wh, ah, Wo, ao, w1, b1, w2, b2, gamma, beta,
                     W2, a2s, a2d, W3, a3s, a3d, out):
    B, N, _ = x.shape
    T = B * N // P
    x_rows = x.rearrange("b n d -> (b n) d")
    out_rows = out.rearrange("b n d -> (b n) d")
    x1_rows = nc.dram_tensor("x1_scratch", (B * N, D), F32).ap()
    att_rows = nc.dram_tensor("att_scratch", (T * P, D), F32).ap()

    def rows(dram, t):
        return dram[bass.ts(t, P), :]

    def chunked(w):
        return w.rearrange("(c p) n -> p c n", p=P)

    with ExitStack() as top:
        def sb(n, shape, dt=F32):
            return top.enter_context(nc.sbuf_tensor(n, shape, dt))

        def sem(n):
            return top.enter_context(nc.semaphore(n))

        NQ = 2 * HEADS * KC
        held = top.enter_context(ExitStack())
        ident = sb("ident", [P, P])
        same_graph = sb("same_graph", [P, P])
        i64 = sb("i64", [P, NODES])
        norm_consts = sb("norm_consts", [P, 3])
        fill1 = sb("fill1", [P, 1])
        mask1 = sb("mask1", [P, NODES], I32)
        bias23 = sb("bias23", [P, NODES])
        gate = sb("gate", [P, 1])
        big_hi = held.enter_context(nc.sbuf_tensor("big_hi", [P, NQ, D], F32R))
        big_lo = held.enter_context(nc.sbuf_tensor("big_lo", [P, NQ, D], F32R))
        att_stored = sem("att_stored")
        stage_loaded = sem("stage_loaded")

        with ExitStack() as ctx:
            def sb(n, shape, dt=F32):
                return ctx.enter_context(nc.sbuf_tensor(n, shape, dt))

            def sem(n):
                return ctx.enter_context(nc.semaphore(n))

            XR, UN = 4, 4
            w0 = (sb("w0_hi", [P, 2 * KC, D], F32R), sb("w0_lo", [P, 2 * KC, D], F32R))
            w0f = sb("w0f", [P, KC, D])
            stage = sb("stage", [P, D])
            xt = [sb(f"xt{r}", [P, D]) for r in range(XR)]
            mix = [(sb(f"mix_hi{b}", [P, KC, 2 * P], F32R), sb(f"mix_lo{b}", [P, KC, 2 * P], F32R))
                   for b in range(2)]
            z = sb("z", [P, D])
            x1 = [sb(f"x1_{b}", [P, D]) for b in range(2)]
            adj_i = sb("adj_i", [P, NODES], I32)
            adj_f = sb("adj_f", [P, NODES])
            zero_f = sb("zero_f", [P, NODES])
            none = sb("none", [P, 1])
            deg = sb("deg", [P, 1])
            adj_bd = sb("adj_bd", [P, P])
            spread = sb("spread", [P, 2 * P])
            db = sb("db", [P, D])
            mixed = [[ctx.enter_context(nc.psum_tensor(f"mixed{b}{k}", [P, 2, 2 * P], F32)) for k in range(2)]
                     for b in range(2)]
            main = [ctx.enter_context(nc.psum_tensor(f"main{b}", [P, D], F32)) for b in range(2)]
            setup_psum = ctx.enter_context(nc.psum_tensor("setup_psum", [P, P], F32))
            first_sem = sem("first_of_layer0")
            norm = Norm(nc, ctx, "n0")
            loaded = [sem(f"loaded{r}") for r in range(XR)]
            small_loaded, w0_loaded, w0_hi_ready, w0_lo_ready = (
                sem("small_loaded"), sem("w0_loaded"), sem("w0_hi_ready"), sem("w0_lo_ready"))
            zeros_set, consts_set, adj_ready, setup_step, bd_ready, bd_turned, spread_ready = (
                sem("zeros_set"), sem("consts_set"), sem("adj_ready"), sem("setup_step"), sem("bd_ready"),
                sem("bd_turned"), sem("spread_ready"))
            mixed_done, mix_hi_ready, mix_lo_ready, main_done = (
                sem("mixed_done"), sem("mix_hi_ready"), sem("mix_lo_ready"), sem("main_done"))
            xb_ready, z_ready, x1_ready = sem("xb_ready"), sem("z_ready"), sem("x1_ready")
            big_hi_ready, big_lo_ready = sem("big_hi_ready"), sem("big_lo_ready")
            x1_out = [sem(f"x1_out{b}") for b in range(2)]
            layer0_sems = range(first_sem.num, x1_out[1].num + 1)
            block = ctx.enter_context(nc.Block())
            Wh_rows = Wh.rearrange("h k o -> (h k) o")

            @block.sync
            def _(sp):
                for g in range(2):
                    sp.dma_start(adj_i[g * NODES:(g + 1) * NODES, :], adj).then_inc(small_loaded, 16)
                sp.dma_start(db[:], b0.partition_broadcast(P)).then_inc(small_loaded, 16)
                for r in range(XR):
                    sp.dma_start(xt[r][:], rows(x_rows, r)).then_inc(loaded[r], 16)

                for k in range(2):
                    ge(sp, w0_lo_ready, k)
                    sp.dma_start(w0f[:], chunked(W0T[k * D:(k + 1) * D, :])).then_inc(w0_loaded, 16)

                def step(t, r, more):
                    sp.wait_ge(x1_ready, t + 1)
                    sp.dma_start(rows(x1_rows, t), x1[r % 2][:]).then_inc(x1_out[r % 2], 16)
                    if more:
                        sp.dma_start(xt[r][:], rows(x_rows, t + XR)).then_inc(loaded[r], 16)

                with sp.Fori(0, T // UN - 1) as g:
                    t = g * UN
                    for r in range(UN):
                        step(t + r, r, True)
                for r in range(XR):
                    step(T - XR + r, r, False)
                for b in range(2):
                    sp.wait_ge(x1_out[b], 16 * T // 2)

            @block.gpsimd
            def _(pool):
                nc.gpsimd.memset(ident[:], 0.0).then_inc(zeros_set, 1)
                nc.gpsimd.memset(i64[:], 0.0).then_inc(zeros_set, 1)
                nc.gpsimd.memset(adj_bd[:], 0.0).then_inc(zeros_set, 1)
                nc.gpsimd.memset(same_graph[:], 0.0).then_inc(zeros_set, 1)
                for k, value in enumerate((LN_EPS, -0.5, -1.0)):
                    nc.gpsimd.memset(norm_consts[:, k:k + 1], value).then_inc(consts_set, 1)
                nc.gpsimd.memset(fill1[:], MASKED_L1).then_inc(consts_set, 1)
                pool.wait_ge(zeros_set, 4)
                for g in range(2):
                    r = slice(g * NODES, (g + 1) * NODES)
                    pool.wait_ge(zeros_set, 4 + g)
                    nc.gpsimd.memset(same_graph[r, r], 1.0).then_inc(consts_set, 1)
                    pool.wait_ge(consts_set, 5 + g)
                    nc.gpsimd.affine_select(out=i64[:], in_=i64[:], compare_op=ALU.not_equal, fill=1.0,
                                            base=-g * NODES, pattern=[[-1, NODES]], channel_multiplier=1
                                            ).then_inc(zeros_set, 1)
                pool.wait_ge(zeros_set, 6)
                nc.gpsimd.affine_select(out=ident[:], in_=ident[:], compare_op=ALU.not_equal, fill=1.0,
                                        base=0, pattern=[[-1, P]], channel_multiplier=1).then_inc(consts_set, 1)
                pool.wait_ge(consts_set, 7)

                def split_block(q, source, k):
                    ge(pool, big_lo_ready, q)
                    pool.dma_start(stage[:], source[bass.ts(k, P), :]).then_inc(stage_loaded, 16)
                    return q

                def split_hi(q):
                    pool.wait_ge(stage_loaded, 16 * q + 16)
                    nc.gpsimd.tensor_copy(big_hi[:, bass.ds(q, 1), :], stage[:, None, :]
                                          ).then_inc(big_hi_ready, 1)

                def split_lo(q):
                    pool.wait_ge(big_hi_ready, q + 1)
                    nc.gpsimd.tensor_tensor(big_lo[:, bass.ds(q, 1), :], stage[:, None, :],
                                            big_hi[:, bass.ds(q, 1), :].bitcast(F32), ALU.subtract
                                            ).then_inc(big_lo_ready, 1)

                def half(source, first_q):
                    def two(q, k):
                        split_block(q, source, k)
                        norm.pool_rstd(nc, pool, 2 * q, x1_ready, norm_consts)
                        split_hi(q)
                        norm.pool_rstd(nc, pool, 2 * q + 1, x1_ready, norm_consts)
                        split_lo(q)
                    if first_q == 0:
                        two(0, 0)
                        with pool.Fori(1, NQ // 2) as k:
                            two(k, k)
                    else:
                        with pool.Fori(0, NQ // 2) as k:
                            two(k + first_q, k)

                half(Wh_rows, 0)
                half(Wo, NQ // 2)

            @block.scalar
            def _(act):
                for k in range(2):
                    s = slice(k * KC, (k + 1) * KC)
                    act.wait_ge(w0_loaded, 16 * (k + 1))
                    nc.scalar.copy(w0[0][:, s, :], w0f[:]).then_inc(w0_hi_ready, 1)

                def step(t, b):
                    for k in range(2):
                        act.wait_ge(mixed_done, 2 * t + k + 1)
                        ge(act, main_done, t - 1)
                        nc.scalar.copy(mix[b][0][:, 2 * k:2 * k + 2, :], mixed[b][k][:]
                                       ).then_inc(mix_hi_ready, 1)

                step(0, 0)
                step(1, 1)
                with act.Fori(1, T // 2) as g:
                    t = g * 2
                    step(t, 0)
                    step(t + 1, 1)

            @block.vector
            def _(dve):
                dve.wait_ge(small_loaded, 48)
                dve.wait_ge(zeros_set, 6)
                nc.vector.tensor_copy(adj_f[:], adj_i[:]).then_inc(adj_ready, 1)
                dve.wait_ge(adj_ready, 1)
                nc.vector.reduce_sum(deg[:], adj_f[:], AX_X).then_inc(setup_step, 1)
                nc.vector.tensor_scalar(mask1[:], adj_f[:], 0.0, None, ALU.is_le).then_inc(setup_step, 1)
                nc.vector.tensor_scalar(bias23[:], adj_f[:], 0.0, MASKED_L23, ALU.is_equal, ALU.mult).then_inc(setup_step, 1)
                nc.vector.tensor_scalar(zero_f[:], adj_f[:], 0.0, None, ALU.is_equal).then_inc(setup_step, 1)
                for g in range(2):
                    r = slice(g * NODES, (g + 1) * NODES)
                    nc.vector.tensor_copy(adj_bd[r, r], adj_f[r, :]).then_inc(bd_ready, 1)
                dve.wait_ge(setup_step, 4)
                nc.vector.tensor_reduce(none[:], zero_f[:], AX_X, ALU.min).then_inc(setup_step, 1)
                dve.wait_ge(consts_set, 7)
                nc.vector.tensor_scalar(spread[:, P:2 * P], ident[:], deg[:], None, ALU.mult
                                        ).then_inc(spread_ready, 1)
                nc.vector.tensor_scalar(db[:], db[:], deg[:], None, ALU.mult).then_inc(setup_step, 1)
                dve.wait_ge(setup_step, 6)
                nc.vector.tensor_scalar(gate[:], none[:], -1.0, 1.0, ALU.mult, ALU.add).then_inc(setup_step, 1)
                dve.wait_ge(bd_turned, 1)
                nc.vector.tensor_copy(spread[:, 0:P], setup_psum[:]).then_inc(spread_ready, 1)
                for k in range(2):
                    s = slice(k * KC, (k + 1) * KC)
                    dve.wait_ge(w0_hi_ready, k + 1)
                    nc.vector.tensor_tensor(w0[1][:, s, :], w0f[:], w0[0][:, s, :].bitcast(F32),
                                            ALU.subtract).then_inc(w0_lo_ready, 1)

                def mix_lo(t, b):
                    for k in range(2):
                        dve.wait_ge(mix_hi_ready, 2 * t + k + 1)
                        nc.vector.tensor_tensor(mix[b][1][:, 2 * k:2 * k + 2, :], mixed[b][k][:],
                                                mix[b][0][:, 2 * k:2 * k + 2, :].bitcast(F32),
                                                ALU.subtract).then_inc(mix_lo_ready, 1)

                def finish(t, r):
                    dve.wait_ge(loaded[r], 16 * (t // XR) + 16 if isinstance(t, int) else 4 * (t - r) + 16)
                    ge(dve, x1_ready, t)
                    nc.vector.tensor_tensor(z[:], xt[r][:], db[:], ALU.add).then_inc(xb_ready, 1)
                    dve.wait_ge(xb_ready, t + 1)
                    dve.wait_ge(main_done, t + 1)
                    nc.vector.tensor_tensor(z[:], main[r % 2][:], z[:], ALU.add).then_inc(z_ready, 1)
                    dve.wait_ge(z_ready, t + 1)
                    norm.dve_stats(nc, dve, t, z[:])
                    norm.dve_mean(nc, dve, t, x1_ready)
                    dve.wait_ge(norm.rstd_ready, t + 1)
                    ge(dve, x1_out[r % 2], 16 * (t // 2) if isinstance(t, int) else 8 * (t - r) + 16 * (r // 2))
                    nc.vector.tensor_scalar(x1[r % 2][:], z[:], norm.mv[:, 0:1], norm.rstd[:],
                                            ALU.subtract, ALU.mult).then_inc(x1_ready, 1)

                dve.wait_ge(setup_step, 7)
                mix_lo(0, 0)
                for r in range(UN):
                    mix_lo(r + 1, (r + 1) % 2)
                    finish(r, r)
                with dve.Fori(1, T // UN - 1) as g:
                    t = g * UN
                    for r in range(UN):
                        mix_lo(t + r + 1, (r + 1) % 2)
                        finish(t + r, r)
                for r in range(UN):
                    if r < UN - 1:
                        mix_lo(T - UN + r + 1, (r + 1) % 2)
                    finish(T - UN + r, r)

            @block.tensor
            def _(pe):
                pe.wait_ge(bd_ready, 2)
                pe.wait_ge(consts_set, 7)
                nc.tensor.transpose(setup_psum[:], adj_bd[:], ident[:]).then_inc(bd_turned, 1)
                pe.wait_ge(spread_ready, 2)

                def mixes(t, r):
                    pe.wait_ge(loaded[r % XR], 16 * (t // XR) + 16 if isinstance(t, int)
                               else 4 * (t - r % XR) + 16)
                    for c in range(KC):
                        if c % 2 == 0:
                            ge(pe, mix_lo_ready, 2 * t + c // 2 - 3)
                        ins = nc.tensor.matmul(mixed[r % 2][c // 2][:, c % 2, :],
                                               xt[r % XR][:, c * P:(c + 1) * P], spread[:],
                                               start=True, stop=True)
                        if c % 2:
                            ins.then_inc(mixed_done, 1)

                def products(t, r):
                    pe.wait_ge(mix_hi_ready, 2 * t + 2)
                    pe.wait_ge(mix_lo_ready, 2 * t + 2)
                    ge(pe, z_ready, t - 1)
                    hi, lo = mix[r % 2]
                    product(nc, main[r % 2][:], (hi[:, :, P:], lo[:, :, P:]), w0,
                            [(c, c) for c in range(KC)], last=False)
                    product(nc, main[r % 2][:], (hi[:, :, :P], lo[:, :, :P]), w0,
                            [(c, KC + c) for c in range(KC)], first=False).then_inc(main_done, 1)

                mixes(0, 0)
                pe.wait_ge(w0_hi_ready, 2)
                pe.wait_ge(w0_lo_ready, 2)
                for r in range(UN):
                    mixes(r + 1, r + 1)
                    products(r, r)
                with pe.Fori(1, T // UN - 1) as g:
                    t = g * UN
                    for r in range(UN):
                        if r < UN - 1:
                            mixes(t + (r + 1), r + 1)
                        else:
                            mixes(t + UN, 0)
                        products(t + r, r)
                for r in range(UN):
                    if r < UN - 1:
                        mixes(T - UN + r + 1, r + 1)
                    products(T - UN + r, r)

        with ExitStack() as ctx:
            def sb(n, shape, dt=F32):
                return ctx.enter_context(nc.sbuf_tensor(n, shape, dt))

            def sem(n):
                return ctx.enter_context(nc.semaphore(n))

            def pb(n, shape):
                return ctx.enter_context(nc.psum_tensor(n, shape, F32))

            xin = sb("xin", [P, D])
            xT = (sb("xT_hi", [P, KC, P], F32R), sb("xT_lo", [P, KC, P], F32R))
            wh = sb("wh", [P, HEADS, D])
            who = sb("who", [P, D])
            ex = [sb(f"ex{b}", [P, D]) for b in range(2)]
            hv = [sb(f"hv{b}", [P, D]) for b in range(2)]
            hT = [(sb(f"hT_hi{b}", [P, KC, P], F32R), sb(f"hT_lo{b}", [P, KC, P], F32R)) for b in range(2)]
            attT = sb("attT", [P, D])
            junk = sb("junk", [P, D])
            ao_row = sb("ao_row", [P, 2, D])
            v_hl = sb("v_hl", [P, KC, 4 * HEADS], F32R)
            v_f = sb("v_f", [P, KC, 2 * HEADS])
            ws = hv[0]
            whp = [pb(f"whp{b}", [P, D]) for b in range(2)]
            wop = pb("wop", [P, D])
            turn = pb("turn", [P, HEADS, P])
            smallp = pb("smallp", [P, D])
            up = [pb(f"up{b}", [P, D]) for b in range(3)]
            U_HEAD, U_OUT = [0, 1, 2, 0], 1
            SF, SO, SH, ST = 0, NODES, P, 3 * P
            first_sem = sem("first_of_layer1")
            at = Attention(nc, ctx, "ah", HEADS, SLOPE_L1, smallp[:, SH:SH + HEADS * NODES], turn[:],
                           mask=mask1)
            ao_ = Attention(nc, ctx, "ao", 1, SLOPE_L1, smallp[:, SO:SO + NODES],
                            smallp[:, ST:ST + P].rearrange("p (h n) -> p h n", h=1), mask=mask1)
            ws_loaded = [sem(f"ws_loaded{b}") for b in range(2)]
            a_loaded, v_part, v_hi_ready, v_lo_ready = (
                sem("a_loaded"), sem("v_part"), sem("v_hi_ready"), sem("v_lo_ready"))
            xin_loaded, xT_done, xT_hi_ready, xT_lo_ready, f_done = (
                sem("xin_loaded"), sem("xT_done"), sem("xT_hi_ready"), sem("xT_lo_ready"), sem("f_done"))
            wh_done, wh_ready, u_done, ex_ready, neg_ready, hv_ready, hT_hi_ready, hT_lo_ready = (
                sem("wh_done"), sem("wh_ready"), sem("u_done"), sem("ex_ready"), sem("neg_ready"),
                sem("hv_ready"), sem("hT_hi_ready"), sem("hT_lo_ready"))
            wo_done, who_ready, fo_part, uo_done, exo_ready, nego_ready, att_ready = (
                sem("wo_done"), sem("who_ready"), sem("fo_part"), sem("uo_done"), sem("exo_ready"),
                sem("nego_ready"), sem("att_ready"))
            layer1_sems = range(first_sem.num, att_ready.num + 1)
            a_rows = ctx.enter_context(nc.sbuf_tensor("a_rows", [P, 2 * HEADS, D], F32))
            block = ctx.enter_context(nc.Block())

            def run(eng, step):
                step(0, True, False, False)
                step(1, True, True, False)
                step(2, True, True, True)
                with eng.Fori(3, T - 1) as n:
                    step(n, True, True, True)
                step(T - 1, True, True, True)
                step(T, False, True, True)
                step(T + 1, False, False, True)

            @block.sync
            def _(sp):
                sp.dma_start(a_rows[:], ah.rearrange("h (s o) -> (h s o)", s=2).partition_broadcast(P)
                             .rearrange("p (k o) -> p k o", o=D)).then_inc(a_loaded, 16)
                sp.dma_start(ao_row[:], ao.partition_broadcast(P).rearrange("p (k o) -> p k o", o=D)
                             ).then_inc(a_loaded, 16)
                sp.dma_start(xin[:], rows(x1_rows, 0)).then_inc(xin_loaded, 16)
                Wr = Wh.rearrange("h k o -> (h k) o")
                for q in range(HEADS * KC):
                    ge(sp, v_part, 2 * (q - 1))
                    sp.dma_start(hv[q % 2][:], rows(Wr, q)).then_inc(ws_loaded[q % 2], 16)

                def store(t):
                    sp.wait_ge(att_ready, t + 1)
                    sp.dma_start(rows(att_rows, t), attT[:]).then_inc(att_stored, 16)

                def load(n):
                    sp.wait_ge(xT_done, n)
                    sp.dma_start(xin[:], rows(x1_rows, n)).then_inc(xin_loaded, 16)

                load(1)
                load(2)
                with sp.Fori(2, T - 1) as n:
                    load(n + 1)
                    store(n - 2)
                for t in range(T - 3, T):
                    store(t)
                sp.wait_ge(att_stored, 16 * T)

            @block.gpsimd
            def _(pool):
                nc.gpsimd.sem_clear(layer0_sems)
                at.pool_zero(nc)
                ao_.pool_zero(nc)

                def step(n, heads, sums, outs):
                    if heads:
                        at.pool_diag(nc, pool, n, i64)
                    if outs:
                        ao_.pool_diag(nc, pool, n - 2, i64)
                    if heads:
                        at.pool_prob(nc, pool, n)
                    if outs:
                        ao_.pool_prob(nc, pool, n - 2)
                run(pool, step)

            @block.scalar
            def _(act):
                def x_hi(t):
                    act.wait_ge(xT_done, t + 1)
                    ge(act, wh_done, 4 * t)
                    nc.scalar.copy(xT[0][:], turn[:]).then_inc(xT_hi_ready, 1)

                def head(n, h, heads, sums):
                    if sums:
                        k = 4 * (n - 1) + h
                        act.wait_ge(u_done, k + 1)
                        ge(act, hv_ready, k - 1)
                        nc.scalar.activation(ex[h % 2][:], up[U_HEAD[h]][:], ACT.Exp).then_inc(ex_ready, 1)
                    if heads:
                        act.wait_ge(wh_done, 4 * n + h + 1)
                        ge(act, u_done, 4 * (n - 1) + h + 1)
                        nc.scalar.copy(wh[:, h, :], whp[h % 2][:]).then_inc(wh_ready, 1)
                    if sums:
                        act.wait_ge(hv_ready, k + 1)
                        ge(act, wo_done, k - 1)
                        nc.scalar.copy(hT[h % 2][0][:].rearrange("p c n -> p (c n)"), hv[h % 2][:]
                                       ).then_inc(hT_hi_ready, 1)

                def step(n, heads, sums, outs):
                    head(n, 0, heads, sums)
                    if outs:
                        act.wait_ge(wo_done, 4 * (n - 1))
                        ge(act, uo_done, n - 2)
                        ge(act, ao_.f_ready, n - 2)
                        nc.scalar.copy(who[:], wop[:]).then_inc(who_ready, 1)
                    head(n, 1, heads, sums)
                    if heads:
                        at.act_exp(nc, act, n)
                    head(n, 2, heads, sums)
                    if outs:
                        ao_.act_exp(nc, act, n - 2)
                    head(n, 3, heads, sums)
                    if outs:
                        ge(act, uo_done, n - 2)
                        ao_.act_turned(nc, act, n - 2)
                    if heads and not (isinstance(n, int) and n == T - 1):
                        x_hi(n + 1)
                    if heads:
                        ge(act, u_done, 4 * n)
                        at.act_turned(nc, act, n)
                    if outs:
                        act.wait_ge(uo_done, n - 1)
                        ge(act, att_ready, n - 2)
                        act.wait_ge(ao_.f_ready, n - 1)
                        nc.scalar.activation(junk[:], up[U_OUT][:], ACT.Exp).then_inc(exo_ready, 1)

                x_hi(0)
                run(act, step)

            @block.vector
            def _(dve):
                dve.wait_ge(a_loaded, 32)
                for q in range(HEADS * KC):
                    h, c = q // KC, q % KC
                    dve.wait_ge(ws_loaded[q % 2], 16 * (q // 2 + 1))
                    for s in range(2):
                        col = h if s == 1 else HEADS + h
                        ge(dve, v_part, 2 * q + s)
                        nc.vector.tensor_tensor_reduce(out=junk[:], in0=hv[q % 2][:], in1=a_rows[:, 2 * h + s, :],
                                                       scale=1.0, scalar=0.0, op0=ALU.mult, op1=ALU.add,
                                                       accum_out=v_f[:, c, col:col + 1]).then_inc(v_part, 1)
                dve.wait_ge(v_part, 2 * HEADS * KC)
                nc.vector.tensor_copy(v_hl[:, :, 0:2 * HEADS], v_f[:]).then_inc(v_hi_ready, 1)
                dve.wait_ge(v_hi_ready, 1)
                nc.vector.tensor_tensor(v_hl[:, :, 2 * HEADS:], v_f[:], v_hl[:, :, 0:2 * HEADS].bitcast(F32),
                                        ALU.subtract).then_inc(v_lo_ready, 1)

                def x_lo(t):
                    dve.wait_ge(xT_hi_ready, t + 1)
                    nc.vector.tensor_tensor(xT[1][:], turn[:], xT[0][:].bitcast(F32), ALU.subtract
                                            ).then_inc(xT_lo_ready, 1)

                def negative(k, h):
                    dve.wait_ge(ex_ready, k + 1)
                    nc.vector.tensor_scalar(ex[h % 2][:], ex[h % 2][:], 1.0, -1.0, ALU.min, ALU.add
                                            ).then_inc(neg_ready, 1)
                    dve.wait_ge(neg_ready, k + 1)
                    ge(dve, hT_lo_ready, k - 1)
                    nc.vector.tensor_tensor(hv[h % 2][:], up[U_HEAD[h]][:], ex[h % 2][:], ALU.max
                                            ).then_inc(hv_ready, 1)

                def low(k, h):
                    dve.wait_ge(hT_hi_ready, k + 1)
                    nc.vector.tensor_tensor(hT[h % 2][1][:].rearrange("p c n -> p (c n)"), hv[h % 2][:],
                                            hT[h % 2][0][:].bitcast(F32).rearrange("p c n -> p (c n)"),
                                            ALU.subtract).then_inc(hT_lo_ready, 1)

                def step(n, heads, sums, outs):
                    k = 4 * (n - 1)
                    if heads:
                        dve.wait_ge(f_done, n + 1)
                        ge(dve, at.diag_ready, n)
                        ge(dve, at.summed, n)
                        nc.vector.reduce_sum(at.f[:], smallp[:, SF:SF + 4 * HEADS]
                                             .rearrange("p (s k) -> p k s", s=2), AX_X).then_inc(at.f_ready, 1)
                    if sums:
                        negative(k, 0)
                        low(k, 0)
                    if outs:
                        dve.wait_ge(who_ready, n - 1)
                        ge(dve, ao_.diag_ready, n - 2)
                        ge(dve, ao_.summed, n - 2)
                        ge(dve, att_ready, n - 2)
                        nc.vector.tensor_tensor_reduce(
                            out=junk[:], in0=who[:], in1=ao_row[:, 0, :], scale=1.0, scalar=0.0,
                            op0=ALU.mult, op1=ALU.add, accum_out=ao_.f[:, 1:2]).then_inc(fo_part, 1)
                        dve.wait_ge(fo_part, n - 1)
                        nc.vector.tensor_tensor_reduce(
                            out=junk[:], in0=who[:], in1=ao_row[:, 1, :], scale=1.0, scalar=0.0,
                            op0=ALU.mult, op1=ALU.add, accum_out=ao_.f[:, 0:1]).then_inc(ao_.f_ready, 1)
                    if heads:
                        at.dve_before_exp(nc, dve, n, fill1)
                    if sums:
                        negative(k + 1, 1)
                        low(k + 1, 1)
                    if outs:
                        ao_.dve_before_exp(nc, dve, n - 2, fill1)
                    if heads:
                        at.dve_after_exp(nc, dve, n)
                    if sums:
                        negative(k + 2, 2)
                    if outs:
                        ao_.dve_after_exp(nc, dve, n - 2)
                    if sums:
                        low(k + 2, 2)
                        negative(k + 3, 3)
                        low(k + 3, 3)
                    if heads and not (isinstance(n, int) and n == T - 1):
                        x_lo(n + 1)
                    if outs:
                        dve.wait_ge(exo_ready, n - 1)
                        nc.vector.tensor_scalar(junk[:], junk[:], 1.0, -1.0, ALU.min, ALU.add
                                                ).then_inc(nego_ready, 1)
                        dve.wait_ge(nego_ready, n - 1)
                        ge(dve, att_stored, 16 * (n - 2))
                        nc.vector.tensor_tensor(attT[:], up[U_OUT][:], junk[:], ALU.max
                                                ).then_inc(att_ready, 1)

                x_lo(0)
                run(dve, step)

            @block.tensor
            def _(pe):
                def turn_x(t):
                    pe.wait_ge(xin_loaded, 16 * t + 16)
                    ge(pe, at.turned_ready, 2 * (t - 1))
                    for c in range(KC):
                        ins = nc.tensor.transpose(turn[:, c, :], xin[:, c * P:(c + 1) * P], ident[:])
                    ins.then_inc(xT_done, 1)

                def sums_of(m, h):
                    k = 4 * m + h
                    pe.wait_ge(wh_ready, k + 1)
                    if h == 1:
                        ge(pe, att_ready, m - 1)
                    else:
                        ge(pe, hv_ready, {0: k, 2: k - 3, 3: k - 2}[h])
                    for c in range(KC):
                        ins = nc.tensor.matmul(up[U_HEAD[h]][:, c * P:(c + 1) * P],
                                               wh[:, h, c * P:(c + 1) * P], at.turned[:, h, :],
                                               start=True, stop=True)
                    ins.then_inc(u_done, 1)

                def project(n, h):
                    ge(pe, wh_ready, 4 * n + h - 1)
                    product(nc, whp[h % 2][:], xT, (big_hi, big_lo),
                            [(c, h * KC + c) for c in range(KC)]).then_inc(wh_done, 1)

                def out_part(k, h):
                    pe.wait_ge(hT_lo_ready, k + 1)
                    pe.wait_ge(hT_hi_ready, k + 1)
                    product(nc, wop[:], hT[h % 2], (big_hi, big_lo),
                            [(c, (HEADS + h) * KC + c) for c in range(KC)],
                            first=h == 0, last=h == HEADS - 1).then_inc(wo_done, 1)

                def step(n, heads, sums, outs):
                    k = 4 * (n - 1)
                    if heads:
                        pe.wait_ge(xT_hi_ready, n + 1)
                        pe.wait_ge(xT_lo_ready, n + 1)
                        ge(pe, at.summed, n)
                        ge(pe, ao_.turned_ready, 2 * (n - 2))
                        for c in range(KC):
                            nc.tensor.matmul(smallp[:, SF:SF + 4 * HEADS], xT[0][:, c, :], v_hl[:, c, :],
                                             start=c == 0, stop=False)
                            ins = nc.tensor.matmul(smallp[:, SF:SF + 2 * HEADS], xT[1][:, c, :],
                                                   v_hl[:, c, 0:2 * HEADS], start=False, stop=c == KC - 1)
                        ins.then_inc(f_done, 1)
                    for h in range(HEADS):
                        if sums:
                            if h == 0:
                                pe.wait_ge(at.turned_ready, 2 * n)
                            sums_of(n - 1, h)
                        if heads:
                            project(n, h)
                        if heads and h == 3 and not (isinstance(n, int) and n == T - 1):
                            turn_x(n + 1)
                        if h == 0:
                            if outs:
                                out_part(k - 1, 3)
                            if heads:
                                at.pe_scores(nc, pe, n, same_graph)
                        else:
                            if sums:
                                if h == 1:
                                    ge(pe, who_ready, n - 1)
                                out_part(k + h - 1, h - 1)
                            if outs and h == 1:
                                ge(pe, at.summed, n + 1 if heads else T)
                                ao_.pe_scores(nc, pe, n - 2, same_graph)
                            if outs and h == 2:
                                pe.wait_ge(ao_.summed, n - 1)
                                ao_.pe_turn(nc, pe, n - 2, ident)
                    if outs:
                        pe.wait_ge(ao_.turned_ready, 2 * (n - 1))
                        if sums:
                            pe.wait_ge(hv_ready, k + 2)
                        for c in range(KC):
                            ins = nc.tensor.matmul(up[U_OUT][:, c * P:(c + 1) * P], who[:, c * P:(c + 1) * P],
                                                   ao_.turned[:, 0, :], start=True, stop=True)
                        ins.then_inc(uo_done, 1)
                    if heads:
                        if not (isinstance(n, int) and n == T - 1):
                            pe.wait_ge(xT_lo_ready, n + 2)
                        at.pe_turn(nc, pe, n, ident)

                turn_x(0)
                pe.wait_ge(v_hi_ready, 1)
                pe.wait_ge(v_lo_ready, 1)
                run(pe, step)

        with nc.Block() as block:
            @block.gpsimd
            def _(pool):
                nc.gpsimd.sem_clear(layer1_sems)

        held.close()
        with ExitStack() as ctx:
            def sb(n, shape, dt=F32):
                return ctx.enter_context(nc.sbuf_tensor(n, shape, dt))

            def sem(n):
                return ctx.enter_context(nc.semaphore(n))

            def pb(n, shape):
                return ctx.enter_context(nc.psum_tensor(n, shape, F32))

            R = 4
            w_hi = sb("w_hi", [P, 4 * KC, D], F32R)
            w_lo = sb("w_lo", [P, 4 * KC, D], F32R)
            stage = [sb(f"stage{b}", [P, KC, D]) for b in range(2)]
            att = [sb(f"att{b}", [P, D]) for b in range(2)]
            attS = [(sb(f"att_hi{b}", [P, KC, P], F32R), sb(f"att_lo{b}", [P, KC, P], F32R)) for b in range(2)]
            h1 = sb("h1", [P, D])
            h1T = (sb("h1T_hi", [P, KC, P], F32R), sb("h1T_lo", [P, KC, P], F32R))
            x1 = [sb(f"x1r{b}", [P, D]) for b in range(2)]
            x1b = sb("x1b", [P, D])
            ones = sb("ones", [P, P])
            att_b2 = sb("att_b2", [P, D])
            y = sb("y", [P, D])
            z1 = sb("z1", [P, D])
            x2 = [sb(f"x2_{r}", [P, D]) for r in range(R)]
            x3 = [sb(f"x3_{b}", [P, D]) for b in range(2)]
            res = sb("res", [P, D])
            b1_row, b2_row, gamma_row, beta_row = (sb("b1_row", [P, D]), sb("b2_row", [P, D]),
                                                   sb("gamma_row", [P, D]), sb("beta_row", [P, D]))
            a_row = sb("a_row", [P, 4, D])
            v_f = sb("v2_f", [P, KC, 4])
            diag_v = [sb(f"diag_v{k}", [P, KC, P]) for k in range(2)]
            scrap = sb("scrap", [P, D])
            bank_a, bank_b = pb("bank_a", [P, D]), pb("bank_b", [P, D])
            turn_h, turn_2, turn_3 = (pb("turn_h", [P, KC, P]), pb("turn_2", [P, KC, P]),
                                      pb("turn_3", [P, KC, P]))
            smallp = pb("smallq", [P, D])
            n_y, n_1 = Norm(nc, ctx, "ny"), Norm(nc, ctx, "n1", shifted=True)

            class Gat:

                def __init__(self, name, q, base, tp):
                    self.q, self.turn = q, tp
                    self.att = Attention(nc, ctx, name, 1, SLOPE_L23, smallp[:, base:base + NODES],
                                         smallp[:, base + NODES:base + NODES + P]
                                         .rearrange("p (h n) -> p h n", h=1))
                    self.v_row = sb(name + "_v_row", [P, 2, D])
                    self.terms = sb(name + "_terms", [P, 2, D])
                    self.xT = (sb(name + "_xT_hi", [P, KC, P], F32R), sb(name + "_xT_lo", [P, KC, P], F32R))
                    self.wh = sb(name + "_wh", [P, D])
                    self.z = sb(name + "_z", [P, D])
                    self.sums = pb(name + "_sums", [P, D])
                    self.norm = Norm(nc, ctx, name + "_n", shifted=True)
                    self.xT_done, self.xT_hi_ready, self.xT_lo_ready = (
                        sem(name + "_xT_done"), sem(name + "_xT_hi_ready"), sem(name + "_xT_lo_ready"))
                    self.wh_done, self.wh_ready, self.sums_done, self.z_ready, self.x_ready = (
                        sem(name + "_wh_done"), sem(name + "_wh_ready"), sem(name + "_sums_done"),
                        sem(name + "_z_ready"), sem(name + "_x_ready"))
                    self.diag_v_ready, self.v_spread, self.v_ready, self.terms_ready = (
                        sem(name + "_diag_v_ready"), sem(name + "_v_spread"), sem(name + "_v_ready"),
                        sem(name + "_terms_ready"))

            g2 = Gat("g2", 2 * KC, 0, turn_2)
            g3 = Gat("g3", 3 * KC, 2 * P, turn_3)
            weights = (w1, w2, W2, W3)
            w_loaded = [sem(f"w_loaded{b}") for b in range(2)]
            w_hi_ready, w_lo_ready, v_part, rows_loaded = (
                sem("w_hi_ready"), sem("w_lo_ready"), sem("v2_part"), sem("rows_loaded"))
            att_loaded = [sem(f"att_loaded{b}") for b in range(2)]
            x1_loaded = [sem(f"x1_loaded{b}") for b in range(2)]
            att_hi_ready, att_lo_ready, h1_done, h1_ready, h1T_done, h1T_hi_ready, h1T_lo_ready = (
                sem("att_hi_ready"), sem("att_lo_ready"), sem("h1_done"), sem("h1_ready"), sem("h1T_done"),
                sem("h1T_hi_ready"), sem("h1T_lo_ready"))
            y_done, scaled, x1b_ready, z1_ready, x2_ready = (
                sem("y_done"), sem("scaled"), sem("x1b_ready"), sem("z1_ready"), sem("x2_ready"))
            att_turned, att_b2_ready, y_ready, ones_ready = (
                sem("att_turned"), sem("att_b2_ready"), sem("y_ready"), sem("ones_ready"))
            res_stored = sem("res_stored")
            block = ctx.enter_context(nc.Block())

            def run(eng, step, ahead=0):
                stop = T // R - (1 if ahead else 0)
                for n in range(2 * R):
                    step(n, n % R)
                with eng.Fori(2, stop) as g:
                    n = g * R
                    for r in range(R):
                        step(n + r, r)
                for n in range(stop * R, T + 4):
                    step(n, n % R)

            def live(n, lag):
                return not isinstance(n, int) or 0 <= n - lag < T

            def pair(t, r):
                return 16 * (t // 2 + 1) if isinstance(t, int) else 8 * (t - r % 2) + 16

            @block.sync
            def _(sp):
                for k, w in enumerate(weights):
                    ge(sp, w_lo_ready, k - 1)
                    sp.dma_start(stage[k % 2][:], chunked(w)).then_inc(w_loaded[k % 2], 16)
                    if k < 2:
                        sp.dma_start(att[k][:], rows(att_rows, k)).then_inc(att_loaded[k], 16)
                        sp.dma_start(x1[k][:], rows(x1_rows, k)).then_inc(x1_loaded[k], 16)
                    if k == 0:
                        for row, src in ((b1_row, b1), (b2_row, b2), (gamma_row, gamma), (beta_row, beta)):
                            sp.dma_start(row[:], src.partition_broadcast(P)).then_inc(rows_loaded, 16)
                        for j, src in enumerate((a2d, a2s, a3d, a3s)):
                            sp.dma_start(a_row[:, j, :], src.partition_broadcast(P)).then_inc(rows_loaded, 16)

                def step(n, r):
                    if live(n, 4):
                        sp.wait_ge(g3.x_ready, n - 3)
                        sp.dma_start(rows(out_rows, n - 4), res[:]).then_inc(res_stored, 16)
                    if live(n, 0) and live(n, -2):
                        sp.wait_ge(att_lo_ready, n + 1)
                        sp.wait_ge(att_turned, n + 1)
                        sp.dma_start(att[r % 2][:], rows(att_rows, n + 2)).then_inc(att_loaded[r % 2], 16)
                        sp.wait_ge(x1b_ready, n + 1)
                        sp.dma_start(x1[r % 2][:], rows(x1_rows, n + 2)).then_inc(x1_loaded[r % 2], 16)

                run(sp, step, ahead=2)
                sp.wait_ge(res_stored, 16 * T)

            @block.gpsimd
            def _(pool):
                nc.gpsimd.memset(ones[:], 1.0).then_inc(ones_ready, 1)
                g2.att.pool_zero(nc)
                g3.att.pool_zero(nc)

                def att_lo(t, r):
                    pool.wait_ge(att_hi_ready, t + 1)
                    nc.gpsimd.tensor_tensor(attS[r % 2][1][:].rearrange("p c n -> p (c n)"), att[r % 2][:],
                                            attS[r % 2][0][:].bitcast(F32).rearrange("p c n -> p (c n)"),
                                            ALU.subtract).then_inc(att_lo_ready, 1)

                def terms(g, t, k, x, ready):
                    if isinstance(t, int) and t == 0:
                        pool.wait_ge(g.v_ready, 2)
                    pool.wait_ge(ready, t + 1)
                    ge(pool, g.att.f_ready, 2 * t + k - 1)
                    nc.gpsimd.tensor_tensor(g.terms[:, k, :], x, g.v_row[:, k, :], ALU.mult
                                            ).then_inc(g.terms_ready, 1)

                def diag(g, t):
                    pool.wait_ge(g.att.f_ready, 2 * t + 1)
                    ge(pool, g.att.scores_done, t)
                    nc.gpsimd.tensor_tensor(g.att.diag[:, 0, :], i64[:],
                                            g.att.f[:, 0:1].to_broadcast([P, NODES]), ALU.mult
                                            ).then_inc(g.att.diag_ready, 1)

                def step(n, r):
                    if live(n, 1):
                        n_y.pool_rstd(nc, pool, n - 1, z1_ready, norm_consts)
                    if live(n, 3):
                        g2.norm.pool_rstd(nc, pool, n - 3, g2.x_ready, norm_consts)
                    if live(n, 1):
                        n_1.pool_rstd(nc, pool, n - 1, x2_ready, norm_consts)
                    if live(n, 3):
                        for k in range(2):
                            terms(g3, n - 3, k, x3[(r - 3) % 2][:], g2.x_ready)
                    if live(n, 2):
                        g2.att.pool_prob(nc, pool, n - 2, gate)
                    if live(n, 1):
                        terms(g2, n - 1, 0, x2[(r - 1) % R][:], x2_ready)
                    if live(n, 3):
                        diag(g3, n - 3)
                    if live(n, 1):
                        terms(g2, n - 1, 1, x2[(r - 1) % R][:], x2_ready)
                    if live(n, 4):
                        g3.norm.pool_rstd(nc, pool, n - 4, g3.x_ready, norm_consts)
                    if live(n, -1):
                        att_lo(n + 1, (r + 1) % R)
                    if live(n, 3):
                        g3.att.pool_prob(nc, pool, n - 3, gate)
                    if live(n, 1):
                        diag(g2, n - 1)
                    if live(n, 0):
                        if isinstance(n, int) and n == 0:
                            pool.wait_ge(rows_loaded, 128)
                        pool.wait_ge(x1_loaded[r % 2], pair(n, r))
                        ge(pool, z1_ready, n)
                        nc.gpsimd.tensor_tensor(x1b[:], x1[r % 2][:], beta_row[:], ALU.add
                                                ).then_inc(x1b_ready, 1)

                att_lo(0, 0)
                run(pool, step, ahead=1)

            @block.scalar
            def _(act):
                def att_hi(t, r):
                    act.wait_ge(att_loaded[r % 2], pair(t, r))
                    ge(act, h1_done, t - 1)
                    nc.scalar.copy(attS[r % 2][0][:].rearrange("p c n -> p (c n)"), att[r % 2][:]
                                   ).then_inc(att_hi_ready, 1)

                def x_hi(g, t):
                    act.wait_ge(g.xT_done, t + 1)
                    ge(act, g.wh_done, t)
                    nc.scalar.copy(g.xT[0][:], g.turn[:]).then_inc(g.xT_hi_ready, 1)

                def wh_out(g, t):
                    act.wait_ge(g.wh_done, t + 1)
                    ge(act, g.sums_done, t)
                    nc.scalar.copy(g.wh[:], bank_a[:]).then_inc(g.wh_ready, 1)

                def turned(g, t):
                    ge(act, g.sums_done, t)
                    g.att.act_turned(nc, act, t)

                def dots(g, t):
                    ge(act, g.att.summed, t)
                    ge(act, g.att.diag_ready, t)
                    for k in range(2):
                        act.wait_ge(g.terms_ready, 2 * t + k + 1)
                        nc.scalar.activation(g.terms[:, k, :], g.terms[:, k, :], ACT.Identity,
                                             accum_out=g.att.f[:, k:k + 1]).then_inc(g.att.f_ready, 1)

                def normalise(norm, t, z, x, ready):
                    act.wait_ge(norm.shift_ready, t + 1)
                    nc.scalar.activation(x, z, ACT.Identity, scale=norm.rstd[:], bias=norm.shift[:]
                                         ).then_inc(ready, 1)

                def step(n, r):
                    if live(n, 4):
                        turned(g3, n - 4)
                    if live(n, -1):
                        att_hi(n + 1, (r + 1) % R)
                    if live(n, 2):
                        wh_out(g2, n - 2)
                    if live(n, 3):
                        ge(act, g3.z_ready, n - 4)
                        normalise(g2.norm, n - 3, g2.z[:], x3[(r - 3) % 2][:], g2.x_ready)
                    if live(n, 2):
                        g2.att.act_exp(nc, act, n - 2)
                    if live(n, 1):
                        ge(act, g2.z_ready, n - 4)
                        normalise(n_1, n - 1, z1[:], x2[(r - 1) % R][:], x2_ready)
                    if live(n, 3):
                        x_hi(g3, n - 3)
                    if live(n, 0):
                        act.wait_ge(h1T_done, n + 1)
                        ge(act, y_done, n)
                        nc.scalar.activation(h1T[0][:], turn_h[:], ACT.Relu).then_inc(h1T_hi_ready, 1)
                    if live(n, 3):
                        dots(g3, n - 3)
                    if live(n, 1):
                        x_hi(g2, n - 1)
                    if live(n, 3):
                        wh_out(g3, n - 3)
                    if live(n, 3):
                        g3.att.act_exp(nc, act, n - 3)
                    if live(n, 2):
                        turned(g2, n - 2)
                    if live(n, 1):
                        dots(g2, n - 1)
                    if live(n, 4):
                        ge(act, res_stored, 16 * (n - 4))
                        normalise(g3.norm, n - 4, g3.z[:], res[:], g3.x_ready)

                for k in range(4):
                    act.wait_ge(w_loaded[k % 2], 16 * (k // 2 + 1))
                    nc.scalar.copy(w_hi[:, k * KC:(k + 1) * KC, :], stage[k % 2][:]
                                   ).then_inc(w_hi_ready, 1)
                    if k == 0:
                        att_hi(0, 0)
                for g in (g2, g3):
                    for k in range(2):
                        act.wait_ge(g.v_spread, k + 1)
                        nc.scalar.copy(g.v_row[:, k, :], g.sums[:]).then_inc(g.v_ready, 1)
                run(act, step, ahead=1)

            @block.vector
            def _(dve):
                for k in range(4):
                    dve.wait_ge(w_hi_ready, k + 1)
                    nc.vector.tensor_tensor(w_lo[:, k * KC:(k + 1) * KC, :], stage[k % 2][:],
                                            w_hi[:, k * KC:(k + 1) * KC, :].bitcast(F32),
                                            ALU.subtract).then_inc(w_lo_ready, 1)
                    if k == 0:
                        dve.wait_ge(rows_loaded, 128)
                    if k < 2:
                        continue
                    g = (g2, g3)[k - 2]
                    for c in range(KC):
                        for s in range(2):
                            j = 2 * KC * (k - 2) + 2 * c + s
                            ge(dve, v_part, j)
                            nc.vector.tensor_tensor_reduce(
                                out=scrap[:], in0=stage[k % 2][:, c, :], in1=a_row[:, 2 * (k - 2) + s, :],
                                scale=1.0, scalar=0.0, op0=ALU.mult, op1=ALU.add,
                                accum_out=v_f[:, c, 2 * (k - 2) + s:2 * (k - 2) + s + 1]).then_inc(v_part, 1)
                    dve.wait_ge(v_part, 2 * KC * (k - 1))
                    for s in range(2):
                        if k == 3:
                            dve.wait_ge(g2.v_spread, s + 1)
                        col = 2 * (k - 2) + s
                        nc.vector.tensor_tensor(diag_v[s][:], ident[:, None, :].to_broadcast([P, KC, P]),
                                                v_f[:, :, col:col + 1].to_broadcast([P, KC, P]), ALU.mult
                                                ).then_inc(g.diag_v_ready, 1)

                def x_lo(g, t):
                    dve.wait_ge(g.xT_hi_ready, t + 1)
                    nc.vector.tensor_tensor(g.xT[1][:], g.turn[:], g.xT[0][:].bitcast(F32), ALU.subtract
                                            ).then_inc(g.xT_lo_ready, 1)

                def scores(g, t):
                    a = g.att
                    dve.wait_ge(a.scores_done, t + 1)
                    dve.wait_ge(a.f_ready, 2 * t + 2)
                    nc.vector.scalar_tensor_tensor(a.e1[:, 0, :], a.scores_psum, a.f[:, 1:2], bias23[:],
                                                   ALU.add, ALU.add).then_inc(a.summed, 1)

                def leaky(g, t):
                    a = g.att
                    dve.wait_ge(a.summed, t + 1)
                    ge(dve, a.exp_ready, t)
                    nc.vector.scalar_tensor_tensor(a.e2[:], a.e1[:], SLOPE_L23, a.e1[:], ALU.mult, ALU.max
                                                   ).then_inc(a.leaky, 1)

                def peak(g, t):
                    dve.wait_ge(g.att.leaky, t + 1)
                    nc.vector.tensor_reduce(g.att.peak[:], g.att.e2[:], AX_X, ALU.max, negate=True
                                            ).then_inc(g.att.peaked, 1)

                def residual(g, t, x):
                    dve.wait_ge(g.sums_done, t + 1)
                    ge(dve, g.x_ready, t)
                    nc.vector.tensor_tensor(g.z[:], g.sums[:], x, ALU.add).then_inc(g.z_ready, 1)

                def stats(g, t):
                    dve.wait_ge(g.z_ready, t + 1)
                    g.norm.dve_stats(nc, dve, t, g.z[:])

                def step(n, r):
                    if live(n, 1):
                        dve.wait_ge(y_done, n)
                        ge(dve, z1_ready, n - 1)
                        dve.wait_ge(att_b2_ready, n)
                        nc.vector.tensor_tensor(y[:], bank_b[:], att_b2[:], ALU.add).then_inc(y_ready, 1)
                    if live(n, 3):
                        residual(g2, n - 3, x2[(r - 3) % R][:])
                    if live(n, 1):
                        dve.wait_ge(y_ready, n)
                        n_y.dve_stats(nc, dve, n - 1, y[:])
                    if live(n, 3):
                        stats(g2, n - 3)
                    if live(n, 1):
                        n_y.dve_mean(nc, dve, n - 1, scaled)
                    if live(n, 3):
                        g2.norm.dve_mean(nc, dve, n - 3, g2.x_ready)
                    if live(n, 1):
                        dve.wait_ge(n_y.mv_ready, n)
                        nc.vector.scalar_tensor_tensor(y[:], y[:], n_y.mv[:, 0:1], gamma_row[:],
                                                       ALU.subtract, ALU.mult).then_inc(scaled, 1)
                    if live(n, 1):
                        dve.wait_ge(scaled, n)
                        dve.wait_ge(n_y.rstd_ready, n)
                        dve.wait_ge(x1b_ready, n)
                        ge(dve, x2_ready, n - 1)
                        nc.vector.scalar_tensor_tensor(z1[:], y[:], n_y.rstd[:], x1b[:], ALU.mult, ALU.add
                                                       ).then_inc(z1_ready, 1)
                    if live(n, 2):
                        scores(g2, n - 2)
                    if live(n, 1):
                        dve.wait_ge(z1_ready, n)
                        n_1.dve_stats(nc, dve, n - 1, z1[:])
                    if live(n, 2):
                        leaky(g2, n - 2)
                    if live(n, 1):
                        n_1.dve_mean(nc, dve, n - 1, x2_ready)
                    if live(n, 2):
                        peak(g2, n - 2)
                    if live(n, 0):
                        dve.wait_ge(att_turned, n + 1)
                        ge(dve, y_ready, n)
                        nc.vector.tensor_tensor(att_b2[:], turn_h[:].rearrange("p c n -> p (c n)"), b2_row[:],
                                                ALU.add).then_inc(att_b2_ready, 1)
                    if live(n, 2):
                        g2.att.dve_after_exp(nc, dve, n - 2, gate)
                    if live(n, 0):
                        dve.wait_ge(h1_done, n + 1)
                        ge(dve, h1T_done, n)
                        nc.vector.tensor_tensor(h1[:], bank_b[:], b1_row[:], ALU.add).then_inc(h1_ready, 1)
                    if live(n, 3):
                        x_lo(g3, n - 3)
                    if live(n, 4):
                        residual(g3, n - 4, x3[r % 2][:])
                    if live(n, 0):
                        dve.wait_ge(h1T_hi_ready, n + 1)
                        nc.vector.scalar_tensor_tensor(h1T[1][:], turn_h[:], 0.0, h1T[0][:].bitcast(F32),
                                                       ALU.max, ALU.subtract).then_inc(h1T_lo_ready, 1)
                    if live(n, 4):
                        stats(g3, n - 4)
                    if live(n, 1):
                        x_lo(g2, n - 1)
                    if live(n, 4):
                        g3.norm.dve_mean(nc, dve, n - 4, g3.x_ready)
                    if live(n, 3):
                        scores(g3, n - 3)
                        leaky(g3, n - 3)
                    if live(n, 3):
                        peak(g3, n - 3)
                        g3.att.dve_after_exp(nc, dve, n - 3, gate)

                run(dve, step)

            @block.tensor
            def _(pe):
                def turn_x(g, t, x, ready):
                    pe.wait_ge(ready, t + 1)
                    ge(pe, g.xT_lo_ready, t)
                    for c in range(KC):
                        ins = nc.tensor.transpose(g.turn[:, c, :], x[:, c * P:(c + 1) * P], ident[:])
                    ins.then_inc(g.xT_done, 1)

                def project(g, t):
                    pe.wait_ge(g.xT_lo_ready, t + 1)
                    if isinstance(t, int) and t == 0:
                        pe.wait_ge(w_lo_ready, g.q // KC + 1)
                    product(nc, bank_a[:], g.xT, (w_hi, w_lo),
                            [(c, g.q + c) for c in range(KC)]).then_inc(g.wh_done, 1)

                def spread(g, t):
                    pe.wait_ge(g.att.diag_ready, t + 1)
                    nc.tensor.matmul(g.att.scores_psum, same_graph[:], g.att.diag[:, 0, :],
                                     start=True, stop=True).then_inc(g.att.scores_done, 1)

                def sums(g, t):
                    pe.wait_ge(g.att.turned_ready, 2 * t + 2)
                    pe.wait_ge(g.wh_ready, t + 1)
                    ge(pe, g.z_ready, t)
                    if isinstance(t, int) and t == 0:
                        pe.wait_ge(g.v_ready, 2)
                    nc.tensor.matmul(g.sums[:], g.att.turned[:, 0, :], g.wh[:], start=True, stop=True
                                     ).then_inc(g.sums_done, 1)

                def step(n, r):
                    if live(n, 4):
                        if live(n, 3):
                            pe.wait_ge(g2.att.turned_ready, 2 * (n - 2))
                        g3.att.pe_turn(nc, pe, n - 4, ident)
                    if live(n, 2):
                        ge(pe, g3.wh_ready, n - 3)
                        project(g2, n - 2)
                        if live(n, 4):
                            pe.wait_ge(g3.att.turned_ready, 2 * (n - 3))
                        elif live(n, 3):
                            pe.wait_ge(g2.att.turned_ready, 2 * (n - 2))
                        spread(g2, n - 2)
                    if live(n, 0):
                        pe.wait_ge(att_loaded[r % 2], pair(n, r))
                        ge(pe, h1T_lo_ready, n)
                        for c in range(KC):
                            ins = nc.tensor.transpose(turn_h[:, c, :], att[r % 2][:, c * P:(c + 1) * P], ident[:])
                        ins.then_inc(att_turned, 1)
                        pe.wait_ge(att_lo_ready, n + 1)
                        ge(pe, y_ready, n)
                        product(nc, bank_b[:], attS[r % 2], (w_hi, w_lo), [(c, c) for c in range(KC)]
                                ).then_inc(h1_done, 1)
                    if live(n, 3):
                        turn_x(g3, n - 3, x3[(r - 3) % 2], g2.x_ready)
                    if live(n, 4):
                        sums(g3, n - 4)
                    if live(n, 0):
                        pe.wait_ge(h1_ready, n + 1)
                        pe.wait_ge(att_b2_ready, n + 1)
                        for c in range(KC):
                            ins = nc.tensor.transpose(turn_h[:, c, :], h1[:, c * P:(c + 1) * P], ident[:])
                        ins.then_inc(h1T_done, 1)
                    if live(n, 1):
                        turn_x(g2, n - 1, x2[(r - 1) % R], x2_ready)
                    if live(n, 3):
                        ge(pe, g2.wh_ready, capped(n - 1, T))
                        project(g3, n - 3)
                        if live(n, 2):
                            pe.wait_ge(g2.att.summed, n - 1)
                        elif live(n, 4):
                            pe.wait_ge(g3.att.turned_ready, 2 * (n - 3))
                        spread(g3, n - 3)
                    if live(n, 0):
                        pe.wait_ge(h1T_lo_ready, n + 1)
                        product(nc, bank_b[:], h1T, (w_hi, w_lo), [(c, KC + c) for c in range(2)], last=False)
                    if live(n, 2):
                        if live(n, 3):
                            pe.wait_ge(g3.att.summed, n - 2)
                        g2.att.pe_turn(nc, pe, n - 2, ident)
                    if live(n, 0):
                        product(nc, bank_b[:], h1T, (w_hi, w_lo), [(c, KC + c) for c in range(2, KC)], first=False
                                ).then_inc(y_done, 1)
                    if live(n, 2):
                        sums(g2, n - 2)

                def vectors(g):
                    pe.wait_ge(ones_ready, 1)
                    for s in range(2):
                        pe.wait_ge(g.diag_v_ready, s + 1)
                        ge(pe, g.v_ready, s)
                        nc.tensor.matmul(g.sums[:], ones[:], diag_v[s][:].rearrange("p c n -> p (c n)"),
                                         start=True, stop=True).then_inc(g.v_spread, 1)

                vectors(g2)
                vectors(g3)
                pe.wait_ge(w_lo_ready, 2)
                run(pe, step)


_INS = ['x', 'adj', 'L0_gnn_W', 'L0_gnn_b', 'L1_gnn_W_heads', 'L1_gnn_a_heads', 'L1_gnn_W_out', 'L1_gnn_a_out',
        'L1_gnn_w1', 'L1_gnn_b1', 'L1_gnn_w2', 'L1_gnn_b2', 'L1_gnn_ln_gamma', 'L1_gnn_ln_beta',
        'L2_gnn_W', 'L2_gnn_a_src', 'L2_gnn_a_dst', 'L3_gnn_W', 'L3_gnn_a_src', 'L3_gnn_a_dst']


def kernel(**inputs):
    import numpy as _np
    import concourse.bacc as _bacc
    from concourse import mybir as _mybir
    from concourse.bass_utils import run_bass_kernel_spmd as _run

    nc = _bacc.Bacc("TRN2", target_bir_lowering=False, num_devices=1)
    arrays, args = {}, []
    for name in _INS:
        a = _np.asarray(inputs[name])
        if name == 'L0_gnn_W':
            a = a.T
        a = _np.ascontiguousarray(a)
        arrays[f"in_{name}"] = a
        args.append(nc.dram_tensor(f"in_{name}", a.shape, _mybir.dt.from_np(a.dtype), kind="ExternalInput").ap())
    shape = inputs['x'].shape
    out = nc.dram_tensor("out_0", shape, _mybir.dt.float32, kind="ExternalOutput").ap()
    gnn_stack_kernel(nc, *args, out)
    r = _run(nc, [arrays], core_ids=[0])
    return r.results[0]["out_0"]
```

```python
from contextlib import ExitStack

import concourse.bass as bass
from concourse import mybir

F32 = mybir.dt.float32
F32R = mybir.dt.float32r
I32 = mybir.dt.int32
ALU = mybir.AluOpType
ACT = mybir.ActivationFunctionType
AX_X = mybir.AxisListType.X

P = 128
D = 512
KC = D // P
NODES = 64
HEADS = 4
LN_EPS = 1e-5
SLOPE_L1 = 0.01
SLOPE_L23 = 0.2
MASKED_L1 = -1e9
MASKED_L23 = -3e38


def ge(eng, sem, value):
    if not isinstance(value, int) or value > 0:
        eng.wait_ge(sem, value)


def capped(n, most):
    return min(n, most) if isinstance(n, int) else n


def split_passes(hi_lhs, lo_lhs, hi_rhs, lo_rhs):
    return ((hi_lhs, hi_rhs), (hi_lhs, lo_rhs), (lo_lhs, hi_rhs))


def product(nc, out, lhs, rhs, chunks, first=True, last=True):
    n = len(chunks)
    for c, (kl, kr) in enumerate(chunks):
        passes = split_passes(lhs[0][:, kl, :], lhs[1][:, kl, :], rhs[0][:, kr, :], rhs[1][:, kr, :])
        for q, (a, b) in enumerate(passes):
            ins = nc.tensor.matmul(out, a, b, start=first and c == 0 and q == 0,
                                   stop=last and c == n - 1 and q == 2)
    return ins


class Attention:

    def __init__(self, nc, ctx, name, heads, slope, scores_psum, turned_psum, mask=None, f_parts=1):
        def sb(n, shape, dt=F32):
            return ctx.enter_context(nc.sbuf_tensor(f"{name}_{n}", shape, dt))

        def sem(n):
            return ctx.enter_context(nc.semaphore(f"{name}_{n}"))

        self.heads, self.slope, self.mask = heads, slope, mask
        self.f_parts = f_parts
        self.scores_psum = scores_psum
        self.turned_psum = turned_psum
        self.f = sb("f", [P, 2 * heads])
        self.diag = sb("diag", [P, heads, NODES])
        self.e1 = sb("e1", [P, heads, NODES])
        self.e2 = sb("e2", [P, heads, NODES])
        self.ex = sb("ex", [P, heads, NODES])
        self.peak = sb("peak", [P, heads])
        self.total = sb("total", [P, heads])
        self.inv = sb("inv", [P, heads])
        self.prob = sb("prob", [P, heads, 2, NODES])
        self.turned = sb("turned", [P, heads, P])
        self.pause = sb("pause", [P, 1])
        self.zeroed = sem("zeroed")
        self.f_ready, self.diag_ready, self.scores_done = sem("f_ready"), sem("diag_ready"), sem("scores_done")
        self.summed, self.leaky, self.masked = sem("summed"), sem("leaky"), sem("masked")
        self.peaked, self.shifted, self.exp_ready = sem("peaked"), sem("shifted"), sem("exp_ready")
        self.totalled, self.inverted, self.gated = sem("totalled"), sem("inverted"), sem("gated")
        self.prob_ready, self.turned_done, self.turned_ready = (
            sem("prob_ready"), sem("turned_done"), sem("turned_ready"))

    def pool_zero(self, nc):
        nc.gpsimd.memset(self.turned[:], 0.0).then_inc(self.zeroed, 1)

    def pool_diag(self, nc, pool, t, i64):
        pool.wait_ge(self.f_ready, self.f_parts * t + (self.f_parts + 1) // 2)
        ge(pool, self.scores_done, t)
        shape = [P, self.heads, NODES]
        nc.gpsimd.tensor_tensor(self.diag[:], i64[:, None, :].to_broadcast(shape),
                                self.f[:, 0:self.heads, None].to_broadcast(shape),
                                ALU.mult).then_inc(self.diag_ready, 1)

    def pe_scores(self, nc, pe, t, same_graph):
        pe.wait_ge(self.diag_ready, t + 1)
        ge(pe, self.summed, t)
        nc.tensor.matmul(self.scores_psum, same_graph[:], self.diag[:].rearrange("p h j -> p (h j)"),
                         start=True, stop=True).then_inc(self.scores_done, 1)

    def dve_before_exp(self, nc, dve, t, fill):
        shape = [P, self.heads, NODES]
        dve.wait_ge(self.scores_done, t + 1)
        dve.wait_ge(self.f_ready, self.f_parts * (t + 1))
        ge(dve, self.exp_ready, t)
        nc.vector.tensor_tensor(self.e1[:], self.scores_psum.rearrange("p (h j) -> p h j", h=self.heads),
                                self.f[:, self.heads:, None].to_broadcast(shape), ALU.add
                                ).then_inc(self.summed, 1)
        dve.wait_ge(self.summed, t + 1)
        nc.vector.scalar_tensor_tensor(self.e2[:], self.e1[:], self.slope, self.e1[:], ALU.mult, ALU.max
                                       ).then_inc(self.leaky, 1)
        dve.wait_ge(self.leaky, t + 1)
        nc.vector.memset(self.pause[:], 0.0)
        nc.vector.copy_predicated(self.e2[:], self.mask[:, None, :].to_broadcast(shape),
                                  fill[:, 0:1, None].to_broadcast(shape)).then_inc(self.masked, 1)
        dve.wait_ge(self.masked, t + 1)
        if self.heads == 1:
            nc.vector.tensor_reduce(self.peak[:], self.e2[:], AX_X, ALU.max, negate=True
                                    ).then_inc(self.peaked, 1)
            return
        nc.vector.reduce_max(self.peak[:], self.e2[:], AX_X).then_inc(self.peaked, 1)
        dve.wait_ge(self.peaked, t + 1)
        nc.vector.tensor_tensor(self.e1[:], self.e2[:], self.peak[:, :, None].to_broadcast(shape),
                                ALU.subtract).then_inc(self.shifted, 1)

    def act_exp(self, nc, act, t):
        ge(act, self.prob_ready, t)
        if self.heads == 1:
            act.wait_ge(self.peaked, t + 1)
            ge(act, self.inverted, t)
            nc.scalar.activation(self.ex[:, 0, :], self.e2[:, 0, :], ACT.Exp, bias=self.peak[:],
                                 accum_out=self.total[:]).then_inc(self.exp_ready, 1)
        else:
            act.wait_ge(self.shifted, t + 1)
            ge(act, self.totalled, t)
            nc.scalar.activation(self.ex[:], self.e1[:], ACT.Exp).then_inc(self.exp_ready, 1)

    def dve_after_exp(self, nc, dve, t, gate=None):
        dve.wait_ge(self.exp_ready, t + 1)
        if self.heads > 1:
            nc.vector.reduce_sum(self.total[:], self.ex[:], AX_X).then_inc(self.totalled, 1)
            dve.wait_ge(self.totalled, t + 1)
        ge(dve, self.prob_ready, t)
        nc.vector.reciprocal(self.inv[:], self.total[:]).then_inc(self.inverted, 1)
        if gate is not None:
            dve.wait_ge(self.inverted, t + 1)
            nc.vector.tensor_tensor(self.inv[:], self.inv[:], gate[:], ALU.mult).then_inc(self.gated, 1)

    def pool_prob(self, nc, pool, t, gate=None):
        if gate is not None:
            pool.wait_ge(self.gated, t + 1)
        else:
            pool.wait_ge(self.inverted, t + 1)
        pool.wait_ge(self.exp_ready, t + 1)
        ge(pool, self.turned_done, t)
        for g in range(2):
            ins = nc.gpsimd.tensor_tensor(self.prob[:, :, g, :], self.ex[:],
                                          self.inv[:, :, None].to_broadcast([P, self.heads, NODES]), ALU.mult)
        ins.then_inc(self.prob_ready, 1)

    def pe_turn(self, nc, pe, t, ident):
        pe.wait_ge(self.prob_ready, t + 1)
        ge(pe, self.turned_ready, 2 * t)
        for h in range(self.heads):
            ins = nc.tensor.transpose(self.turned_psum[:, h, :],
                                      self.prob[:, h, :, :].rearrange("p g j -> p (g j)"), ident[:])
        ins.then_inc(self.turned_done, 1)

    def act_turned(self, nc, act, t):
        act.wait_ge(self.turned_done, t + 1)
        if isinstance(t, int) and t == 0:
            act.wait_ge(self.zeroed, 1)
        for g in range(2):
            r = slice(g * NODES, (g + 1) * NODES)
            nc.scalar.copy(self.turned[r, :, r], self.turned_psum[r, :, r]).then_inc(self.turned_ready, 1)


class Norm:

    def __init__(self, nc, ctx, name, shifted=False):
        def sb(n, shape):
            return ctx.enter_context(nc.sbuf_tensor(f"{name}_{n}", shape, F32))

        def sem(n):
            return ctx.enter_context(nc.semaphore(f"{name}_{n}"))

        self.shifted = shifted
        self.pause = sb("pause", [P, 1])
        self.stats, self.mv = sb("stats", [P, 6]), sb("mv", [P, 2])
        self.veps, self.rstd, self.shift = sb("veps", [P, 1]), sb("rstd", [P, 1]), sb("shift", [P, 1])
        self.stats_ready, self.mv_ready, self.veps_ready, self.rstd_ready = (
            sem("stats_ready"), sem("mv_ready"), sem("veps_ready"), sem("rstd_ready"))
        self.shift_ready = self.rstd_ready
        if shifted:
            self.less = sb("less", [P, 1])
            self.less_ready, self.shift_ready = sem("less_ready"), sem("shift_ready")

    def dve_stats(self, nc, dve, t, x):
        nc.vector.bn_stats(self.stats[:], x).then_inc(self.stats_ready, 1)

    def dve_mean(self, nc, dve, t, used):
        dve.wait_ge(self.stats_ready, t + 1)
        ge(dve, used, t)
        ge(dve, self.shift_ready, t)
        nc.vector.memset(self.pause[:], 0.0)
        nc.vector.bn_aggr(self.mv[:], self.stats[:]).then_inc(self.mv_ready, 1)

    def pool_rstd(self, nc, pool, t, used, consts):
        pool.wait_ge(self.mv_ready, t + 1)
        nc.gpsimd.tensor_tensor(self.veps[:], self.mv[:, 1:2], consts[:, 0:1], ALU.add
                                ).then_inc(self.veps_ready, 1)
        if self.shifted:
            nc.gpsimd.tensor_tensor(self.less[:], self.mv[:, 0:1], consts[:, 2:3], ALU.mult
                                    ).then_inc(self.less_ready, 1)
        pool.wait_ge(self.veps_ready, t + 1)
        ge(pool, used, t)
        nc.gpsimd.tensor_tensor(self.rstd[:], self.veps[:], consts[:, 1:2], ALU.pow
                                ).then_inc(self.rstd_ready, 1)
        if self.shifted:
            pool.wait_ge(self.rstd_ready, t + 1)
            pool.wait_ge(self.less_ready, t + 1)
            nc.gpsimd.tensor_tensor(self.shift[:], self.less[:], self.rstd[:], ALU.mult
                                    ).then_inc(self.shift_ready, 1)


def gnn_stack_kernel(nc, x, adj, W0T, b0, Wh, ah, Wo, ao, w1, b1, w2, b2, gamma, beta,
                     W2, a2s, a2d, W3, a3s, a3d, out):
    B, N, _ = x.shape
    T = B * N // P
    x_rows = x.rearrange("b n d -> (b n) d")
    out_rows = out.rearrange("b n d -> (b n) d")
    x1_rows = nc.dram_tensor("x1_scratch", (B * N, D), F32).ap()
    att_rows = nc.dram_tensor("att_scratch", (T * P, D), F32).ap()

    def rows(dram, t):
        return dram[bass.ts(t, P), :]

    def chunked(w):
        return w.rearrange("(c p) n -> p c n", p=P)

    with ExitStack() as top:
        def sb(n, shape, dt=F32):
            return top.enter_context(nc.sbuf_tensor(n, shape, dt))

        def sem(n):
            return top.enter_context(nc.semaphore(n))

        NQ = 2 * HEADS * KC
        held = top.enter_context(ExitStack())
        ident = sb("ident", [P, P])
        ones = sb("ones", [P, P])
        v_cols = sb("v_cols", [P, (HEADS + 2) * KC, 2])
        same_graph = sb("same_graph", [P, P])
        i64 = sb("i64", [P, NODES])
        norm_consts = sb("norm_consts", [P, 3])
        fill1 = sb("fill1", [P, 1])
        mask1 = sb("mask1", [P, NODES], I32)
        bias23 = sb("bias23", [P, NODES])
        gate = sb("gate", [P, 1])
        w_first = sb("w_first", [P, KC, D])
        w_first_loaded = sem("w_first_loaded")
        big_hi = held.enter_context(nc.sbuf_tensor("big_hi", [P, NQ, D], F32R))
        big_lo = held.enter_context(nc.sbuf_tensor("big_lo", [P, NQ, D], F32R))
        att_stored = sem("att_stored")
        stage_loaded = sem("stage_loaded")

        with ExitStack() as ctx:
            def sb(n, shape, dt=F32):
                return ctx.enter_context(nc.sbuf_tensor(n, shape, dt))

            def sem(n):
                return ctx.enter_context(nc.semaphore(n))

            XR, UN = 4, 4
            GROUP = 2 * KC
            WP = 2
            w0 = (sb("w0_hi", [P, 2 * KC, D], F32R), sb("w0_lo", [P, 2 * KC, D], F32R))
            w0f = [w_first[:, b * WP:(b + 1) * WP, :] for b in range(KC // WP)]
            stage = sb("stage", [P, D])
            v_stage = sb("v_stage", [P, D])
            a_pair = sb("a_pair", [P, 2, D])
            v_sums = sb("v_sums", [P, KC, 2])
            xt = [sb(f"xt{r}", [P, D]) for r in range(XR)]
            xT = [(sb(f"x0T_hi{b}", [P, KC, P], F32R), sb(f"x0T_lo{b}", [P, KC, P], F32R)) for b in range(2)]
            xb = sb("xb", [P, D])
            wj = sb("wj", [P, D])
            z = sb("z", [P, D])
            x1 = [sb(f"x1_{b}", [P, D]) for b in range(2)]
            adj_i = sb("adj_i", [P, NODES], I32)
            adj_f = sb("adj_f", [P, NODES])
            adj_bd, zero_f = z[:, 0:P], z[:, P:P + NODES]
            none = sb("none", [P, 1])
            deg = sb("deg", [P, 1])
            adj_T = sb("adj_T", [P, P])
            db = sb("db", [P, D])
            turn = [ctx.enter_context(nc.psum_tensor(f"turn0{b}", [P, KC, P], F32)) for b in range(2)]
            wj_psum = ctx.enter_context(nc.psum_tensor("wj_psum", [P, D], F32))
            wi_psum = [ctx.enter_context(nc.psum_tensor(f"wi_psum{b}", [P, D], F32)) for b in range(2)]
            nb_psum = [ctx.enter_context(nc.psum_tensor(f"nb_psum{b}", [P, D], F32)) for b in range(2)]
            junk = ctx.enter_context(nc.psum_tensor("junk0", [P, D], F32))
            first_sem = sem("first_of_layer0")
            norm = Norm(nc, ctx, "n0")
            loaded = [sem(f"loaded{r}") for r in range(XR)]
            w0_loaded = [sem(f"w0_loaded{b}") for b in range(2)]
            small_loaded, b0_loaded, w0_hi_ready, w0_lo_ready = (
                sem("small_loaded"), sem("b0_loaded"), sem("w0_hi_ready"), sem("w0_lo_ready"))
            zeros_set, consts_set, adj_ready, setup_step, bd_ready, bd_turned, adj_T_ready = (
                sem("zeros_set"), sem("consts_set"), sem("adj_ready"), sem("setup_step"), sem("bd_ready"),
                sem("bd_turned"), sem("adj_T_ready"))
            xT_done, xT_hi_ready, xT_lo_ready, wj_done, wj_ready, wi_done, nb_done = (
                sem("x0T_done"), sem("x0T_hi_ready"), sem("x0T_lo_ready"), sem("wj_done"), sem("wj_ready"),
                sem("wi_done"), sem("nb_done"))
            xb_ready, own_ready, z_ready, x1_ready = (
                sem("xb_ready"), sem("own_ready"), sem("z_ready"), sem("x1_ready"))
            big_hi_ready, big_lo_ready = sem("big_hi_ready"), sem("big_lo_ready")
            v_loaded, pair_loaded, v_part, v_kept = sem("v_loaded"), sem("pair_loaded"), sem("v_part"), sem("v_kept")
            x1_out = [sem(f"x1_out{b}") for b in range(2)]
            layer0_sems = range(first_sem.num, x1_out[1].num + 1)
            block = ctx.enter_context(nc.Block())
            Wh_rows = Wh.rearrange("h k o -> (h k) o")

            def count(t, r):
                return 16 * (t // XR) + 16 if isinstance(t, int) else 4 * (t - r) + 16

            def groups(eng, step):
                def group(G, vectors):
                    for r in range(GROUP):
                        step(G * GROUP + r, r, G * KC + r // 2 if vectors else None, G)
                group(0, True)
                with eng.Fori(1, HEADS) as G:
                    group(G, True)
                for G in range(HEADS, HEADS + 2):
                    group(G, True)
                for G in range(HEADS + 2, T // GROUP):
                    group(G, False)

            @block.sync
            def _(sp):
                sp.dma_start(xt[0][:], rows(x_rows, 0)).then_inc(loaded[0], 16)
                for g in range(2):
                    sp.dma_start(adj_i[g * NODES:(g + 1) * NODES, :], adj).then_inc(small_loaded, 16)
                for k in range(2 * KC // WP):
                    piece = (k * WP + KC) % (2 * KC) * P
                    ge(sp, w0_lo_ready, k - 1)
                    sp.dma_start(w0f[k % 2], W0T[piece:piece + WP * P, :].rearrange("(c p) n -> p c n", p=P)
                                 ).then_inc(w0_loaded[k % 2], 16)
                    if k == 1:
                        sp.dma_start(db[:], b0.partition_broadcast(P)).then_inc(b0_loaded, 16)
                        for r in range(1, XR):
                            sp.dma_start(xt[r][:], rows(x_rows, r)).then_inc(loaded[r], 16)

                def step(t, r, q, G):
                    late = isinstance(G, int) and G >= HEADS
                    if q is not None and r == 0:
                        ge(sp, v_part, 2 * q)
                        for k in range(2):
                            a = ((a2d, a2s), (a3d, a3s))[G - HEADS][k] if late else ah[
                                bass.ds(G, 1), k * D:(k + 1) * D].rearrange("a o -> (a o)")
                            sp.dma_start(a_pair[:, k, :], a.partition_broadcast(P)).then_inc(pair_loaded, 16)
                    if q is not None and r % 2 == 0:
                        ge(sp, v_part, 2 * q)
                        source = (W2, W3)[G - HEADS][q % KC * P:(q % KC + 1) * P, :] if late else rows(Wh_rows, q)
                        sp.dma_start(v_stage[:], source).then_inc(v_loaded, 16)
                    sp.wait_ge(x1_ready, t + 1)
                    sp.dma_start(rows(x1_rows, t), x1[r % 2][:]).then_inc(x1_out[r % 2], 16)
                    if not isinstance(t, int) or t + XR < T:
                        sp.dma_start(xt[r % XR][:], rows(x_rows, t + XR)).then_inc(loaded[r % XR], 16)

                groups(sp, step)
                for b in range(2):
                    sp.wait_ge(x1_out[b], 16 * T // 2)

            @block.gpsimd
            def _(pool):
                nc.gpsimd.memset(ident[:], 0.0).then_inc(zeros_set, 1)
                nc.gpsimd.memset(i64[:], 0.0).then_inc(zeros_set, 1)
                nc.gpsimd.memset(adj_bd, 0.0).then_inc(zeros_set, 1)
                nc.gpsimd.memset(same_graph[:], 0.0).then_inc(zeros_set, 1)
                for k, value in enumerate((LN_EPS, -0.5, -1.0)):
                    nc.gpsimd.memset(norm_consts[:, k:k + 1], value).then_inc(consts_set, 1)
                nc.gpsimd.memset(fill1[:], MASKED_L1).then_inc(consts_set, 1)
                nc.gpsimd.memset(ones[:], 1.0).then_inc(consts_set, 1)
                pool.wait_ge(zeros_set, 4)
                for g in range(2):
                    r = slice(g * NODES, (g + 1) * NODES)
                    pool.wait_ge(zeros_set, 4 + g)
                    nc.gpsimd.memset(same_graph[r, r], 1.0).then_inc(consts_set, 1)
                    pool.wait_ge(consts_set, 6 + g)
                    nc.gpsimd.affine_select(out=i64[:], in_=i64[:], compare_op=ALU.not_equal, fill=1.0,
                                            base=-g * NODES, pattern=[[-1, NODES]], channel_multiplier=1
                                            ).then_inc(zeros_set, 1)
                pool.wait_ge(zeros_set, 6)
                nc.gpsimd.affine_select(out=ident[:], in_=ident[:], compare_op=ALU.not_equal, fill=1.0,
                                        base=0, pattern=[[-1, P]], channel_multiplier=1).then_inc(consts_set, 1)
                pool.wait_ge(consts_set, 8)
                pool.wait_ge(setup_step, 7)

                def load_block(q, source, k):
                    ge(pool, big_lo_ready, q)
                    pool.dma_start(stage[:], source[bass.ts(k, P), :]).then_inc(stage_loaded, 16)

                def split_hi(q):
                    pool.wait_ge(stage_loaded, 16 * q + 16)
                    nc.gpsimd.tensor_copy(big_hi[:, bass.ds(q, 1), :], stage[:, None, :]
                                          ).then_inc(big_hi_ready, 1)

                def split_lo(q):
                    pool.wait_ge(big_hi_ready, q + 1)
                    nc.gpsimd.tensor_tensor(big_lo[:, bass.ds(q, 1), :], stage[:, None, :],
                                            big_hi[:, bass.ds(q, 1), :].bitcast(F32), ALU.subtract
                                            ).then_inc(big_lo_ready, 1)

                def tile(t, r):
                    pool.wait_ge(loaded[r], count(t, r))
                    ge(pool, own_ready, t)
                    nc.gpsimd.tensor_tensor(xb[:], xt[r][:], db[:], ALU.add).then_inc(xb_ready, 1)

                def two(t, r, q, source, k):
                    load_block(q, source, k)
                    tile(t, r)
                    split_hi(q)
                    norm.pool_rstd(nc, pool, t, x1_ready, norm_consts)
                    tile(t + 1, r + 1)
                    split_lo(q)
                    norm.pool_rstd(nc, pool, t + 1, x1_ready, norm_consts)

                def four(k, source, before):
                    for i in range(2):
                        q = 2 * k + i + before
                        two(2 * q, 2 * i, q, source, 2 * k + i)

                four(0, Wh_rows, 0)
                with pool.Fori(1, NQ // 4) as k:
                    four(k, Wh_rows, 0)
                with pool.Fori(0, NQ // 4) as k:
                    four(k, Wo, NQ // 2)

            @block.scalar
            def _(act):
                for k in range(2 * KC // WP):
                    first = (k * WP + KC) % (2 * KC)
                    if k == 0:
                        act.wait_ge(xT_done, 1)
                        nc.scalar.copy(xT[0][0][:], turn[0][:]).then_inc(xT_hi_ready, 1)
                    act.wait_ge(w0_loaded[k % 2], 16 * (k // 2 + 1))
                    nc.scalar.copy(w0[0][:, first:first + WP, :], w0f[k % 2]).then_inc(w0_hi_ready, 1)

                def x_hi(t, b):
                    act.wait_ge(xT_done, t + 1)
                    ge(act, wi_done, t - 1)
                    nc.scalar.copy(xT[b][0][:], turn[b][:]).then_inc(xT_hi_ready, 1)

                def step(t, b, more=True):
                    if more:
                        x_hi(t + 1, 1 - b)
                    act.wait_ge(wj_done, t + 1)
                    ge(act, nb_done, t)
                    nc.scalar.copy(wj[:], wj_psum[:]).then_inc(wj_ready, 1)

                step(0, 0)
                step(1, 1)
                with act.Fori(1, T // 2 - 1) as g:
                    step(g * 2, 0)
                    step(g * 2 + 1, 1)
                step(T - 2, 0)
                step(T - 1, 1, False)

            @block.vector
            def _(dve):
                dve.wait_ge(small_loaded, 32)
                dve.wait_ge(zeros_set, 6)
                nc.vector.tensor_copy(adj_f[:], adj_i[:]).then_inc(adj_ready, 1)
                dve.wait_ge(adj_ready, 1)
                nc.vector.reduce_sum(deg[:], adj_f[:], AX_X).then_inc(setup_step, 1)
                nc.vector.tensor_scalar(mask1[:], adj_f[:], 0.0, None, ALU.is_le).then_inc(setup_step, 1)
                nc.vector.tensor_scalar(bias23[:], adj_f[:], 0.0, MASKED_L23, ALU.is_equal, ALU.mult
                                        ).then_inc(setup_step, 1)
                nc.vector.tensor_scalar(zero_f, adj_f[:], 0.0, None, ALU.is_equal).then_inc(setup_step, 1)
                for g in range(2):
                    r = slice(g * NODES, (g + 1) * NODES)
                    nc.vector.tensor_copy(adj_bd[r, r], adj_f[r, :]).then_inc(bd_ready, 1)
                dve.wait_ge(setup_step, 4)
                nc.vector.tensor_reduce(none[:], zero_f, AX_X, ALU.min).then_inc(setup_step, 1)
                dve.wait_ge(setup_step, 5)
                nc.vector.tensor_scalar(gate[:], none[:], -1.0, 1.0, ALU.mult, ALU.add).then_inc(setup_step, 1)
                dve.wait_ge(bd_turned, 1)
                nc.vector.tensor_copy(adj_T[:], nb_psum[1][:, 0:P]).then_inc(adj_T_ready, 1)

                def x_lo(t, b):
                    dve.wait_ge(xT_hi_ready, t + 1)
                    nc.vector.tensor_tensor(xT[b][1][:], turn[b][:], xT[b][0][:].bitcast(F32), ALU.subtract
                                            ).then_inc(xT_lo_ready, 1)

                for k in range(2 * KC // WP):
                    first = (k * WP + KC) % (2 * KC)
                    dve.wait_ge(w0_hi_ready, k + 1)
                    nc.vector.tensor_tensor(w0[1][:, first:first + WP, :], w0f[k % 2],
                                            w0[0][:, first:first + WP, :].bitcast(F32),
                                            ALU.subtract).then_inc(w0_lo_ready, 1)
                    if k == 0:
                        x_lo(0, 0)
                    if k == 1:
                        dve.wait_ge(b0_loaded, 16)
                        nc.vector.tensor_scalar(db[:], db[:], deg[:], None, ALU.mult).then_inc(setup_step, 1)

                def step(t, r, q, G):
                    b = r % 2
                    if not isinstance(t, int) or t + 1 < T:
                        x_lo(t + 1, 1 - b)
                    dve.wait_ge(xb_ready, t + 1)
                    dve.wait_ge(wi_done, t + 1)
                    ge(dve, x1_ready, t)
                    nc.vector.scalar_tensor_tensor(z[:], wi_psum[b][:], deg[:], xb[:], ALU.mult, ALU.add
                                                   ).then_inc(own_ready, 1)
                    dve.wait_ge(own_ready, t + 1)
                    dve.wait_ge(nb_done, t + 1)
                    nc.vector.tensor_tensor(z[:], nb_psum[b][:], z[:], ALU.add).then_inc(z_ready, 1)
                    dve.wait_ge(z_ready, t + 1)
                    norm.dve_stats(nc, dve, t, z[:])
                    norm.dve_mean(nc, dve, t, x1_ready)
                    if q is not None and b == 1:
                        dve.wait_ge(pair_loaded, pairs(q, r))
                        dve.wait_ge(v_loaded, 16 * q + 16)
                        for k in range(2):
                            ge(dve, v_part, 2 * q + k)
                            if r == 1 and k == 0:
                                ge(dve, v_kept, G)
                            nc.vector.tensor_tensor_reduce(
                                out=junk[:], in0=v_stage[:], in1=a_pair[:, k, :], scale=1.0, scalar=0.0,
                                op0=ALU.mult, op1=ALU.add,
                                accum_out=v_sums[:, r // 2, k:k + 1]).then_inc(v_part, 1)
                        if r == GROUP - 1:
                            dve.wait_ge(v_part, 2 * q + 2)
                            nc.vector.tensor_copy(v_cols[:, bass.ts(G, KC), :], v_sums[:]).then_inc(v_kept, 1)
                    dve.wait_ge(norm.rstd_ready, t + 1)
                    ge(dve, x1_out[b], 16 * (t // 2) if isinstance(t, int) else 8 * (t - b))
                    nc.vector.tensor_scalar(x1[b][:], z[:], norm.mv[:, 0:1], norm.rstd[:],
                                            ALU.subtract, ALU.mult).then_inc(x1_ready, 1)

                def pairs(q, r):
                    return 32 * (q // KC + 1) if isinstance(q, int) else 8 * (q - r // 2) + 32

                groups(dve, step)

            @block.tensor
            def _(pe):
                def turn_x(t, r):
                    pe.wait_ge(loaded[r % XR], count(t, r % XR))
                    ge(pe, xT_lo_ready, t - 1)
                    for c in range(KC):
                        ins = nc.tensor.transpose(turn[r % 2][:, c, :], xt[r % XR][:, c * P:(c + 1) * P], ident[:])
                    ins.then_inc(xT_done, 1)

                def products(t, r):
                    b = r % 2
                    pe.wait_ge(xT_hi_ready, t + 1)
                    pe.wait_ge(xT_lo_ready, t + 1)
                    ge(pe, wj_ready, t)
                    for part in range(2):
                        if isinstance(t, int) and t == 0:
                            pe.wait_ge(w0_lo_ready, part + 1)
                        chunks = [(c, KC + c) for c in range(2 * part, 2 * part + 2)]
                        ins = product(nc, wj_psum[:], xT[b], w0, chunks, first=part == 0, last=part == 1)
                    ins.then_inc(wj_done, 1)
                    ge(pe, own_ready, t - 1)
                    for part in range(2):
                        if isinstance(t, int) and t == 0:
                            pe.wait_ge(w0_lo_ready, part + 3)
                        chunks = [(c, c) for c in range(2 * part, 2 * part + 2)]
                        ins = product(nc, wi_psum[b][:], xT[b], w0, chunks, first=part == 0, last=part == 1)
                    ins.then_inc(wi_done, 1)
                    pe.wait_ge(wj_ready, t + 1)
                    ge(pe, z_ready, t - 1)
                    nc.tensor.matmul(nb_psum[b][:], adj_T[:], wj[:], start=True, stop=True).then_inc(nb_done, 1)

                pe.wait_ge(consts_set, 8)
                pe.wait_ge(bd_ready, 2)
                nc.tensor.transpose(nb_psum[1][:, 0:P], adj_bd, ident[:]).then_inc(bd_turned, 1)
                turn_x(0, 0)
                pe.wait_ge(adj_T_ready, 1)
                for r in range(UN):
                    turn_x(r + 1, r + 1)
                    products(r, r)
                with pe.Fori(1, T // UN - 1) as g:
                    t = g * UN
                    for r in range(UN):
                        if r < UN - 1:
                            turn_x(t + (r + 1), r + 1)
                        else:
                            turn_x(t + UN, 0)
                        products(t + r, r)
                for r in range(UN):
                    if r < UN - 1:
                        turn_x(T - UN + r + 1, r + 1)
                    products(T - UN + r, r)

        with ExitStack() as ctx:
            def sb(n, shape, dt=F32):
                return ctx.enter_context(nc.sbuf_tensor(n, shape, dt))

            def sem(n):
                return ctx.enter_context(nc.semaphore(n))

            def pb(n, shape):
                return ctx.enter_context(nc.psum_tensor(n, shape, F32))

            xin = sb("xin", [P, D])
            xT = (sb("xT_hi", [P, KC, P], F32R), sb("xT_lo", [P, KC, P], F32R))
            wh = sb("wh", [P, HEADS, D])
            who = sb("who", [P, D])
            ex = [sb(f"ex{b}", [P, D]) for b in range(2)]
            hv = [sb(f"hv{b}", [P, D]) for b in range(2)]
            hT = [(sb(f"hT_hi{b}", [P, KC, P], F32R), sb(f"hT_lo{b}", [P, KC, P], F32R)) for b in range(2)]
            attT = sb("attT", [P, D])
            junk = sb("junk", [P, D])
            ao_row = sb("ao_row", [P, 2, D])
            NV = 2 * HEADS
            v_row = sb("v_row", [P, NV, D])
            TR = KC
            terms = w_first
            whp = [pb(f"whp{b}", [P, D]) for b in range(2)]
            wop = pb("wop", [P, D])
            turn = pb("turn", [P, HEADS, P])
            smallp = pb("smallp", [P, D])
            up = [pb(f"up{b}", [P, D]) for b in range(3)]
            U_HEAD, U_OUT = [0, 1, 2, 0], 1
            SO, SH, ST = NODES, P, 3 * P
            first_sem = sem("first_of_layer1")
            at = Attention(nc, ctx, "ah", HEADS, SLOPE_L1, smallp[:, SH:SH + HEADS * NODES], turn[:],
                           mask=mask1, f_parts=NV)
            ao_ = Attention(nc, ctx, "ao", 1, SLOPE_L1, smallp[:, SO:SO + NODES],
                            smallp[:, ST:ST + P].rearrange("p (h n) -> p h n", h=1), mask=mask1)
            a_loaded, v_diag_ready, v_spread, v_ready, terms_ready = (
                sem("a_loaded"), sem("v_diag_ready"), sem("v_spread"), sem("v_ready"), sem("terms_ready"))
            xin_loaded, xT_done, xT_hi_ready, xT_lo_ready = (
                sem("xin_loaded"), sem("xT_done"), sem("xT_hi_ready"), sem("xT_lo_ready"))
            wh_done, wh_ready, u_done, ex_ready, neg_ready, hv_ready, hT_hi_ready, hT_lo_ready = (
                sem("wh_done"), sem("wh_ready"), sem("u_done"), sem("ex_ready"), sem("neg_ready"),
                sem("hv_ready"), sem("hT_hi_ready"), sem("hT_lo_ready"))
            wo_done, who_ready, fo_part, uo_done, exo_ready, nego_ready, att_ready = (
                sem("wo_done"), sem("who_ready"), sem("fo_part"), sem("uo_done"), sem("exo_ready"),
                sem("nego_ready"), sem("att_ready"))
            layer1_sems = range(first_sem.num, att_ready.num + 1)
            block = ctx.enter_context(nc.Block())

            def run(eng, step):
                step(0, True, False, False)
                step(1, True, True, False)
                step(2, True, True, True)
                with eng.Fori(3, T - 1) as n:
                    step(n, True, True, True)
                step(T - 1, True, True, True)
                step(T, False, True, True)
                step(T + 1, False, False, True)

            @block.sync
            def _(sp):
                sp.dma_start(xin[:], rows(x1_rows, 0)).then_inc(xin_loaded, 16)
                sp.dma_start(ao_row[:], ao.partition_broadcast(P).rearrange("p (k o) -> p k o", o=D)
                             ).then_inc(a_loaded, 16)

                def store(t):
                    sp.wait_ge(att_ready, t + 1)
                    sp.dma_start(rows(att_rows, t), attT[:]).then_inc(att_stored, 16)

                def load(n):
                    multiplied = NV * n
                    sp.wait_ge(terms_ready, multiplied)
                    sp.wait_ge(xT_done, n)
                    sp.dma_start(xin[:], rows(x1_rows, n)).then_inc(xin_loaded, 16)

                for n in range(3):
                    load(n + 1)
                with sp.Fori(3, T - 1) as n:
                    load(n + 1)
                    store(n - 3)
                store(T - 4)
                sp.wait_ge(at.f_ready, NV * T)
                sp.dma_start(w_first[:], chunked(w1)).then_inc(w_first_loaded, 16)
                for t in range(T - 3, T):
                    store(t)
                sp.wait_ge(att_stored, 16 * T)

            @block.gpsimd
            def _(pool):
                nc.gpsimd.sem_clear(layer0_sems)
                at.pool_zero(nc)
                ao_.pool_zero(nc)

                def products_of(t, ks):
                    for k in ks:
                        if isinstance(t, int) and t == 0:
                            pool.wait_ge(v_ready, k + 1)
                        pool.wait_ge(xin_loaded, 16 * t + 16)
                        ge(pool, at.f_ready, NV * t + k - TR + 1)
                        nc.gpsimd.tensor_tensor(terms[:, k % TR, :], xin[:], v_row[:, k, :], ALU.mult
                                                ).then_inc(terms_ready, 1)

                def step(n, heads, sums, outs):
                    more = heads and not (isinstance(n, int) and n == T - 1)
                    if heads:
                        at.pool_diag(nc, pool, n, i64)
                    if more:
                        products_of(n + 1, range(0, 4))
                    if outs:
                        ao_.pool_diag(nc, pool, n - 2, i64)
                    if more:
                        products_of(n + 1, (4,))
                    if outs:
                        ao_.pool_prob(nc, pool, n - 2)
                    if heads:
                        at.pool_prob(nc, pool, n)
                    if more:
                        products_of(n + 1, range(5, NV))

                products_of(0, range(NV))
                run(pool, step)

            @block.scalar
            def _(act):
                def x_hi(t):
                    act.wait_ge(xT_done, t + 1)
                    ge(act, wh_done, 4 * t)
                    nc.scalar.copy(xT[0][:], turn[:]).then_inc(xT_hi_ready, 1)

                def dots(t, ks):
                    for k in ks:
                        if k == 0:
                            ge(act, at.diag_ready, t)
                        if k == HEADS:
                            ge(act, at.summed, t)
                        act.wait_ge(terms_ready, NV * t + k + 1)
                        nc.scalar.activation(terms[:, k % TR, :], terms[:, k % TR, :], ACT.Identity,
                                             accum_out=at.f[:, k:k + 1]).then_inc(at.f_ready, 1)

                def head(n, h, heads, sums, between=None):
                    if sums:
                        k = 4 * (n - 1) + h
                        act.wait_ge(u_done, k + 1)
                        ge(act, hv_ready, k - 1)
                        nc.scalar.activation(ex[h % 2][:], up[U_HEAD[h]][:], ACT.Exp).then_inc(ex_ready, 1)
                    if between is not None:
                        between()
                    if heads:
                        act.wait_ge(wh_done, 4 * n + h + 1)
                        ge(act, u_done, 4 * (n - 1) + h + 1)
                        nc.scalar.copy(wh[:, h, :], whp[h % 2][:]).then_inc(wh_ready, 1)
                    if sums:
                        act.wait_ge(hv_ready, k + 1)
                        ge(act, wo_done, k - 1)
                        nc.scalar.copy(hT[h % 2][0][:].rearrange("p c n -> p (c n)"), hv[h % 2][:]
                                       ).then_inc(hT_hi_ready, 1)

                def step(n, heads, sums, outs):
                    more = heads and not (isinstance(n, int) and n == T - 1)
                    head(n, 0, heads, sums, between=lambda: dots(n, range(HEADS, NV)) if heads else None)
                    if outs:
                        act.wait_ge(wo_done, 4 * (n - 1))
                        ge(act, uo_done, n - 2)
                        ge(act, ao_.f_ready, n - 2)
                        nc.scalar.copy(who[:], wop[:]).then_inc(who_ready, 1)
                    if more:
                        dots(n + 1, (0,))
                    head(n, 1, heads, sums)
                    if more:
                        dots(n + 1, (1,))
                    if heads:
                        at.act_exp(nc, act, n)
                    head(n, 2, heads, sums, between=lambda: ao_.act_exp(nc, act, n - 2) if outs else None)
                    if more:
                        dots(n + 1, (2,))
                    head(n, 3, heads, sums)
                    if outs:
                        ge(act, uo_done, n - 2)
                        ao_.act_turned(nc, act, n - 2)
                    if heads and not (isinstance(n, int) and n == T - 1):
                        x_hi(n + 1)
                        dots(n + 1, (3,))
                    if heads:
                        ge(act, u_done, 4 * n)
                        at.act_turned(nc, act, n)
                    if outs:
                        act.wait_ge(uo_done, n - 1)
                        ge(act, att_ready, n - 2)
                        act.wait_ge(ao_.f_ready, n - 1)
                        nc.scalar.activation(junk[:], up[U_OUT][:], ACT.Exp).then_inc(exo_ready, 1)

                x_hi(0)
                for k in range(NV):
                    act.wait_ge(v_spread, k + 1)
                    nc.scalar.copy(v_row[:, k, :], up[k % 2][:]).then_inc(v_ready, 1)
                    if 0 < k <= HEADS:
                        dots(0, (k - 1,))
                run(act, step)

            @block.vector
            def _(dve):
                for k in range(NV):
                    h, half = k % HEADS, 1 - k // HEADS
                    ge(dve, v_spread, k - 1)
                    nc.vector.tensor_tensor(hv[k % 2][:].rearrange("p (c n) -> p c n", c=KC),
                                            ident[:, None, :].to_broadcast([P, KC, P]),
                                            v_cols[:, h * KC:(h + 1) * KC, half:half + 1]
                                            .to_broadcast([P, KC, P]), ALU.mult).then_inc(v_diag_ready, 1)
                dve.wait_ge(a_loaded, 16)

                def x_lo(t):
                    dve.wait_ge(xT_hi_ready, t + 1)
                    nc.vector.tensor_tensor(xT[1][:], turn[:], xT[0][:].bitcast(F32), ALU.subtract
                                            ).then_inc(xT_lo_ready, 1)

                def negative(k, h):
                    dve.wait_ge(ex_ready, k + 1)
                    nc.vector.tensor_scalar(ex[h % 2][:], ex[h % 2][:], 1.0, -1.0, ALU.min, ALU.add
                                            ).then_inc(neg_ready, 1)
                    dve.wait_ge(neg_ready, k + 1)
                    ge(dve, hT_lo_ready, k - 1)
                    nc.vector.tensor_tensor(hv[h % 2][:], up[U_HEAD[h]][:], ex[h % 2][:], ALU.max
                                            ).then_inc(hv_ready, 1)

                def low(k, h):
                    dve.wait_ge(hT_hi_ready, k + 1)
                    nc.vector.tensor_tensor(hT[h % 2][1][:].rearrange("p c n -> p (c n)"), hv[h % 2][:],
                                            hT[h % 2][0][:].bitcast(F32).rearrange("p c n -> p (c n)"),
                                            ALU.subtract).then_inc(hT_lo_ready, 1)

                def step(n, heads, sums, outs):
                    k = 4 * (n - 1)
                    if sums:
                        negative(k, 0)
                        low(k, 0)
                    if outs:
                        dve.wait_ge(who_ready, n - 1)
                        ge(dve, ao_.diag_ready, n - 2)
                        ge(dve, ao_.summed, n - 2)
                        ge(dve, att_ready, n - 2)
                        nc.vector.tensor_tensor_reduce(
                            out=junk[:], in0=who[:], in1=ao_row[:, 0, :], scale=1.0, scalar=0.0,
                            op0=ALU.mult, op1=ALU.add, accum_out=ao_.f[:, 1:2]).then_inc(fo_part, 1)
                        dve.wait_ge(fo_part, n - 1)
                        nc.vector.tensor_tensor_reduce(
                            out=junk[:], in0=who[:], in1=ao_row[:, 1, :], scale=1.0, scalar=0.0,
                            op0=ALU.mult, op1=ALU.add, accum_out=ao_.f[:, 0:1]).then_inc(ao_.f_ready, 1)
                    if heads:
                        at.dve_before_exp(nc, dve, n, fill1)
                    if sums:
                        negative(k + 1, 1)
                        low(k + 1, 1)
                    if outs:
                        ao_.dve_before_exp(nc, dve, n - 2, fill1)
                    if heads:
                        at.dve_after_exp(nc, dve, n)
                    if sums:
                        negative(k + 2, 2)
                    if outs:
                        ao_.dve_after_exp(nc, dve, n - 2)
                    if sums:
                        low(k + 2, 2)
                        negative(k + 3, 3)
                        low(k + 3, 3)
                    if heads and not (isinstance(n, int) and n == T - 1):
                        x_lo(n + 1)
                    if outs:
                        dve.wait_ge(exo_ready, n - 1)
                        nc.vector.tensor_scalar(junk[:], junk[:], 1.0, -1.0, ALU.min, ALU.add
                                                ).then_inc(nego_ready, 1)
                        dve.wait_ge(nego_ready, n - 1)
                        ge(dve, att_stored, 16 * (n - 2))
                        nc.vector.tensor_tensor(attT[:], up[U_OUT][:], junk[:], ALU.max
                                                ).then_inc(att_ready, 1)

                x_lo(0)
                run(dve, step)

            @block.tensor
            def _(pe):
                def turn_x(t):
                    pe.wait_ge(xin_loaded, 16 * t + 16)
                    ge(pe, at.turned_ready, 2 * (t - 1))
                    for c in range(KC):
                        ins = nc.tensor.transpose(turn[:, c, :], xin[:, c * P:(c + 1) * P], ident[:])
                    ins.then_inc(xT_done, 1)

                def sums_of(m, h):
                    k = 4 * m + h
                    pe.wait_ge(wh_ready, k + 1)
                    if h == 1:
                        ge(pe, att_ready, m - 1)
                    else:
                        ge(pe, hv_ready, {0: k, 2: k - 3, 3: k - 2}[h])
                    for c in range(KC):
                        ins = nc.tensor.matmul(up[U_HEAD[h]][:, c * P:(c + 1) * P],
                                               wh[:, h, c * P:(c + 1) * P], at.turned[:, h, :],
                                               start=True, stop=True)
                    ins.then_inc(u_done, 1)

                def project(n, h):
                    ge(pe, wh_ready, 4 * n + h - 1)
                    product(nc, whp[h % 2][:], xT, (big_hi, big_lo),
                            [(c, h * KC + c) for c in range(KC)]).then_inc(wh_done, 1)

                def out_part(k, h):
                    pe.wait_ge(hT_lo_ready, k + 1)
                    pe.wait_ge(hT_hi_ready, k + 1)
                    product(nc, wop[:], hT[h % 2], (big_hi, big_lo),
                            [(c, (HEADS + h) * KC + c) for c in range(KC)],
                            first=h == 0, last=h == HEADS - 1).then_inc(wo_done, 1)

                def step(n, heads, sums, outs):
                    k = 4 * (n - 1)
                    if heads:
                        pe.wait_ge(xT_hi_ready, n + 1)
                        pe.wait_ge(xT_lo_ready, n + 1)
                    for h in range(HEADS):
                        if sums:
                            if h == 0:
                                pe.wait_ge(at.turned_ready, 2 * n)
                            sums_of(n - 1, h)
                        if heads:
                            project(n, h)
                        if heads and h == 3 and not (isinstance(n, int) and n == T - 1):
                            turn_x(n + 1)
                        if h == 0:
                            if outs:
                                out_part(k - 1, 3)
                            if heads:
                                ge(pe, ao_.turned_ready, 2 * (n - 2))
                                at.pe_scores(nc, pe, n, same_graph)
                        else:
                            if sums:
                                if h == 1:
                                    ge(pe, who_ready, n - 1)
                                out_part(k + h - 1, h - 1)
                            if outs and h == 1:
                                ge(pe, at.summed, n + 1 if heads else T)
                                ao_.pe_scores(nc, pe, n - 2, same_graph)
                            if outs and h == 2:
                                pe.wait_ge(ao_.summed, n - 1)
                                ao_.pe_turn(nc, pe, n - 2, ident)
                    if heads:
                        if not (isinstance(n, int) and n == T - 1):
                            pe.wait_ge(xT_lo_ready, n + 2)
                        at.pe_turn(nc, pe, n, ident)
                    if outs:
                        pe.wait_ge(ao_.turned_ready, 2 * (n - 1))
                        if sums:
                            pe.wait_ge(hv_ready, k + 2)
                        for c in range(KC):
                            ins = nc.tensor.matmul(up[U_OUT][:, c * P:(c + 1) * P], who[:, c * P:(c + 1) * P],
                                                   ao_.turned[:, 0, :], start=True, stop=True)
                        ins.then_inc(uo_done, 1)

                turn_x(0)
                for k in range(NV):
                    pe.wait_ge(v_diag_ready, k + 1)
                    ge(pe, v_ready, k - 1)
                    nc.tensor.matmul(up[k % 2][:], ones[:], hv[k % 2][:], start=True, stop=True
                                     ).then_inc(v_spread, 1)
                run(pe, step)

        with nc.Block() as block:
            @block.gpsimd
            def _(pool):
                nc.gpsimd.sem_clear(layer1_sems)

        held.close()
        with ExitStack() as ctx:
            def sb(n, shape, dt=F32):
                return ctx.enter_context(nc.sbuf_tensor(n, shape, dt))

            def sem(n):
                return ctx.enter_context(nc.semaphore(n))

            def pb(n, shape):
                return ctx.enter_context(nc.psum_tensor(n, shape, F32))

            R = 4
            w_hi = sb("w_hi", [P, 4 * KC, D], F32R)
            w_lo = sb("w_lo", [P, 4 * KC, D], F32R)
            stage = [w_first, sb("w_second", [P, KC, D])]
            att = [sb(f"att{b}", [P, D]) for b in range(2)]
            attS = [(sb(f"att_hi{b}", [P, KC, P], F32R), sb(f"att_lo{b}", [P, KC, P], F32R)) for b in range(2)]
            h1 = sb("h1", [P, D])
            h1T = (sb("h1T_hi", [P, KC, P], F32R), sb("h1T_lo", [P, KC, P], F32R))
            x1 = [sb(f"x1r{b}", [P, D]) for b in range(2)]
            x1b = sb("x1b", [P, D])
            att_b2 = sb("att_b2", [P, D])
            y = sb("y", [P, D])
            z1 = sb("z1", [P, D])
            x2 = [sb(f"x2_{r}", [P, D]) for r in range(R)]
            x3 = [sb(f"x3_{b}", [P, D]) for b in range(2)]
            res = sb("res", [P, D])
            b1_row, b2_row, gamma_row, beta_row = (sb("b1_row", [P, D]), sb("b2_row", [P, D]),
                                                   sb("gamma_row", [P, D]), sb("beta_row", [P, D]))
            diag_v = [sb(f"diag_v{k}", [P, KC, P]) for k in range(2)]
            bank_a, bank_b = pb("bank_a", [P, D]), pb("bank_b", [P, D])
            turn_h, turn_2, turn_3 = (pb("turn_h", [P, KC, P]), pb("turn_2", [P, KC, P]),
                                      pb("turn_3", [P, KC, P]))
            smallp = pb("smallq", [P, D])
            n_y, n_1 = Norm(nc, ctx, "ny"), Norm(nc, ctx, "n1", shifted=True)

            class Gat:

                def __init__(self, name, q, base, tp):
                    self.q, self.turn = q, tp
                    self.att = Attention(nc, ctx, name, 1, SLOPE_L23, smallp[:, base:base + NODES],
                                         smallp[:, base + NODES:base + NODES + P]
                                         .rearrange("p (h n) -> p h n", h=1))
                    self.v_row = sb(name + "_v_row", [P, 2, D])
                    self.terms = sb(name + "_terms", [P, 2, D])
                    self.xT = (sb(name + "_xT_hi", [P, KC, P], F32R), sb(name + "_xT_lo", [P, KC, P], F32R))
                    self.wh = sb(name + "_wh", [P, D])
                    self.z = sb(name + "_z", [P, D])
                    self.sums = pb(name + "_sums", [P, D])
                    self.norm = Norm(nc, ctx, name + "_n", shifted=True)
                    self.xT_done, self.xT_hi_ready, self.xT_lo_ready = (
                        sem(name + "_xT_done"), sem(name + "_xT_hi_ready"), sem(name + "_xT_lo_ready"))
                    self.wh_done, self.wh_ready, self.sums_done, self.z_ready, self.x_ready = (
                        sem(name + "_wh_done"), sem(name + "_wh_ready"), sem(name + "_sums_done"),
                        sem(name + "_z_ready"), sem(name + "_x_ready"))
                    self.diag_v_ready, self.v_spread, self.v_ready, self.terms_ready = (
                        sem(name + "_diag_v_ready"), sem(name + "_v_spread"), sem(name + "_v_ready"),
                        sem(name + "_terms_ready"))

            g2 = Gat("g2", 2 * KC, 0, turn_2)
            g3 = Gat("g3", 3 * KC, 2 * P, turn_3)
            weights = (w1, w2, W2, W3)
            w_loaded = [sem(f"w_loaded{b}") for b in range(2)]
            w_hi_parts, w_lo_parts, rows_loaded = sem("w_hi_parts"), sem("w_lo_parts"), sem("rows_loaded")
            att_loaded = [sem(f"att_loaded{b}") for b in range(2)]
            x1_loaded = [sem(f"x1_loaded{b}") for b in range(2)]
            att_hi_ready, att_lo_ready, h1_done, h1_ready, h1T_done, h1T_hi_ready, h1T_lo_ready = (
                sem("att_hi_ready"), sem("att_lo_ready"), sem("h1_done"), sem("h1_ready"), sem("h1T_done"),
                sem("h1T_hi_ready"), sem("h1T_lo_ready"))
            y_done, scaled, x1b_ready, z1_ready, x2_ready = (
                sem("y_done"), sem("scaled"), sem("x1b_ready"), sem("z1_ready"), sem("x2_ready"))
            att_turned, att_b2_ready, y_ready = sem("att_turned"), sem("att_b2_ready"), sem("y_ready")
            res_stored = sem("res_stored")
            block = ctx.enter_context(nc.Block())

            def run(eng, step, ahead=0, behind=None):
                stop = T // R - (1 if ahead else 0)
                for n in range(2 * R):
                    step(n, n % R)
                    if behind is not None and n < 2:
                        behind((g2, g3)[n], n + 2)
                with eng.Fori(2, stop) as g:
                    n = g * R
                    for r in range(R):
                        step(n + r, r)
                for n in range(stop * R, T + 4):
                    step(n, n % R)

            def live(n, lag):
                return not isinstance(n, int) or 0 <= n - lag < T

            def pair(t, r):
                return 16 * (t // 2 + 1) if isinstance(t, int) else 8 * (t - r % 2) + 16

            @block.sync
            def _(sp):
                sp.dma_start(att[0][:], rows(att_rows, 0)).then_inc(att_loaded[0], 16)
                for k, w in enumerate(weights):
                    ge(sp, w_lo_parts, KC * (k - 1))
                    if k > 0:
                        sp.dma_start(stage[k % 2][:], chunked(w)).then_inc(w_loaded[k % 2], 16)
                    if k == 1:
                        sp.dma_start(x1[0][:], rows(x1_rows, 0)).then_inc(x1_loaded[0], 16)
                        sp.dma_start(att[1][:], rows(att_rows, 1)).then_inc(att_loaded[1], 16)
                        sp.dma_start(x1[1][:], rows(x1_rows, 1)).then_inc(x1_loaded[1], 16)
                        for row, src in ((b1_row, b1), (b2_row, b2), (gamma_row, gamma), (beta_row, beta)):
                            sp.dma_start(row[:], src.partition_broadcast(P)).then_inc(rows_loaded, 16)

                def step(n, r):
                    if live(n, 4):
                        sp.wait_ge(g3.x_ready, n - 3)
                        sp.dma_start(rows(out_rows, n - 4), res[:]).then_inc(res_stored, 16)
                    if live(n, 0) and live(n, -2):
                        sp.wait_ge(att_lo_ready, n + 1)
                        sp.wait_ge(att_turned, n + 1)
                        sp.dma_start(att[r % 2][:], rows(att_rows, n + 2)).then_inc(att_loaded[r % 2], 16)
                        sp.wait_ge(x1b_ready, n + 1)
                        sp.dma_start(x1[r % 2][:], rows(x1_rows, n + 2)).then_inc(x1_loaded[r % 2], 16)

                run(sp, step, ahead=2)
                sp.wait_ge(res_stored, 16 * T)

            @block.gpsimd
            def _(pool):
                g2.att.pool_zero(nc)
                g3.att.pool_zero(nc)

                def att_lo(t, r):
                    pool.wait_ge(att_hi_ready, t + 1)
                    nc.gpsimd.tensor_tensor(attS[r % 2][1][:].rearrange("p c n -> p (c n)"), att[r % 2][:],
                                            attS[r % 2][0][:].bitcast(F32).rearrange("p c n -> p (c n)"),
                                            ALU.subtract).then_inc(att_lo_ready, 1)

                def terms(g, t, k, x, ready):
                    if isinstance(t, int) and t == 0:
                        pool.wait_ge(g.v_ready, 2)
                    pool.wait_ge(ready, t + 1)
                    ge(pool, g.att.f_ready, 2 * t + k - 1)
                    nc.gpsimd.tensor_tensor(g.terms[:, k, :], x, g.v_row[:, k, :], ALU.mult
                                            ).then_inc(g.terms_ready, 1)

                def diag(g, t):
                    pool.wait_ge(g.att.f_ready, 2 * t + 1)
                    ge(pool, g.att.scores_done, t)
                    nc.gpsimd.tensor_tensor(g.att.diag[:, 0, :], i64[:],
                                            g.att.f[:, 0:1].to_broadcast([P, NODES]), ALU.mult
                                            ).then_inc(g.att.diag_ready, 1)

                def step(n, r):
                    if live(n, 1):
                        n_y.pool_rstd(nc, pool, n - 1, z1_ready, norm_consts)
                    if live(n, 3):
                        g2.norm.pool_rstd(nc, pool, n - 3, g2.x_ready, norm_consts)
                    if live(n, 1):
                        n_1.pool_rstd(nc, pool, n - 1, x2_ready, norm_consts)
                    if live(n, 3):
                        for k in range(2):
                            terms(g3, n - 3, k, x3[(r - 3) % 2][:], g2.x_ready)
                    if live(n, 2):
                        g2.att.pool_prob(nc, pool, n - 2, gate)
                    if live(n, 1):
                        terms(g2, n - 1, 0, x2[(r - 1) % R][:], x2_ready)
                    if live(n, 3):
                        diag(g3, n - 3)
                    if live(n, 1):
                        terms(g2, n - 1, 1, x2[(r - 1) % R][:], x2_ready)
                    if live(n, 4):
                        g3.norm.pool_rstd(nc, pool, n - 4, g3.x_ready, norm_consts)
                    if live(n, -1):
                        att_lo(n + 1, (r + 1) % R)
                    if live(n, 3):
                        g3.att.pool_prob(nc, pool, n - 3, gate)
                    if live(n, 1):
                        diag(g2, n - 1)
                    if live(n, 0):
                        if isinstance(n, int) and n == 0:
                            pool.wait_ge(rows_loaded, 64)
                        pool.wait_ge(x1_loaded[r % 2], pair(n, r))
                        ge(pool, z1_ready, n)
                        nc.gpsimd.tensor_tensor(x1b[:], x1[r % 2][:], beta_row[:], ALU.add
                                                ).then_inc(x1b_ready, 1)

                att_lo(0, 0)
                run(pool, step, ahead=1)

            @block.scalar
            def _(act):
                def att_hi(t, r):
                    act.wait_ge(att_loaded[r % 2], pair(t, r))
                    ge(act, h1_done, t - 1)
                    nc.scalar.copy(attS[r % 2][0][:].rearrange("p c n -> p (c n)"), att[r % 2][:]
                                   ).then_inc(att_hi_ready, 1)

                def x_hi(g, t):
                    act.wait_ge(g.xT_done, t + 1)
                    ge(act, g.wh_done, t)
                    nc.scalar.copy(g.xT[0][:], g.turn[:]).then_inc(g.xT_hi_ready, 1)

                def wh_out(g, t):
                    act.wait_ge(g.wh_done, t + 1)
                    ge(act, g.sums_done, t)
                    nc.scalar.copy(g.wh[:], bank_a[:]).then_inc(g.wh_ready, 1)

                def turned(g, t):
                    ge(act, g.sums_done, t)
                    g.att.act_turned(nc, act, t)

                def dots(g, t):
                    ge(act, g.att.summed, t)
                    ge(act, g.att.diag_ready, t)
                    for k in range(2):
                        act.wait_ge(g.terms_ready, 2 * t + k + 1)
                        nc.scalar.activation(g.terms[:, k, :], g.terms[:, k, :], ACT.Identity,
                                             accum_out=g.att.f[:, k:k + 1]).then_inc(g.att.f_ready, 1)

                def normalise(norm, t, z, x, ready):
                    act.wait_ge(norm.shift_ready, t + 1)
                    nc.scalar.activation(x, z, ACT.Identity, scale=norm.rstd[:], bias=norm.shift[:]
                                         ).then_inc(ready, 1)

                def step(n, r):
                    if live(n, 4):
                        turned(g3, n - 4)
                    if live(n, -1):
                        att_hi(n + 1, (r + 1) % R)
                    if live(n, 2):
                        wh_out(g2, n - 2)
                    if live(n, 3):
                        ge(act, g3.z_ready, n - 4)
                        normalise(g2.norm, n - 3, g2.z[:], x3[(r - 3) % 2][:], g2.x_ready)
                    if live(n, 2):
                        g2.att.act_exp(nc, act, n - 2)
                    if live(n, 1):
                        ge(act, g2.z_ready, n - 4)
                        normalise(n_1, n - 1, z1[:], x2[(r - 1) % R][:], x2_ready)
                    if live(n, 3):
                        x_hi(g3, n - 3)
                    if live(n, 0):
                        act.wait_ge(h1T_done, n + 1)
                        ge(act, y_done, n)
                        nc.scalar.activation(h1T[0][:], turn_h[:], ACT.Relu).then_inc(h1T_hi_ready, 1)
                    if live(n, 3):
                        dots(g3, n - 3)
                    if live(n, 1):
                        x_hi(g2, n - 1)
                    if live(n, 3):
                        wh_out(g3, n - 3)
                    if live(n, 3):
                        g3.att.act_exp(nc, act, n - 3)
                    if live(n, 2):
                        turned(g2, n - 2)
                    if live(n, 1):
                        dots(g2, n - 1)
                    if live(n, 4):
                        ge(act, res_stored, 16 * (n - 4))
                        normalise(g3.norm, n - 4, g3.z[:], res[:], g3.x_ready)

                def weights_hi(k):
                    if k == 0:
                        act.wait_ge(w_first_loaded, 16)
                    else:
                        act.wait_ge(w_loaded[k % 2], 16 * ((k + 1) // 2))
                    for c in range(KC):
                        nc.scalar.copy(w_hi[:, k * KC + c, :], stage[k % 2][:, c, :]).then_inc(w_hi_parts, 1)

                def behind(g, k):
                    weights_hi(k)
                    for s in range(2):
                        act.wait_ge(g.v_spread, s + 1)
                        nc.scalar.copy(g.v_row[:, s, :], g.sums[:]).then_inc(g.v_ready, 1)

                weights_hi(0)
                att_hi(0, 0)
                weights_hi(1)
                run(act, step, ahead=1, behind=behind)

            @block.vector
            def _(dve):
                def weights_lo(k):
                    for c in range(KC):
                        dve.wait_ge(w_hi_parts, k * KC + c + 1)
                        nc.vector.tensor_tensor(w_lo[:, k * KC + c, :], stage[k % 2][:, c, :],
                                                w_hi[:, k * KC + c, :].bitcast(F32), ALU.subtract
                                                ).then_inc(w_lo_parts, 1)

                def behind(g, k):
                    for s in range(2):
                        if k == 3:
                            dve.wait_ge(g2.v_spread, s + 1)
                        first = (HEADS + k - 2) * KC
                        nc.vector.tensor_tensor(diag_v[s][:], ident[:, None, :].to_broadcast([P, KC, P]),
                                                v_cols[:, first:first + KC, s:s + 1]
                                                .to_broadcast([P, KC, P]), ALU.mult
                                                ).then_inc(g.diag_v_ready, 1)
                    weights_lo(k)

                def x_lo(g, t):
                    dve.wait_ge(g.xT_hi_ready, t + 1)
                    nc.vector.tensor_tensor(g.xT[1][:], g.turn[:], g.xT[0][:].bitcast(F32), ALU.subtract
                                            ).then_inc(g.xT_lo_ready, 1)

                def scores(g, t):
                    a = g.att
                    dve.wait_ge(a.scores_done, t + 1)
                    dve.wait_ge(a.f_ready, 2 * t + 2)
                    nc.vector.scalar_tensor_tensor(a.e1[:, 0, :], a.scores_psum, a.f[:, 1:2], bias23[:],
                                                   ALU.add, ALU.add).then_inc(a.summed, 1)

                def leaky(g, t):
                    a = g.att
                    dve.wait_ge(a.summed, t + 1)
                    ge(dve, a.exp_ready, t)
                    nc.vector.scalar_tensor_tensor(a.e2[:], a.e1[:], SLOPE_L23, a.e1[:], ALU.mult, ALU.max
                                                   ).then_inc(a.leaky, 1)

                def peak(g, t):
                    dve.wait_ge(g.att.leaky, t + 1)
                    nc.vector.tensor_reduce(g.att.peak[:], g.att.e2[:], AX_X, ALU.max, negate=True
                                            ).then_inc(g.att.peaked, 1)

                def residual(g, t, x):
                    dve.wait_ge(g.sums_done, t + 1)
                    ge(dve, g.x_ready, t)
                    nc.vector.tensor_tensor(g.z[:], g.sums[:], x, ALU.add).then_inc(g.z_ready, 1)

                def stats(g, t):
                    dve.wait_ge(g.z_ready, t + 1)
                    g.norm.dve_stats(nc, dve, t, g.z[:])

                def step(n, r):
                    if live(n, 1):
                        dve.wait_ge(y_done, n)
                        ge(dve, z1_ready, n - 1)
                        dve.wait_ge(att_b2_ready, n)
                        nc.vector.tensor_tensor(y[:], bank_b[:], att_b2[:], ALU.add).then_inc(y_ready, 1)
                    if live(n, 3):
                        residual(g2, n - 3, x2[(r - 3) % R][:])
                    if live(n, 1):
                        dve.wait_ge(y_ready, n)
                        n_y.dve_stats(nc, dve, n - 1, y[:])
                    if live(n, 3):
                        stats(g2, n - 3)
                    if live(n, 1):
                        n_y.dve_mean(nc, dve, n - 1, scaled)
                    if live(n, 3):
                        g2.norm.dve_mean(nc, dve, n - 3, g2.x_ready)
                    if live(n, 1):
                        dve.wait_ge(n_y.mv_ready, n)
                        nc.vector.scalar_tensor_tensor(y[:], y[:], n_y.mv[:, 0:1], gamma_row[:],
                                                       ALU.subtract, ALU.mult).then_inc(scaled, 1)
                    if live(n, 1):
                        dve.wait_ge(scaled, n)
                        dve.wait_ge(n_y.rstd_ready, n)
                        dve.wait_ge(x1b_ready, n)
                        ge(dve, x2_ready, n - 1)
                        nc.vector.scalar_tensor_tensor(z1[:], y[:], n_y.rstd[:], x1b[:], ALU.mult, ALU.add
                                                       ).then_inc(z1_ready, 1)
                    if live(n, 2):
                        scores(g2, n - 2)
                    if live(n, 1):
                        dve.wait_ge(z1_ready, n)
                        n_1.dve_stats(nc, dve, n - 1, z1[:])
                    if live(n, 2):
                        leaky(g2, n - 2)
                    if live(n, 1):
                        n_1.dve_mean(nc, dve, n - 1, x2_ready)
                    if live(n, 2):
                        peak(g2, n - 2)
                    if live(n, 0):
                        dve.wait_ge(att_turned, n + 1)
                        ge(dve, y_ready, n)
                        nc.vector.tensor_tensor(att_b2[:], turn_h[:].rearrange("p c n -> p (c n)"), b2_row[:],
                                                ALU.add).then_inc(att_b2_ready, 1)
                    if live(n, 2):
                        g2.att.dve_after_exp(nc, dve, n - 2, gate)
                    if live(n, 0):
                        dve.wait_ge(h1_done, n + 1)
                        ge(dve, h1T_done, n)
                        nc.vector.tensor_tensor(h1[:], bank_b[:], b1_row[:], ALU.add).then_inc(h1_ready, 1)
                    if live(n, 3):
                        x_lo(g3, n - 3)
                    if live(n, 4):
                        residual(g3, n - 4, x3[r % 2][:])
                    if live(n, 0):
                        dve.wait_ge(h1T_hi_ready, n + 1)
                        nc.vector.scalar_tensor_tensor(h1T[1][:], turn_h[:], 0.0, h1T[0][:].bitcast(F32),
                                                       ALU.max, ALU.subtract).then_inc(h1T_lo_ready, 1)
                    if live(n, 4):
                        stats(g3, n - 4)
                    if live(n, 1):
                        x_lo(g2, n - 1)
                    if live(n, 4):
                        g3.norm.dve_mean(nc, dve, n - 4, g3.x_ready)
                    if live(n, 3):
                        scores(g3, n - 3)
                        leaky(g3, n - 3)
                    if live(n, 3):
                        peak(g3, n - 3)
                        g3.att.dve_after_exp(nc, dve, n - 3, gate)

                weights_lo(0)
                weights_lo(1)
                dve.wait_ge(rows_loaded, 64)
                run(dve, step, behind=behind)

            @block.tensor
            def _(pe):
                def turn_x(g, t, x, ready):
                    pe.wait_ge(ready, t + 1)
                    ge(pe, g.xT_lo_ready, t)
                    for c in range(KC):
                        ins = nc.tensor.transpose(g.turn[:, c, :], x[:, c * P:(c + 1) * P], ident[:])
                    ins.then_inc(g.xT_done, 1)

                def project(g, t):
                    pe.wait_ge(g.xT_lo_ready, t + 1)
                    if isinstance(t, int) and t == 0:
                        pe.wait_ge(w_lo_parts, g.q + KC)
                    product(nc, bank_a[:], g.xT, (w_hi, w_lo),
                            [(c, g.q + c) for c in range(KC)]).then_inc(g.wh_done, 1)

                def spread(g, t):
                    pe.wait_ge(g.att.diag_ready, t + 1)
                    nc.tensor.matmul(g.att.scores_psum, same_graph[:], g.att.diag[:, 0, :],
                                     start=True, stop=True).then_inc(g.att.scores_done, 1)

                def sums(g, t):
                    pe.wait_ge(g.att.turned_ready, 2 * t + 2)
                    pe.wait_ge(g.wh_ready, t + 1)
                    ge(pe, g.z_ready, t)
                    if isinstance(t, int) and t == 0:
                        pe.wait_ge(g.v_ready, 2)
                    nc.tensor.matmul(g.sums[:], g.att.turned[:, 0, :], g.wh[:], start=True, stop=True
                                     ).then_inc(g.sums_done, 1)

                def step(n, r):
                    if live(n, 4):
                        if live(n, 3):
                            pe.wait_ge(g2.att.turned_ready, 2 * (n - 2))
                        g3.att.pe_turn(nc, pe, n - 4, ident)
                    if live(n, 2):
                        ge(pe, g3.wh_ready, n - 3)
                        project(g2, n - 2)
                        if live(n, 4):
                            pe.wait_ge(g3.att.turned_ready, 2 * (n - 3))
                        elif live(n, 3):
                            pe.wait_ge(g2.att.turned_ready, 2 * (n - 2))
                        spread(g2, n - 2)
                    if live(n, 0):
                        pe.wait_ge(att_loaded[r % 2], pair(n, r))
                        ge(pe, h1T_lo_ready, n)
                        for c in range(KC):
                            ins = nc.tensor.transpose(turn_h[:, c, :], att[r % 2][:, c * P:(c + 1) * P], ident[:])
                        ins.then_inc(att_turned, 1)
                        pe.wait_ge(att_lo_ready, n + 1)
                        ge(pe, y_ready, n)
                        product(nc, bank_b[:], attS[r % 2], (w_hi, w_lo), [(c, c) for c in range(KC)]
                                ).then_inc(h1_done, 1)
                    if live(n, 3):
                        turn_x(g3, n - 3, x3[(r - 3) % 2], g2.x_ready)
                    if live(n, 4):
                        sums(g3, n - 4)
                    if live(n, 0):
                        pe.wait_ge(h1_ready, n + 1)
                        pe.wait_ge(att_b2_ready, n + 1)
                        for c in range(KC):
                            ins = nc.tensor.transpose(turn_h[:, c, :], h1[:, c * P:(c + 1) * P], ident[:])
                        ins.then_inc(h1T_done, 1)
                    if live(n, 1):
                        turn_x(g2, n - 1, x2[(r - 1) % R], x2_ready)
                    if live(n, 3):
                        ge(pe, g2.wh_ready, capped(n - 1, T))
                        project(g3, n - 3)
                        if live(n, 2):
                            pe.wait_ge(g2.att.summed, n - 1)
                        elif live(n, 4):
                            pe.wait_ge(g3.att.turned_ready, 2 * (n - 3))
                        spread(g3, n - 3)
                    if live(n, 0):
                        pe.wait_ge(h1T_lo_ready, n + 1)
                        if isinstance(n, int) and n == 0:
                            pe.wait_ge(w_lo_parts, 2 * KC)
                        product(nc, bank_b[:], h1T, (w_hi, w_lo), [(c, KC + c) for c in range(2)], last=False)
                    if live(n, 2):
                        if live(n, 3):
                            pe.wait_ge(g3.att.summed, n - 2)
                        g2.att.pe_turn(nc, pe, n - 2, ident)
                    if live(n, 0):
                        product(nc, bank_b[:], h1T, (w_hi, w_lo), [(c, KC + c) for c in range(2, KC)], first=False
                                ).then_inc(y_done, 1)
                    if live(n, 2):
                        sums(g2, n - 2)

                def behind(g, k):
                    for s in range(2):
                        pe.wait_ge(g.diag_v_ready, s + 1)
                        ge(pe, g.v_ready, s)
                        nc.tensor.matmul(g.sums[:], ones[:], diag_v[s][:].rearrange("p c n -> p (c n)"),
                                         start=True, stop=True).then_inc(g.v_spread, 1)

                pe.wait_ge(w_lo_parts, KC)
                run(pe, step, behind=behind)


_INS = ['x', 'adj', 'L0_gnn_W', 'L0_gnn_b', 'L1_gnn_W_heads', 'L1_gnn_a_heads', 'L1_gnn_W_out', 'L1_gnn_a_out',
        'L1_gnn_w1', 'L1_gnn_b1', 'L1_gnn_w2', 'L1_gnn_b2', 'L1_gnn_ln_gamma', 'L1_gnn_ln_beta',
        'L2_gnn_W', 'L2_gnn_a_src', 'L2_gnn_a_dst', 'L3_gnn_W', 'L3_gnn_a_src', 'L3_gnn_a_dst']


def kernel(**inputs):
    import numpy as _np
    import concourse.bacc as _bacc
    from concourse import mybir as _mybir
    from concourse.bass_utils import run_bass_kernel_spmd as _run

    nc = _bacc.Bacc("TRN2", target_bir_lowering=False, num_devices=1)
    arrays, args = {}, []
    for name in _INS:
        a = _np.asarray(inputs[name])
        if name == 'L0_gnn_W':
            a = a.T
        a = _np.ascontiguousarray(a)
        arrays[f"in_{name}"] = a
        args.append(nc.dram_tensor(f"in_{name}", a.shape, _mybir.dt.from_np(a.dtype), kind="ExternalInput").ap())
    shape = inputs['x'].shape
    out = nc.dram_tensor("out_0", shape, _mybir.dt.float32, kind="ExternalOutput").ap()
    gnn_stack_kernel(nc, *args, out)
    r = _run(nc, [arrays], core_ids=[0])
    return r.results[0]["out_0"]
```
